# Optimizing a Trainium2 kernel written in Bass

```python
import numpy as np
import jax
import jax.numpy as jnp

def _softmax(x, axis=-1):
    return jax.nn.softmax(x, axis=axis)

def _gelu(x):
    return jax.nn.gelu(x, approximate=True)

def _silu(x):
    return jax.nn.silu(x)

def _sigmoid(x):
    return jax.nn.sigmoid(x)

def _layernorm(x, axis=-1, eps=1e-05):
    m = jnp.mean(x, axis=axis, keepdims=True)
    v = jnp.var(x, axis=axis, keepdims=True)
    return (x - m) / jnp.sqrt(v + eps)

def _scatter_add(tgt, idx, src, axis=0):
    return tgt.at[idx].add(src)

def _segment_sum(src, seg, n):
    return jax.ops.segment_sum(src, seg, n)
kernel_name = 'mk_adaln_d1_jaxref_r8_932cc4'

def setup_inputs(seed: int=0):
    np.random.seed(seed)
    _w = jnp.asarray

    def _L0_attn_setup():
        import jax, jax.numpy as jnp
        import numpy as np
        D_MODEL, D_STATE, D_CONV, EXPAND, DT_RANK = (128, 16, 4, 2, 32)
        D_INNER = D_MODEL * EXPAND

        def _ssm_forward(x, Wi, bi, conv_w, conv_b, Wdt, bdt, A_log, Bm, Cm, Dv, Wo, bo):
            Bb, T, _ = x.shape
            xz = x @ Wi.T + bi
            x_in, z = (xz[..., :D_INNER], xz[..., D_INNER:])
            xc = jnp.transpose(x_in, (0, 2, 1))
            xc = jax.lax.conv_general_dilated(xc, conv_w, (1,), [(D_CONV - 1, 0)], dimension_numbers=('NCH', 'OIH', 'NCH'), feature_group_count=D_INNER)
            xc = xc + conv_b[None, :, None]
            u = jax.nn.silu(jnp.transpose(xc, (0, 2, 1)))
            dt = jax.nn.softplus(x_in[..., :DT_RANK] @ Wdt.T + bdt)
            A = -jnp.exp(A_log)

            def step(h, inp):
                dt_t, u_t = inp
                h = h * jnp.exp(dt_t[:, :, None] * A[None]) + dt_t[:, :, None] * Bm[None] * u_t[:, :, None]
                y = jnp.einsum('bdn,dn->bd', h, Cm)
                return (h, y)
            h0 = jnp.zeros((Bb, D_INNER, D_STATE), x.dtype)
            _, ys = jax.lax.scan(step, h0, (jnp.swapaxes(dt, 0, 1), jnp.swapaxes(u, 0, 1)))
            out = jnp.swapaxes(ys, 0, 1) * jax.nn.silu(z)
            return out @ Wo.T + bo + x * Dv.mean()
        key = jax.random.key(seed)
        ks = jax.random.split(key, 12)
        B, T = (4, 256)
        s_in = 1.0 / np.sqrt(D_MODEL)
        s_dt = 1.0 / np.sqrt(DT_RANK)
        s_out = 1.0 / np.sqrt(D_INNER)
        return {'x': jax.random.normal(ks[0], (B, T, D_MODEL), jnp.float32), 'Wi': jax.random.uniform(ks[1], (2 * D_INNER, D_MODEL), jnp.float32, -s_in, s_in), 'bi': jax.random.uniform(ks[2], (2 * D_INNER,), jnp.float32, -s_in, s_in), 'conv_w': jax.random.uniform(ks[3], (D_INNER, 1, D_CONV), jnp.float32, -0.5, 0.5), 'conv_b': jax.random.uniform(ks[4], (D_INNER,), jnp.float32, -0.5, 0.5), 'Wdt': jax.random.uniform(ks[5], (D_INNER, DT_RANK), jnp.float32, -s_dt, s_dt), 'bdt': jax.random.uniform(ks[6], (D_INNER,), jnp.float32, -s_dt, s_dt), 'A_log': jnp.log(0.99 - jax.random.uniform(ks[7], (D_INNER, D_STATE), jnp.float32) * 0.01), 'Bm': jax.random.normal(ks[8], (D_INNER, D_STATE), jnp.float32) * 0.01, 'Cm': jax.random.normal(ks[9], (D_INNER, D_STATE), jnp.float32) * 0.01, 'Dv': jnp.ones((D_INNER,), jnp.float32) * 0.1, 'Wo': jax.random.uniform(ks[10], (D_MODEL, D_INNER), jnp.float32, -s_out, s_out), 'bo': jax.random.uniform(ks[11], (D_MODEL,), jnp.float32, -s_out, s_out)}
    _L0_attn_in = _L0_attn_setup()

    def _L0_ffn_setup():
        import jax, jax.numpy as jnp
        import numpy as np
        S_LEN, BATCH, HIDDEN = (256, 2, 128)
        N_HEADS, N_KV = (16, 8)
        N_EXP, TOP_K, CAP_F = (8, 2, 1.25)
        FFN = 512
        HEAD_DIM = HIDDEN // N_HEADS
        Q_PER_KV = N_HEADS // N_KV
        EPS = 1e-05
        NEG = -1000000000.0

        def _ln(x, w, b):
            mu = jnp.mean(x, -1, keepdims=True)
            var = jnp.var(x, -1, keepdims=True)
            return (x - mu) * jax.lax.rsqrt(var + EPS) * w + b

        def _forward(hidden_states, ln1_weight, ln1_bias, ln2_weight, ln2_bias, qkv_weight, proj_weight, router_weight, moe_w1, moe_w2):
            S, B, H = hidden_states.shape
            ln1 = _ln(hidden_states, ln1_weight, ln1_bias)
            qkv = (ln1 @ qkv_weight.T).reshape(S, B, N_KV, (Q_PER_KV + 2) * HEAD_DIM)
            q_dim = Q_PER_KV * HEAD_DIM
            q = qkv[..., :q_dim].reshape(S, B, N_HEADS, HEAD_DIM)
            k = jnp.repeat(qkv[..., q_dim:q_dim + HEAD_DIM], Q_PER_KV, axis=2)
            v = jnp.repeat(qkv[..., q_dim + HEAD_DIM:], Q_PER_KV, axis=2)
            scores = jnp.einsum('sbhd,tbhd->bhst', q, k) / jnp.sqrt(jnp.float32(HEAD_DIM))
            causal = jnp.tril(jnp.ones((S, S), bool))
            attn = jax.nn.softmax(jnp.where(causal[None, None], scores, NEG), axis=-1)
            attn_out = jnp.einsum('bhst,tbhd->sbhd', attn, v).reshape(S, B, H)
            hidden_after_attn = hidden_states + attn_out @ proj_weight.T
            x = _ln(hidden_after_attn, ln2_weight, ln2_bias).reshape(-1, H)
            N = S * B
            probs = jax.nn.softmax(x.astype(jnp.float32) @ router_weight, axis=-1)
            top_p, top_i = jax.lax.top_k(probs, TOP_K)
            top_p = top_p / jnp.sum(top_p, -1, keepdims=True)
            flat_exp = top_i.reshape(-1)
            order = jnp.argsort(flat_exp)
            sorted_exp = flat_exp[order]
            counts = jnp.bincount(sorted_exp, length=N_EXP)
            offsets = jnp.concatenate([jnp.zeros((1,), counts.dtype), jnp.cumsum(counts)])
            within = jnp.arange(N * TOP_K) - offsets[sorted_exp]
            cap = int(np.ceil(N * TOP_K / N_EXP * CAP_F))
            keep = within < cap
            slot = jnp.where(keep, sorted_exp * cap + within, N_EXP * cap)
            tok_id = order // TOP_K
            padded_tokens = jnp.zeros((N_EXP * cap + 1, H), x.dtype).at[slot].set(x[tok_id])[:-1]
            padded_probs = jnp.zeros((N_EXP * cap + 1,), jnp.float32).at[slot].set(top_p.reshape(-1)[order])[:-1]
            padded_ids = jnp.zeros((N_EXP * cap + 1,), jnp.int32).at[slot].set(tok_id.astype(jnp.int32))[:-1]
            exp_in = padded_tokens.reshape(N_EXP, cap, H)
            act = jax.nn.gelu(jnp.einsum('ech,ehf->ecf', exp_in, moe_w1), approximate=False)
            exp_out = jnp.einsum('ecf,efh->ech', act, moe_w2).reshape(N_EXP * cap, H)
            weighted = exp_out * padded_probs[:, None].astype(exp_out.dtype)
            moe = jnp.zeros((N, H), exp_out.dtype).at[padded_ids].add(weighted)
            return hidden_after_attn + moe.reshape(S, B, H)
        ks = jax.random.split(jax.random.key(seed), 6)
        qkv_out = N_KV * (Q_PER_KV + 2) * HEAD_DIM
        sc = 0.02
        return {'hidden_states': jax.random.normal(ks[0], (S_LEN, BATCH, HIDDEN), jnp.float32), 'ln1_weight': jnp.ones((HIDDEN,), jnp.float32), 'ln1_bias': jnp.zeros((HIDDEN,), jnp.float32), 'ln2_weight': jnp.ones((HIDDEN,), jnp.float32), 'ln2_bias': jnp.zeros((HIDDEN,), jnp.float32), 'qkv_weight': jax.random.normal(ks[1], (qkv_out, HIDDEN), jnp.float32) * sc, 'proj_weight': jax.random.normal(ks[2], (HIDDEN, HIDDEN), jnp.float32) * sc, 'router_weight': jax.random.normal(ks[3], (HIDDEN, N_EXP), jnp.float32) * sc, 'moe_w1': jax.random.normal(ks[4], (N_EXP, HIDDEN, FFN), jnp.float32) * sc, 'moe_w2': jax.random.normal(ks[5], (N_EXP, FFN, HIDDEN), jnp.float32) * sc}
    _L0_ffn_in = _L0_ffn_setup()
    _L0_c = _w((lambda *s: np.random.randn(*s).astype(np.float32) * 0.05)(32, 128))
    _L0_wmod = _w((lambda *s: np.random.randn(*s).astype(np.float32) * 0.05)(128, 6 * 128) * 128 ** (-0.5))
    _d = {'L0_attn_x': _L0_attn_in['x'], 'L0_attn_Wi': _L0_attn_in['Wi'], 'L0_attn_bi': _L0_attn_in['bi'], 'L0_attn_conv_w': _L0_attn_in['conv_w'], 'L0_attn_conv_b': _L0_attn_in['conv_b'], 'L0_attn_Wdt': _L0_attn_in['Wdt'], 'L0_attn_bdt': _L0_attn_in['bdt'], 'L0_attn_A_log': _L0_attn_in['A_log'], 'L0_attn_Bm': _L0_attn_in['Bm'], 'L0_attn_Cm': _L0_attn_in['Cm'], 'L0_attn_Dv': _L0_attn_in['Dv'], 'L0_attn_Wo': _L0_attn_in['Wo'], 'L0_attn_bo': _L0_attn_in['bo'], 'L0_ffn_ln1_weight': _L0_ffn_in['ln1_weight'], 'L0_ffn_ln1_bias': _L0_ffn_in['ln1_bias'], 'L0_ffn_ln2_weight': _L0_ffn_in['ln2_weight'], 'L0_ffn_ln2_bias': _L0_ffn_in['ln2_bias'], 'L0_ffn_qkv_weight': _L0_ffn_in['qkv_weight'], 'L0_ffn_proj_weight': _L0_ffn_in['proj_weight'], 'L0_ffn_router_weight': _L0_ffn_in['router_weight'], 'L0_ffn_moe_w1': _L0_ffn_in['moe_w1'], 'L0_ffn_moe_w2': _L0_ffn_in['moe_w2'], 'L0_c': _L0_c, 'L0_wmod': _L0_wmod}
    _x0 = _d['L0_attn_x']
    _d['L0_attn_x'] = jax.random.normal(jax.random.fold_in(jax.random.key(seed), 1), (32, 256, 128), dtype=_x0.dtype)
    del _x0
    return _d

def reference(L0_attn_x, L0_attn_Wi, L0_attn_bi, L0_attn_conv_w, L0_attn_conv_b, L0_attn_Wdt, L0_attn_bdt, L0_attn_A_log, L0_attn_Bm, L0_attn_Cm, L0_attn_Dv, L0_attn_Wo, L0_attn_bo, L0_ffn_ln1_weight, L0_ffn_ln1_bias, L0_ffn_ln2_weight, L0_ffn_ln2_bias, L0_ffn_qkv_weight, L0_ffn_proj_weight, L0_ffn_router_weight, L0_ffn_moe_w1, L0_ffn_moe_w2, L0_c, L0_wmod):

    def _L0_attn_ref(x, Wi, bi, conv_w, conv_b, Wdt, bdt, A_log, Bm, Cm, Dv, Wo, bo):
        import jax, jax.numpy as jnp
        import numpy as np
        D_MODEL, D_STATE, D_CONV, EXPAND, DT_RANK = (128, 16, 4, 2, 32)
        D_INNER = D_MODEL * EXPAND

        def _ssm_forward(x, Wi, bi, conv_w, conv_b, Wdt, bdt, A_log, Bm, Cm, Dv, Wo, bo):
            Bb, T, _ = x.shape
            xz = x @ Wi.T + bi
            x_in, z = (xz[..., :D_INNER], xz[..., D_INNER:])
            xc = jnp.transpose(x_in, (0, 2, 1))
            xc = jax.lax.conv_general_dilated(xc, conv_w, (1,), [(D_CONV - 1, 0)], dimension_numbers=('NCH', 'OIH', 'NCH'), feature_group_count=D_INNER)
            xc = xc + conv_b[None, :, None]
            u = jax.nn.silu(jnp.transpose(xc, (0, 2, 1)))
            dt = jax.nn.softplus(x_in[..., :DT_RANK] @ Wdt.T + bdt)
            A = -jnp.exp(A_log)

            def step(h, inp):
                dt_t, u_t = inp
                h = h * jnp.exp(dt_t[:, :, None] * A[None]) + dt_t[:, :, None] * Bm[None] * u_t[:, :, None]
                y = jnp.einsum('bdn,dn->bd', h, Cm)
                return (h, y)
            h0 = jnp.zeros((Bb, D_INNER, D_STATE), x.dtype)
            _, ys = jax.lax.scan(step, h0, (jnp.swapaxes(dt, 0, 1), jnp.swapaxes(u, 0, 1)))
            out = jnp.swapaxes(ys, 0, 1) * jax.nn.silu(z)
            return out @ Wo.T + bo + x * Dv.mean()
        return _ssm_forward(x, Wi, bi, conv_w, conv_b, Wdt, bdt, A_log, Bm, Cm, Dv, Wo, bo)

    def _L0_ffn_ref(hidden_states, ln1_weight, ln1_bias, ln2_weight, ln2_bias, qkv_weight, proj_weight, router_weight, moe_w1, moe_w2):
        import jax, jax.numpy as jnp
        import numpy as np
        S_LEN, BATCH, HIDDEN = (256, 2, 128)
        N_HEADS, N_KV = (16, 8)
        N_EXP, TOP_K, CAP_F = (8, 2, 1.25)
        FFN = 512
        HEAD_DIM = HIDDEN // N_HEADS
        Q_PER_KV = N_HEADS // N_KV
        EPS = 1e-05
        NEG = -1000000000.0

        def _ln(x, w, b):
            mu = jnp.mean(x, -1, keepdims=True)
            var = jnp.var(x, -1, keepdims=True)
            return (x - mu) * jax.lax.rsqrt(var + EPS) * w + b

        def _forward(hidden_states, ln1_weight, ln1_bias, ln2_weight, ln2_bias, qkv_weight, proj_weight, router_weight, moe_w1, moe_w2):
            S, B, H = hidden_states.shape
            ln1 = _ln(hidden_states, ln1_weight, ln1_bias)
            qkv = (ln1 @ qkv_weight.T).reshape(S, B, N_KV, (Q_PER_KV + 2) * HEAD_DIM)
            q_dim = Q_PER_KV * HEAD_DIM
            q = qkv[..., :q_dim].reshape(S, B, N_HEADS, HEAD_DIM)
            k = jnp.repeat(qkv[..., q_dim:q_dim + HEAD_DIM], Q_PER_KV, axis=2)
            v = jnp.repeat(qkv[..., q_dim + HEAD_DIM:], Q_PER_KV, axis=2)
            scores = jnp.einsum('sbhd,tbhd->bhst', q, k) / jnp.sqrt(jnp.float32(HEAD_DIM))
            causal = jnp.tril(jnp.ones((S, S), bool))
            attn = jax.nn.softmax(jnp.where(causal[None, None], scores, NEG), axis=-1)
            attn_out = jnp.einsum('bhst,tbhd->sbhd', attn, v).reshape(S, B, H)
            hidden_after_attn = hidden_states + attn_out @ proj_weight.T
            x = _ln(hidden_after_attn, ln2_weight, ln2_bias).reshape(-1, H)
            N = S * B
            probs = jax.nn.softmax(x.astype(jnp.float32) @ router_weight, axis=-1)
            top_p, top_i = jax.lax.top_k(probs, TOP_K)
            top_p = top_p / jnp.sum(top_p, -1, keepdims=True)
            flat_exp = top_i.reshape(-1)
            order = jnp.argsort(flat_exp)
            sorted_exp = flat_exp[order]
            counts = jnp.bincount(sorted_exp, length=N_EXP)
            offsets = jnp.concatenate([jnp.zeros((1,), counts.dtype), jnp.cumsum(counts)])
            within = jnp.arange(N * TOP_K) - offsets[sorted_exp]
            cap = int(np.ceil(N * TOP_K / N_EXP * CAP_F))
            keep = within < cap
            slot = jnp.where(keep, sorted_exp * cap + within, N_EXP * cap)
            tok_id = order // TOP_K
            padded_tokens = jnp.zeros((N_EXP * cap + 1, H), x.dtype).at[slot].set(x[tok_id])[:-1]
            padded_probs = jnp.zeros((N_EXP * cap + 1,), jnp.float32).at[slot].set(top_p.reshape(-1)[order])[:-1]
            padded_ids = jnp.zeros((N_EXP * cap + 1,), jnp.int32).at[slot].set(tok_id.astype(jnp.int32))[:-1]
            exp_in = padded_tokens.reshape(N_EXP, cap, H)
            act = jax.nn.gelu(jnp.einsum('ech,ehf->ecf', exp_in, moe_w1), approximate=False)
            exp_out = jnp.einsum('ecf,efh->ech', act, moe_w2).reshape(N_EXP * cap, H)
            weighted = exp_out * padded_probs[:, None].astype(exp_out.dtype)
            moe = jnp.zeros((N, H), exp_out.dtype).at[padded_ids].add(weighted)
            return hidden_after_attn + moe.reshape(S, B, H)
        return _forward(hidden_states, ln1_weight, ln1_bias, ln2_weight, ln2_bias, qkv_weight, proj_weight, router_weight, moe_w1, moe_w2)
    x = L0_attn_x
    mod = (_silu(L0_c) @ L0_wmod).reshape(L0_c.shape[0], 6, 1, -1)
    sa, ca, ga, sb, cb, gb = (mod[:, 0], mod[:, 1], mod[:, 2], mod[:, 3], mod[:, 4], mod[:, 5])
    ga = (2 * (ga >= 0) - 1) * jnp.maximum(jnp.abs(ga), 0.25)
    gb = (2 * (gb >= 0) - 1) * jnp.maximum(jnp.abs(gb), 0.25)
    h = _layernorm(x, axis=-1) * (1 + ca) + sa
    x = x + ga * _L0_attn_ref(h, L0_attn_Wi, L0_attn_bi, L0_attn_conv_w, L0_attn_conv_b, L0_attn_Wdt, L0_attn_bdt, L0_attn_A_log, L0_attn_Bm, L0_attn_Cm, L0_attn_Dv, L0_attn_Wo, L0_attn_bo)
    h = _layernorm(x, axis=-1) * (1 + cb) + sb
    x = x + gb * _L0_ffn_ref(h, L0_ffn_ln1_weight, L0_ffn_ln1_bias, L0_ffn_ln2_weight, L0_ffn_ln2_bias, L0_ffn_qkv_weight, L0_ffn_proj_weight, L0_ffn_router_weight, L0_ffn_moe_w1, L0_ffn_moe_w2)
    return x

_drawn_inputs = setup_inputs


def setup_inputs(seed=0):
    import zlib

    import numpy as np

    out = dict(_drawn_inputs(seed))
    spreads = {'L0_attn_Dv': (0.10000000149011612, 0.6),
     'L0_ffn_ln1_weight': (1.0, 0.6),
     'L0_ffn_ln1_bias': (0.0, 0.8),
     'L0_ffn_ln2_weight': (1.0, 0.6),
     'L0_ffn_ln2_bias': (0.0, 2.0)}
    factors = {'L0_attn_Wi': 8.0,
     'L0_attn_bi': 8.0,
     'L0_attn_conv_w': 8.0,
     'L0_attn_conv_b': 8.0,
     'L0_attn_Wdt': 8.0,
     'L0_attn_bdt': 8.0,
     'L0_attn_A_log': 64.0,
     'L0_attn_Bm': 8.0,
     'L0_attn_Cm': 8.0,
     'L0_attn_Wo': 8.0,
     'L0_attn_bo': 161.772,
     'L0_ffn_qkv_weight': 8.0,
     'L0_ffn_proj_weight': 8.0,
     'L0_ffn_router_weight': 20.917,
     'L0_ffn_moe_w1': 17.965,
     'L0_ffn_moe_w2': 5.871}
    for name, (base, spread) in spreads.items():
        noise = np.random.default_rng([zlib.crc32(name.encode()), seed]).standard_normal(out[name].shape)
        drawn = base * np.exp(spread * noise) if base else spread * noise
        out[name] = jnp.asarray(drawn.astype(out[name].dtype))
    for name, factor in factors.items():
        out[name] = (out[name] * factor).astype(out[name].dtype)
    return out
```

```python
from contextlib import ExitStack

import numpy as np

import concourse.bass as bass
from concourse import mybir

F32 = mybir.dt.float32
U32 = mybir.dt.uint32
ALU = mybir.AluOpType
ACT = mybir.ActivationFunctionType
AX_X = mybir.AxisListType.X

P = 128
S, B, D = 32, 256, 128
NT = S * B
DI, NST, DCONV, DTR = 256, 16, 4, 32
NH, NKV, HD = 16, 8, 8
NE, FFN = 8, 512
CAP = -(-NT * 2 * 5 // (NE * 4))
SLOTS = NE * CAP
EPS = 1e-5
BIG = 3e38
NEG = -1e30

CH = 512
NCH = NT // CH
GR = 1024
GS = GR // B
NG = NT // GR
PADB = B + DCONV - 1
RING = 4
TILES = NT // P


def constants():
    p = np.arange(P)
    causal = np.where(np.arange(S)[None, :] <= (p % S)[:, None], 0.0, NEG)
    tile_token = np.arange(TILES)[None, :] * P + p[:, None]
    t = {
        "ident": np.eye(P),
        "ones": np.ones((P, P)),
        "before": (p[:, None] < p[None, :]) * 1.0,
        "causal": causal,
        "head4": ((p[:, None] // HD) % 4 == np.arange(4)[None, :]) * 1.0,
        "slot0": np.tile(np.arange(NE) * float(CAP), (P, 1)),
        "rev": np.tile(NE - np.arange(NE) * 1.0, (P, 1)),
        "eps": np.full((P, 1), EPS),
        "big": np.full((P, 1), BIG),
        "spare1": SLOTS + tile_token,
        "spare2": SLOTS + NT + tile_token,
    }
    return {k: np.ascontiguousarray(v, dtype=np.float32) for k, v in t.items()}


CONST = constants()
CONST_AT = {}
_n = 0
for _k, _v in CONST.items():
    CONST_AT[_k] = (_n, _n + _v.shape[1])
    _n += _v.shape[1]
CONST_COLS = _n


def wait(eng, sem, value):
    if isinstance(value, int) and value <= 0:
        return
    eng.wait_ge(sem, value)


class Turn:

    def __init__(self, v, par, n, static):
        self.v, self.par, self.n, self.static = v, par, n, static

    def back(self, k):
        if self.static:
            c = self.v - k
            return Turn(c, c % 2, self.n, True) if 0 <= c < self.n else None
        return Turn(self.v - k if k else self.v, (self.par - k) % 2, self.n, False)

    def times(self, per, plus=0):
        return self.v * per + plus

    def count(self, plus):
        return self.v + plus if plus else self.v

    def upto(self, k):
        return min(self.v - k, self.n) if self.static else self.count(-k)

    def loads(self):
        return (self.v - self.par) * 8 + 16 if self.par else self.v * 8 + 16


def turns(eng, n, lag):
    head = lag + 2 + (lag % 2)
    for t in range(head):
        yield Turn(t, t % 2, n, True)
    if n > head:
        with eng.Fori(head // 2, n // 2) as i:
            yield Turn(i * 2, 0, n, False)
            yield Turn(i * 2 + 1, 1, n, False)
    for t in range(max(n, head), n + lag):
        yield Turn(t, t % 2, n, True)


def build(nc, t, stop_after=None):
    top = ExitStack()

    def sb(stack, name, shape, dt=F32):
        return stack.enter_context(nc.sbuf_tensor(name, shape, dt))

    def ps(stack, name, shape):
        return stack.enter_context(nc.psum_tensor(name, shape, F32))

    def sems(stack, *names):
        return [stack.enter_context(nc.semaphore(n)) for n in names]

    with top:
        E = Resident()
        E.con = sb(top, "con", [P, CONST_COLS])
        E.ident, E.ones, E.eps = E.const("ident"), E.const("ones"), E.const("eps")
        E.wi = sb(top, "wi", [P, 4 * P])
        E.wdt = sb(top, "wdt", [DTR, DI])
        E.wo = sb(top, "wo", [P, 2, D])
        E.wq = sb(top, "wq", [P, P])
        E.wk = sb(top, "wk", [P, P])
        E.wv = sb(top, "wv", [P, P])
        E.wp4 = sb(top, "wp4", [P, 4, D])
        E.router = sb(top, "router", [P, NE])
        E.cols = sb(top, "cols", [P, NCOLS])
        E.mod = sb(top, "mod", [P, 6, S])
        E.gabo = sb(top, "gabo", [P, S])
        E.A = sb(top, "A", [P, 2, NST])
        E.diag_dv = sb(top, "diag_dv", [P, P])
        E.bufX = sb(top, "bufX", [P, NT])
        E.bufH = sb(top, "bufH", [P, NT])

        with ExitStack() as scan_stack:
            E.diag_cb = sb(scan_stack, "diag_cb", [P, 2, NST, P])
            prep(nc, t, sb, ps, sems, E)
            norm_in(nc, t, sb, ps, sems, E)
            scan_phase(nc, t, sb, ps, sems, E)
        if stop_after == "scan":
            return dump(nc, t, sems, E.bufX)
        E.bufA = sb(top, "bufA", [P, NT])
        norm_mid(nc, t, sb, ps, sems, E)
        if stop_after == "mid":
            return dump(nc, t, sems, E.bufH)
        attention(nc, t, sb, ps, sems, E)
        if stop_after == "attn":
            return dump(nc, t, sems, E.bufA)
        with ExitStack() as st:
            E.logits = sb(st, "logits", [P, TILES, NE])
            E.idx = sb(st, "idx", [P, 4, TILES], U32)
            E.gate = sb(st, "gate", [P, 2, TILES])
            norm_out(nc, t, sb, ps, sems, E)
            route(nc, t, sb, ps, sems, E)
            experts(nc, t, sb, ps, sems, E)
            combine(nc, t, sb, ps, sems, E)


COLS = {}
_c = 0
for _name, _w in (("bi", 4), ("conv_w", 8), ("conv_b", 2), ("bdt", 2), ("bo", 1), ("dv", 2),
                  ("ln1w", 1), ("ln1b", 1), ("ln2w", 1), ("ln2b", 1)):
    COLS[_name] = _c
    _c += _w
NCOLS = _c


class Resident:

    def col(self, name, k=0):
        lo = COLS[name] + k
        return self.cols[:, lo:lo + 1]

    def const(self, name):
        lo, hi = CONST_AT[name]
        return self.con[:, lo:hi]


def dump(nc, t, sems, buf):
    with ExitStack() as st:
        (stored,) = sems(st, "stored")
        block = st.enter_context(nc.Block())

        @block.sync
        def _(sp):
            sp.dma_start(t["out"], buf[:]).then_inc(stored, 16)
            sp.wait_ge(stored, 16)


def prep(nc, t, sb, ps, sems, E):
    with ExitStack() as st:
        alog = sb(st, "alog", [P, 2, NST])
        bm = sb(st, "bm", [P, 2, NST])
        cm = sb(st, "cm", [P, 2, NST])
        cb = sb(st, "cb", [P, 2, NST])
        ct = sb(st, "ct", [P, S])
        sct = sb(st, "sct", [P, S])
        wmod = sb(st, "wmod", [P, 6, D])
        wproj = sb(st, "wproj", [P, D])
        aexp = sb(st, "aexp", [P, 2, NST])
        sign = sb(st, "sign", [P, S])
        mag = sb(st, "mag", [P, S])
        dvm = sb(st, "dvm", [P, 1])
        pmod = ps(st, "pmod", [P, 6, S])
        pdv = ps(st, "pdv", [P, 1])
        (loaded, c_silu, a_exp, mod_ready, dv_ready, done, x_loaded) = sems(
            st, "loaded", "c_silu", "a_exp", "mod_ready", "dv_ready", "prep_done", "x_all_loaded")
        pairs = [(E.con[:], "con"), (E.wi[:], "wi"), (E.wdt[:], "wdt"), (E.wo[:], "wo"), (E.wq[:], "wq"),
                 (E.wk[:], "wk"), (E.wv[:], "wv"), (wproj[:], "wproj"), (E.router[:], "router"),
                 (E.cols[:], "cols"), (alog[:], "alog"), (bm[:], "bm"), (cm[:], "cm"),
                 (ct[:], "ct"), (wmod[:], "wmod")]
        block = st.enter_context(nc.Block())

        @block.sync
        def _(sp):
            for dst, name in pairs:
                sp.dma_start(dst, t[name]).then_inc(loaded, 16)
            sp.dma_start(E.bufX[:], t["xT"]).then_inc(x_loaded, 16)
            sp.wait_ge(x_loaded, 16)

        @block.scalar
        def _(act):
            act.wait_ge(loaded, 16 * len(pairs))
            nc.scalar.activation(sct[:], ct[:], ACT.Silu).then_inc(c_silu, 1)
            nc.scalar.activation(aexp[:], alog[:], ACT.Exp).then_inc(a_exp, 1)

        @block.tensor
        def _(pe):
            pe.wait_ge(loaded, 16 * len(pairs))
            for k in range(2):
                mm = nc.tensor.matmul(pdv[:], E.ones, E.col("dv", k), start=(k == 0), stop=(k == 1))
            mm.then_inc(dv_ready, 1)
            pe.wait_ge(c_silu, 1)
            for k in range(6):
                mm = nc.tensor.matmul(pmod[:, k, :], wmod[:, k, :], sct[:], start=True, stop=True)
            mm.then_inc(mod_ready, 1)

        @block.vector
        def _(dve):
            n = 0

            def link(ins):
                nonlocal n
                n += 1
                ins.then_inc(done, 1)
                dve.wait_ge(done, n)

            dve.wait_ge(loaded, 16 * len(pairs))
            nc.vector.tensor_tensor(cb[:], cm[:], bm[:], ALU.mult).then_inc(done, 1)
            n += 1
            for k in range(4):
                nc.vector.tensor_scalar(E.wp4[:, k, :], wproj[:], E.const("head4")[:, k:k + 1], None, ALU.mult)
            dve.wait_ge(dv_ready, 1)
            link(nc.vector.tensor_scalar(dvm[:], pdv[:], 1.0 / DI, None, ALU.mult))
            nc.vector.tensor_scalar(E.diag_dv[:], E.ident, dvm[:, 0:1], None, ALU.mult)
            for h in range(2):
                for k in range(NST):
                    nc.vector.tensor_scalar(E.diag_cb[:, h, k, :], E.ident, cb[:, h, k:k + 1], None, ALU.mult)
            dve.wait_ge(a_exp, 1)
            nc.vector.tensor_scalar(E.A[:], aexp[:], -1.0, -1e-30, ALU.mult, ALU.min)
            dve.wait_ge(mod_ready, 1)
            link(nc.vector.tensor_copy(E.mod[:], pmod[:]))
            for k in (1, 4):
                nc.vector.tensor_scalar(E.mod[:, k, :], E.mod[:, k, :], 1.0, None, ALU.add)
            for k in (2, 5):
                link(nc.vector.tensor_scalar(mag[:], E.mod[:, k, :], -1.0, 0.25, ALU.mult, ALU.max))
                link(nc.vector.tensor_tensor(mag[:], mag[:], E.mod[:, k, :], ALU.max))
                link(nc.vector.tensor_scalar(sign[:], E.mod[:, k, :], 0.0, None, ALU.is_ge))
                link(nc.vector.tensor_scalar(sign[:], sign[:], 2.0, -1.0, ALU.mult, ALU.add))
                link(nc.vector.tensor_tensor(E.mod[:, k, :], sign[:], mag[:], ALU.mult))
            link(nc.vector.tensor_scalar(E.gabo[:], E.mod[:, 2, :], E.col("bo"), None, ALU.mult))


def norm_in(nc, t, sb, ps, sems, E):
    with ExitStack() as st:
        xt = [sb(st, f"xt{i}", [P, 4, D]) for i in range(2)]
        stats = [sb(st, f"stats{i}", [P, 4, 6]) for i in range(2)]
        mv = [sb(st, f"mv{i}", [P, 4, 2]) for i in range(2)]
        std = [sb(st, f"std{i}", [P, 4]) for i in range(2)]
        rstd = [sb(st, f"rstd{i}", [P, 4]) for i in range(2)]
        spare = sb(st, "spare", [P, 1])
        pt = [ps(st, f"pt{i}", [P, CH]) for i in range(2)]
        x_in = sems(st, "x_in0", "x_in1")
        (stats_made, mv_ready, std_ready, rstd_ready, normed, turned, h_ready) = sems(
            st, "stats_made", "mv_ready", "std_ready", "rstd_ready", "normed", "turned", "h_ready")
        block = st.enter_context(nc.Block())

        @block.sync
        def _(sp):
            for s in turns(sp, NCH, 0):
                if c := s.back(0):
                    wait(sp, turned, c.times(1, -1))
                    sp.dma_start(xt[c.par][:], t["x"][:, bass.ds(c.v * 4, 4), :]).then_inc(x_in[c.par], 16)

        @block.vector
        def _(dve):
            for s in turns(dve, NCH, 1):
                if c := s.back(0):
                    dve.wait_ge(x_in[c.par], c.loads())
                    for j in range(4):
                        i = nc.vector.bn_stats(stats[c.par][:, j, :], xt[c.par][:, j, :])
                    i.then_inc(stats_made, 1)
                    dve.wait_ge(stats_made, c.times(1, 1))
                    nc.vector.tensor_copy(spare[:], E.eps)
                    for j in range(4):
                        i = nc.vector.bn_aggr(mv[c.par][:, j, :], stats[c.par][:, j, :])
                    i.then_inc(mv_ready, 1)
                if c := s.back(1):
                    dve.wait_ge(std_ready, c.times(1, 1))
                    nc.vector.reciprocal(rstd[c.par][:], std[c.par][:]).then_inc(rstd_ready, 1)
                    dve.wait_ge(rstd_ready, c.times(1, 1))
                    for j in range(4):
                        i = nc.vector.tensor_scalar(xt[c.par][:, j, :], xt[c.par][:, j, :], mv[c.par][:, j, 0:1],
                                                    rstd[c.par][:, j:j + 1], ALU.subtract, ALU.mult)
                    i.then_inc(normed, 1)

        @block.tensor
        def _(pe):
            for s in turns(pe, NCH, 1):
                if c := s.back(1):
                    pe.wait_ge(normed, c.times(1, 1))
                    wait(pe, h_ready, c.times(1, -1))
                    for j in range(4):
                        i = nc.tensor.transpose(pt[c.par][:, j * P:(j + 1) * P], xt[c.par][:, j, :], E.ident)
                    i.then_inc(turned, 1)

        @block.scalar
        def _(act):
            for s in turns(act, NCH, 2):
                if c := s.back(0):
                    act.wait_ge(mv_ready, c.times(1, 1))
                    nc.scalar.activation(std[c.par][:], mv[c.par][:, :, 1], ACT.Sqrt, bias=E.eps).then_inc(std_ready, 1)
                if c := s.back(2):
                    act.wait_ge(turned, c.times(1, 1))
                    for k in range(2):
                        i = nc.scalar.activation(E.bufH[:, bass.ds(c.v * CH + k * B, B)], pt[c.par][:, k * B:(k + 1) * B],
                                                 ACT.Identity, bias=E.mod[:, 0, bass.ds(c.v * 2 + k, 1)],
                                                 scale=E.mod[:, 1, bass.ds(c.v * 2 + k, 1)])
                    i.then_inc(h_ready, 1)


def scan_phase(nc, t, sb, ps, sems, E):
    ITEMS = 2 * NST
    with ExitStack() as st:
        xin = [sb(st, f"xin{i}", [P, GS, PADB]) for i in range(2)]
        u = [sb(st, f"u{i}", [P, 2, GR]) for i in range(2)]
        dt = [sb(st, f"dt{i}", [P, 2, GR]) for i in range(2)]
        z = [sb(st, f"z{i}", [P, 2, GR]) for i in range(2)]
        tap = [sb(st, f"tap{i}", [P, GR]) for i in range(2)]
        soft = [sb(st, f"soft{i}", [P, GR]) for i in range(2)]
        a = [sb(st, f"a{i}", [P, GR]) for i in range(RING)]
        g_ = [sb(st, f"g{i}", [P, GR]) for i in range(RING)]
        yg = [sb(st, f"yg{i}", [P, GR]) for i in range(2)]
        mix = sb(st, "mix", [P, GR])
        fp = [ps(st, f"fp{i}", [P, GR]) for i in range(2)]
        yp = [ps(st, f"yp{i}", [P, GR]) for i in range(2)]
        (padded, filled, drained, tap_ready, tap_added, relu_ready, exp1_ready, soft_ready, dt_added, u_ready,
         w_ready, dt_set, decay_ready, scanned, summed, gated, x1_ready) = sems(
            st, "padded", "filled", "drained", "tap_ready", "tap_added", "relu_ready", "exp1_ready", "soft_ready",
            "dt_added", "u_ready", "w_ready", "dt_set", "decay_ready", "scanned", "summed", "gated", "x1_ready")

        OUT, XIN0, DT0, Z0 = 0, 1, 3, 5

        def unit(g, k):
            if isinstance(g, int) and g < 1:
                return 6 * (g + 1) + k - 1
            if isinstance(g, int) and g == NG:
                return unit(NG - 1, 0) + 1
            return g * 7 + (5 + k)

        def slot(par, g, k):
            if isinstance(g, int):
                return unit(g, k) % 2
            return (par + 5 + k) % 2

        def groups(eng, slots):
            slots(-1, 1, False, True)
            slots(0, 0, False, True)
            with eng.Fori(0, NG // 2 - 1) as i:
                slots(i * 2 + 1, 1, True, True)
                slots(i * 2 + 2, 0, True, True)
            slots(NG - 1, 1, True, False)
            slots(NG, 0, True, False)

        block = st.enter_context(nc.Block())

        @block.tensor
        def _(pe):
            def project(g, par, k, m):
                f = fp[slot(par, g, k)]
                wait(pe, drained, unit(g, k) - 1)
                for n in range(2):
                    i = nc.tensor.matmul(f[:, n * CH:(n + 1) * CH], E.wi[:, m * P:(m + 1) * P],
                                         E.bufH[:, bass.ds((g + 1) * GR + n * CH, CH)], start=True, stop=True)
                i.then_inc(filled, 1)

            def project_dt(g, par, k, h):
                f = fp[slot(par, g, k)]
                wait(pe, drained, unit(g, k) - 1)
                pe.wait_ge(drained, unit(g, XIN0) + 1)
                for n in range(2):
                    i = nc.tensor.matmul(f[:, n * CH:(n + 1) * CH], E.wdt[:, h * P:(h + 1) * P],
                                         xin[0][0:DTR, 2 * n:2 * n + 2, DCONV - 1:PADB], start=True, stop=True)
                i.then_inc(filled, 1)

            def output(g, par):
                f = fp[slot(par, g, OUT)]
                wait(pe, drained, unit(g, OUT) - 1)
                pe.wait_ge(gated, g * 2)
                for n in range(2):
                    o = f[:, n * CH:(n + 1) * CH]
                    nc.tensor.matmul(o, E.wo[:, 0, :], yg[0][:, n * CH:(n + 1) * CH], start=True, stop=False)
                    nc.tensor.matmul(o, E.wo[:, 1, :], yg[1][:, n * CH:(n + 1) * CH], start=False, stop=False)
                    i = nc.tensor.matmul(o, E.diag_dv[:], E.bufH[:, bass.ds((g - 1) * GR + n * CH, CH)],
                                         start=False, stop=True)
                i.then_inc(filled, 1)

            def sum_states(g, j):
                h, n = j // NST, j % NST
                if n == 0:
                    wait(pe, gated, g * 2 + h - 1)
                pe.wait_ge(scanned, g * ITEMS + j + 1)
                for q in range(2):
                    i = nc.tensor.matmul(yp[h][:, q * CH:(q + 1) * CH], E.diag_cb[:, h, n, :],
                                         g_[j % RING][:, q * CH:(q + 1) * CH], start=(n == 0), stop=(n == NST - 1))
                i.then_inc(summed, 1)

            def slots(g, par, prev, nxt):
                scans = nxt or (isinstance(g, int) and g == NG - 1)
                if isinstance(g, int) and g < 0:
                    scans = False
                for j in range(ITEMS):
                    if j == 4 and prev:
                        output(g, par)
                    if nxt:
                        if j in (6, 8):
                            project(g, par, XIN0 + (j - 6) // 2, (j - 6) // 2)
                        if j in (12, 14):
                            project_dt(g, par, DT0 + (j - 12) // 2, (j - 12) // 2)
                        if j in (24, 26):
                            project(g, par, Z0 + (j - 24) // 2, 2 + (j - 24) // 2)
                    if scans:
                        sum_states(g, j)

            pe.wait_ge(padded, 2)
            groups(pe, slots)

        @block.scalar
        def _(act):
            def evac_xin(g, par, h):
                k = XIN0 + h
                act.wait_ge(filled, unit(g, k) + 1)
                wait(act, tap_ready, (g + 1) * 8)
                i = nc.scalar.activation(xin[h][:, :, DCONV - 1:PADB], fp[slot(par, g, k)][:].rearrange("p (s b) -> p s b", s=GS),
                                         ACT.Identity, bias=E.col("bi", h))
                i.then_inc(drained, 1)

            def taps(g, par, h, ks):
                act.wait_ge(drained, unit(g, XIN0 + h) + 1)
                for k in ks:
                    src = xin[h][:, :, k:k + B]
                    w = E.col("conv_w", h * 4 + k)
                    n = (g + 1) * 6 + h * 3 + k - 1
                    if k == 0:
                        wait(act, scanned, g * ITEMS)
                        dst = u[1 - par][:, h, :].rearrange("p (s b) -> p s b", s=GS)
                        i = nc.scalar.activation(dst, src, ACT.Identity, bias=E.col("conv_b", h), scale=w)
                    else:
                        wait(act, tap_added, n - 1)
                        dst = tap[(h * 3 + k - 1) % 2][:].rearrange("p (s b) -> p s b", s=GS)
                        i = nc.scalar.activation(dst, src, ACT.Identity, scale=w)
                    i.then_inc(tap_ready, 1)

            def soft_plus(g, par, h, part):
                k = DT0 + h
                if part == 0:
                    act.wait_ge(filled, unit(g, k) + 1)
                    wait(act, dt_added, (g + 1) * 2 + h - 1)
                    nc.scalar.activation(dt[1 - par][:, h, :], fp[slot(par, g, k)][:], ACT.Relu,
                                         bias=E.col("bdt", h)).then_inc(relu_ready, 1)
                    i = nc.scalar.activation(soft[h][:], fp[slot(par, g, k)][:], ACT.Abs, bias=E.col("bdt", h))
                    i.then_inc(drained, 1)
                else:
                    act.wait_ge(drained, unit(g, k) + 1)
                    nc.scalar.activation(soft[h][:], soft[h][:], ACT.Exp, scale=-1.0).then_inc(exp1_ready, 1)
                    act.wait_ge(exp1_ready, (g + 1) * 2 + h + 1)
                    nc.scalar.activation(soft[h][:], soft[h][:], ACT.Ln, bias=E.ones[:, 0:1]).then_inc(soft_ready, 1)

            def silu_u(g, par, h):
                act.wait_ge(tap_added, (g + 1) * 6 + 3 * h + 3)
                nc.scalar.activation(u[1 - par][:, h, :], u[1 - par][:, h, :], ACT.Silu).then_inc(u_ready, 1)

            def silu_z(g, par, h):
                k = Z0 + h
                act.wait_ge(filled, unit(g, k) + 1)
                wait(act, gated, g * 2)
                i = nc.scalar.activation(z[1 - par][:, h, :], fp[slot(par, g, k)][:], ACT.Silu, bias=E.col("bi", 2 + h))
                i.then_inc(drained, 1)

            def evac_out(g, par):
                act.wait_ge(filled, unit(g, OUT) + 1)
                wait(act, x1_ready, g - 1)
                for s in range(GS):
                    at = bass.ds((g - 1) * GS + s, 1)
                    i = nc.scalar.activation(mix[:, s * B:(s + 1) * B], fp[slot(par, g, OUT)][:, s * B:(s + 1) * B],
                                             ACT.Identity, bias=E.gabo[:, at], scale=E.mod[:, 2, at])
                i.then_inc(drained, 1)

            def decay(g, par, j):
                h, n = j // NST, j % NST
                if j == 0:
                    act.wait_ge(dt_set, g + 1)
                wait(act, scanned, g * ITEMS + j - RING + 1)
                nc.scalar.activation(a[j % RING][:], dt[par][:, h, :], ACT.Exp, scale=E.A[:, h, n:n + 1]).then_inc(decay_ready, 1)

            def slots(g, par, prev, nxt):
                scans = not (isinstance(g, int) and (g < 0 or g == NG))
                for j in range(ITEMS):
                    if scans:
                        decay(g, par, j)
                    if j == 5 and prev:
                        evac_out(g, par)
                    if nxt:
                        if j == 7:
                            evac_xin(g, par, 0)
                        if j == 9:
                            taps(g, par, 0, (0, 1))
                        if j == 10:
                            evac_xin(g, par, 1)
                        if j == 11:
                            taps(g, par, 0, (2, 3))
                        if j in (12, 13):
                            taps(g, par, 1, ((0, 1), (2, 3))[j - 12])
                        if j in (14, 16):
                            soft_plus(g, par, (j - 14) // 2, 0)
                        if j in (15, 17):
                            soft_plus(g, par, (j - 15) // 2, 1)
                        if j == 27:
                            silu_u(g, par, 0)
                            silu_u(g, par, 1)
                            silu_z(g, par, 0)
                            silu_z(g, par, 1)

            act.wait_ge(padded, 2)
            groups(act, slots)

        @block.gpsimd
        def _(pool):
            def slots(g, par, prev, nxt):
                if prev:
                    pool.wait_ge(drained, unit(g, OUT) + 1)
                    x1 = E.bufX[:, bass.ds((g - 1) * GR, GR)]
                    nc.gpsimd.tensor_tensor(x1, x1, mix[:], ALU.add).then_inc(x1_ready, 1)
                if nxt:
                    for h in range(2):
                        uh = u[1 - par][:, h, :]
                        for k in range(1, DCONV):
                            pool.wait_ge(tap_ready, (g + 1) * 8 + h * 4 + k + 1)
                            wait(pool, tap_added, (g + 1) * 6 + h * 3 + k - 1)
                            nc.gpsimd.tensor_tensor(uh, uh, tap[(h * 3 + k - 1) % 2][:], ALU.add).then_inc(tap_added, 1)
                    for h in range(2):
                        dh = dt[1 - par][:, h, :]
                        pool.wait_ge(soft_ready, (g + 1) * 2 + h + 1)
                        nc.gpsimd.tensor_tensor(dh, dh, soft[h][:], ALU.add).then_inc(dt_added, 1)
                    for h in range(2):
                        uh, dh = u[1 - par][:, h, :], dt[1 - par][:, h, :]
                        pool.wait_ge(u_ready, (g + 1) * 2 + h + 1)
                        pool.wait_ge(dt_added, (g + 1) * 2 + h + 1)
                        nc.gpsimd.tensor_tensor(uh, uh, dh, ALU.mult).then_inc(w_ready, 1)
                    pool.wait_ge(w_ready, (g + 1) * 2 + 2)
                    firsts = dt[1 - par][:].rearrange("p h (s b) -> p (h s) b", s=GS)[:, :, 0:1]
                    nc.gpsimd.tensor_tensor(firsts, firsts, E.const("big").unsqueeze(1).to_broadcast([P, 2 * GS, 1]),
                                            ALU.add).then_inc(dt_set, 1)

            for h in range(2):
                nc.gpsimd.memset(xin[h][:, :, 0:DCONV - 1], 0.0).then_inc(padded, 1)
            groups(pool, slots)

        @block.vector
        def _(dve):
            def gate_y(g, h, par):
                dve.wait_ge(summed, g * ITEMS + (h + 1) * NST)
                if h == 0:
                    dve.wait_ge(drained, unit(g - 1, Z0 + 1) + 1)
                if not (isinstance(g, int) and g == 0):
                    dve.wait_ge(filled, unit(g, OUT) + 1)
                nc.vector.tensor_tensor(yg[h][:], yp[h][:], z[par][:, h, :], ALU.mult).then_inc(gated, 1)

            def slots(g, par, prev, nxt):
                scans = not (isinstance(g, int) and (g < 0 or g == NG))
                for j in range(ITEMS):
                    h = j // NST
                    if scans:
                        if j % NST == 0:
                            dve.wait_ge(w_ready, g * 2 + h + 1)
                        dve.wait_ge(decay_ready, g * ITEMS + j + 1)
                        wait(dve, summed, g * ITEMS + j - RING + 1)
                        nc.vector.tensor_tensor_scan(g_[j % RING][:], a[j % RING][:], u[par][:, h, :], 0.0,
                                                     ALU.mult, ALU.add).then_inc(scanned, 1)
                    if j == 2 and prev:
                        gate_y(g - 1, 1, 1 - par)
                    if j == NST + 2 and scans:
                        gate_y(g, 0, par)

            groups(dve, slots)


def norm_mid(nc, t, sb, ps, sems, E):
    NB = CH // S
    with ExitStack() as st:
        def two(name, shape):
            return [sb(st, f"{name}{i}", shape) for i in range(2)]

        xb, xn, hm, hb, xm = (two(n, [P, CH]) for n in ("mxb", "mxn", "mhm", "mhb", "mxm"))
        stats = [two("mstatsA", [P, 4, 6]), two("mstatsB", [P, 4, 6])]
        mv = [two("mmvA", [P, 4, 2]), two("mmvB", [P, 4, 2])]
        std = [two("mstdA", [P, 4]), two("mstdB", [P, 4])]
        rstd = [two("mrstdA", [P, 4]), two("mrstdB", [P, 4])]
        pp = [[ps(st, f"mp{k}{i}", [P, CH]) for i in range(2)] for k in range(4)]
        zero = sb(st, "zero", [P, 1024])
        spare = sb(st, "mspare", [P, 1])
        (xb_ready, scaled, h_ready, h_kept, zeroed, cleared) = sems(
            st, "m_xb_ready", "m_scaled", "m_h_ready", "m_h_kept", "m_zeroed", "m_cleared")
        turn_in, stats_made, mv_ready, std_ready, rstd_ready, normed, turn_out = (
            sems(st, f"m_{n}_A", f"m_{n}_B")
            for n in ("turn_in", "stats_made", "mv_ready", "std_ready", "rstd_ready", "normed", "turn_out"))
        (l1_ready,) = sems(st, "m_l1_ready")
        block = st.enter_context(nc.Block())
        first, second = (xb, xn), (hb, xm)

        @block.sync
        def _(sp):
            sp.wait_ge(zeroed, 1)
            rows = t["slots_in"][0:SLOTS, :].rearrange("(n p r) d -> n p (r d)", p=P, r=8)
            for k in range(SLOTS // (P * 8)):
                sp.dma_start(rows[k], zero[:]).then_inc(cleared, 16)
            sp.wait_ge(cleared, 16 * (SLOTS // (P * 8)))

        @block.gpsimd
        def _(pool):
            nc.gpsimd.memset(zero[:], 0.0).then_inc(zeroed, 1)
            x1 = E.bufX[:].rearrange("p (s b) -> p b s", s=S)
            for s in turns(pool, NCH, 1):
                if c := s.back(0):
                    wait(pool, turn_in[0], c.times(1, -1))
                    nc.gpsimd.tensor_copy(xb[c.par][:].rearrange("p (b s) -> p b s", s=S),
                                          x1[:, bass.ds(c.v * NB, NB), :]).then_inc(xb_ready, 1)
                if c := s.back(1):
                    pool.wait_ge(scaled, c.times(1, 1))
                    wait(pool, turn_in[1], c.times(1, -1))
                    wait(pool, h_kept, c.times(1, -1))
                    nc.gpsimd.tensor_tensor(hb[c.par][:].rearrange("p (b s) -> p b s", s=S),
                                            hm[c.par][:].rearrange("p (b s) -> p b s", s=S),
                                            E.mod[:, 3, :].unsqueeze(1).to_broadcast([P, NB, S]), ALU.add).then_inc(h_ready, 1)

        @block.tensor
        def _(pe):
            for s in turns(pe, NCH, 3):
                if c := s.back(3):
                    pe.wait_ge(normed[1], c.times(1, 1))
                    wait(pe, l1_ready, c.times(1, -1))
                    for j in range(4):
                        i = nc.tensor.transpose(pp[3][c.par][:, j * P:(j + 1) * P], xm[c.par][:, j * P:(j + 1) * P], E.ident)
                    i.then_inc(turn_out[1], 1)
                if c := s.back(2):
                    pe.wait_ge(h_ready, c.times(1, 1))
                    wait(pe, normed[1], c.times(1, -1))
                    for j in range(4):
                        i = nc.tensor.transpose(pp[2][c.par][:, j * P:(j + 1) * P], hb[c.par][:, j * P:(j + 1) * P], E.ident)
                    i.then_inc(turn_in[1], 1)
                if c := s.back(1):
                    pe.wait_ge(normed[0], c.times(1, 1))
                    wait(pe, scaled, c.times(1, -1))
                    for j in range(4):
                        i = nc.tensor.transpose(pp[1][c.par][:, j * P:(j + 1) * P], xn[c.par][:, j * P:(j + 1) * P], E.ident)
                    i.then_inc(turn_out[0], 1)
                if c := s.back(0):
                    pe.wait_ge(xb_ready, c.times(1, 1))
                    wait(pe, normed[0], c.times(1, -1))
                    for j in range(4):
                        i = nc.tensor.transpose(pp[0][c.par][:, j * P:(j + 1) * P], xb[c.par][:, j * P:(j + 1) * P], E.ident)
                    i.then_inc(turn_in[0], 1)

        @block.vector
        def _(dve):
            def statistics(k, c):
                dve.wait_ge(turn_in[k], c.times(1, 1))
                for j in range(4):
                    i = nc.vector.bn_stats(stats[k][c.par][:, j, :], pp[2 * k][c.par][:, j * P:(j + 1) * P])
                i.then_inc(stats_made[k], 1)
                dve.wait_ge(stats_made[k], c.times(1, 1))
                nc.vector.tensor_copy(spare[:], E.eps)
                for j in range(4):
                    i = nc.vector.bn_aggr(mv[k][c.par][:, j, :], stats[k][c.par][:, j, :])
                i.then_inc(mv_ready[k], 1)

            def normalise(k, c, out):
                dve.wait_ge(std_ready[k], c.times(1, 1))
                wait(dve, turn_out[k], c.times(1, -1))
                nc.vector.reciprocal(rstd[k][c.par][:], std[k][c.par][:]).then_inc(rstd_ready[k], 1)
                dve.wait_ge(rstd_ready[k], c.times(1, 1))
                for j in range(4):
                    i = nc.vector.tensor_scalar(out[c.par][:, j * P:(j + 1) * P], pp[2 * k][c.par][:, j * P:(j + 1) * P],
                                                mv[k][c.par][:, j, 0:1], rstd[k][c.par][:, j:j + 1],
                                                ALU.subtract, ALU.mult)
                i.then_inc(normed[k], 1)

            for s in turns(dve, NCH, 3):
                if c := s.back(3):
                    normalise(1, c, xm)
                if c := s.back(1):
                    normalise(0, c, xn)
                if c := s.back(0):
                    statistics(0, c)
                if c := s.back(1):
                    dve.wait_ge(turn_out[0], c.times(1, 1))
                    wait(dve, h_ready, c.times(1, -1))
                    nc.vector.tensor_tensor(hm[c.par][:].rearrange("p (b s) -> p b s", s=S),
                                            pp[1][c.par][:].rearrange("p (b s) -> p b s", s=S),
                                            E.mod[:, 4, :].unsqueeze(1).to_broadcast([P, NB, S]), ALU.mult).then_inc(scaled, 1)
                if c := s.back(2):
                    statistics(1, c)

        @block.scalar
        def _(act):
            for s in turns(act, NCH, 3):
                if c := s.back(0):
                    act.wait_ge(mv_ready[0], c.times(1, 1))
                    nc.scalar.activation(std[0][c.par][:], mv[0][c.par][:, :, 1], ACT.Sqrt, bias=E.eps).then_inc(std_ready[0], 1)
                if c := s.back(2):
                    act.wait_ge(h_ready, c.times(1, 1))
                    nc.scalar.activation(E.bufA[:, bass.ds(c.v * CH, CH)], hb[c.par][:], ACT.Identity).then_inc(h_kept, 1)
                    act.wait_ge(mv_ready[1], c.times(1, 1))
                    nc.scalar.activation(std[1][c.par][:], mv[1][c.par][:, :, 1], ACT.Sqrt, bias=E.eps).then_inc(std_ready[1], 1)
                if c := s.back(3):
                    act.wait_ge(turn_out[1], c.times(1, 1))
                    nc.scalar.activation(E.bufH[:, bass.ds(c.v * CH, CH)], pp[3][c.par][:], ACT.Identity,
                                         bias=E.col("ln1b"), scale=E.col("ln1w")).then_inc(l1_ready, 1)


def attention(nc, t, sb, ps, sems, E):
    NB = 16
    G = NB // 4
    BT = NB * S
    W = BT * 4
    NBLK = NT // BT
    with ExitStack() as st:
        def two(name, shape):
            return [sb(st, f"{name}{i}", shape) for i in range(2)]

        lb = two("lb", [P, BT])
        q = two("q", [P, NB, S])
        kd = two("kd", [P, NB, 4, S])
        v = two("v", [P, G, P])
        sc = two("sc", [P, 4, W // 4])
        mx = two("mx", [P, W // S])
        sm = two("sm", [P, W // S])
        rs = two("rs", [P, W // S])
        pT = two("pT", [P, 4, W // 4])
        ot = two("ot", [P, 4, G, 4 * S])
        psL = ps(st, "psL", [P, 4, 512])
        psR = ps(st, "psR", [P, 4, 512])
        (lb_ready, qkv_made, q_ready, k_ready, v_ready, scored, masked, max_ready, shifted, exped, sum_ready,
         rcp_ready, probs_ready, pT_ready, av_made, ot_ready, projected, added) = sems(
            st, "lb_ready", "qkv_made", "q_ready", "k_ready", "v_ready", "scored", "masked", "max_ready", "shifted",
            "exped", "sum_ready", "rcp_ready", "probs_ready", "pT_ready", "av_made", "ot_ready", "projected", "added")
        block = st.enter_context(nc.Block())

        def rows(x):
            return x[:].rearrange("p q (c t) -> p (q c) t", t=S)

        def carry(bank):
            nc.tensor.matmul(bank[:, 0:1], E.ident, E.ident[:, 0:1], start=True, stop=True)

        @block.tensor
        def _(pe):
            for s in turns(pe, NBLK, 3):
                if c := s.back(3):
                    pe.wait_ge(pT_ready, c.times(1, 1))
                    wait(pe, q_ready, s.upto(0))
                    wait(pe, k_ready, s.upto(0))
                    wait(pe, v_ready, s.upto(1))
                    carry(psR[:, 0, :])
                    for g in range(G):
                        for k in range(4):
                            for b in range(4):
                                r = slice(32 * b, 32 * b + 32)
                                i = nc.tensor.matmul(psR[32 * k:32 * k + 32, b, g * P:(g + 1) * P],
                                                     v[c.par][r, g, 32 * k:32 * k + 32],
                                                     pT[c.par][r, k, g * P:(g + 1) * P], start=True, stop=True,
                                                     tile_position=(32 * b, 32 * k))
                    i.then_inc(av_made, 1)
                if c := s.back(1):
                    pe.wait_ge(q_ready, c.times(1, 1))
                    pe.wait_ge(k_ready, c.times(1, 1))
                    wait(pe, masked, c.times(1, 0))
                    wait(pe, added, c.times(1, -2))
                    carry(psL[:, 0, :])
                    for g in range(G):
                        for b in range(4):
                            for k in range(4):
                                r = slice(32 * k, 32 * k + 32)
                                i = nc.tensor.matmul(psL[32 * b:32 * b + 32, k, g * P:(g + 1) * P],
                                                     q[c.par][r, g * 4 + b, :], kd[c.par][r, g * 4 + b, :, :],
                                                     start=True, stop=True, tile_position=(32 * k, 32 * b))
                    i.then_inc(scored, 1)
                if s.back(0) or s.back(1):
                    wait(pe, ot_ready, s.count(-2))
                    wait(pe, v_ready, s.upto(1))
                    if c := s.back(0):
                        pe.wait_ge(lb_ready, c.times(1, 1))
                        nc.tensor.matmul(psR[:, 0, :], E.wq[:], lb[c.par][:], start=True, stop=True)
                        i = nc.tensor.matmul(psR[:, 1, :], E.wk[:], lb[c.par][:], start=True, stop=True)
                    if c := s.back(1):
                        for g in range(G):
                            i = nc.tensor.matmul(psR[:, 2, g * P:(g + 1) * P], lb[c.par][:, g * P:(g + 1) * P],
                                                 E.wv[:], start=True, stop=True)
                    i.then_inc(qkv_made, 1)
                if c := s.back(3):
                    pe.wait_ge(ot_ready, c.times(1, 1))
                    wait(pe, masked, s.upto(0))
                    for k in range(4):
                        rhs = ot[c.par][:, :, :, k * S:(k + 1) * S].rearrange("p b g s -> p g b s")
                        i = nc.tensor.matmul(psL[:, 0, :], E.wp4[:, k, :], rhs, start=(k == 0), stop=(k == 3))
                    i.then_inc(projected, 1)

        @block.gpsimd
        def _(pool):
            for s in turns(pool, NBLK, 2):
                if c := s.back(0):
                    wait(pool, qkv_made, c.times(1, 0))
                    nc.gpsimd.tensor_copy(lb[c.par][:], E.bufH[:, bass.ds(c.v * BT, BT)]).then_inc(lb_ready, 1)
                if c := s.back(2):
                    pool.wait_ge(rcp_ready, c.times(1, 1))
                    nc.gpsimd.tensor_tensor(rows(sc[c.par]), rows(sc[c.par]),
                                            rs[c.par][:].unsqueeze(2).to_broadcast([P, W // S, S]),
                                            ALU.mult).then_inc(probs_ready, 1)
                if c := s.back(1):
                    pool.wait_ge(max_ready, c.times(1, 1))
                    nc.gpsimd.tensor_tensor(rows(sc[c.par]), rows(sc[c.par]),
                                            mx[c.par][:].unsqueeze(2).to_broadcast([P, W // S, S]),
                                            ALU.subtract).then_inc(shifted, 1)

        @block.scalar
        def _(act):
            for s in turns(act, NBLK, 3):
                if c := s.back(3):
                    act.wait_ge(av_made, c.times(1, 1))
                    wait(act, projected, c.times(1, -1))
                    nc.scalar.activation(ot[c.par][:].rearrange("p b g s -> p b (g s)"), psR[:],
                                         ACT.Identity).then_inc(ot_ready, 1)
                if c := s.back(0):
                    act.wait_ge(qkv_made, c.times(1, 1))
                    wait(act, scored, c.times(1, -1))
                    nc.scalar.activation(q[c.par][:], psR[:, 0, :].rearrange("p (b s) -> p b s", s=S),
                                         ACT.Identity).then_inc(q_ready, 1)
                if c := s.back(1):
                    act.wait_ge(qkv_made, c.times(1, 2))
                    wait(act, av_made, c.times(1, -1))
                    nc.scalar.activation(v[c.par][:], psR[:, 2, :].rearrange("p (g d) -> p g d", g=G),
                                         ACT.Identity).then_inc(v_ready, 1)
                    act.wait_ge(shifted, c.times(1, 1))
                    nc.scalar.activation(sc[c.par][:], sc[c.par][:], ACT.Exp, scale=float(HD) ** -0.5).then_inc(exped, 1)

        @block.vector
        def _(dve):
            mask = E.const("causal").unsqueeze(1).to_broadcast([P, W // S, S])
            for s in turns(dve, NBLK, 3):
                if c := s.back(3):
                    dve.wait_ge(probs_ready, c.times(1, 1))
                    wait(dve, av_made, c.times(1, -1))
                    nc.vector.transpose(pT[c.par][:].rearrange("p q c -> p (q c)"),
                                        sc[c.par][:].rearrange("p q c -> p (q c)")).then_inc(pT_ready, 1)
                if c := s.back(2):
                    dve.wait_ge(exped, c.times(1, 1))
                    nc.vector.tensor_reduce(sm[c.par][:], rows(sc[c.par]), AX_X, ALU.add).then_inc(sum_ready, 1)
                    dve.wait_ge(sum_ready, c.times(1, 1))
                    nc.vector.reciprocal(rs[c.par][:], sm[c.par][:]).then_inc(rcp_ready, 1)
                if c := s.back(1):
                    dve.wait_ge(scored, c.times(1, 1))
                    wait(dve, pT_ready, c.times(1, -1))
                    nc.vector.tensor_tensor(rows(sc[c.par]), psL[:].rearrange("p q (c t) -> p (q c) t", t=S), mask,
                                            ALU.add).then_inc(masked, 1)
                    dve.wait_ge(masked, c.times(1, 1))
                    nc.vector.tensor_reduce(mx[c.par][:], rows(sc[c.par]), AX_X, ALU.max).then_inc(max_ready, 1)
                if c := s.back(0):
                    dve.wait_ge(qkv_made, c.times(1, 1))
                    wait(dve, scored, c.times(1, -1))
                    kp = psR[:, 1, :].rearrange("p (b s) -> p b s", s=S)
                    nc.vector.tensor_tensor(kd[c.par][:], kp.unsqueeze(2).to_broadcast([P, NB, 4, S]),
                                            E.const("head4").unsqueeze(1).unsqueeze(3).to_broadcast([P, NB, 4, S]),
                                            ALU.mult).then_inc(k_ready, 1)
                if c := s.back(3):
                    dve.wait_ge(projected, c.times(1, 1))
                    ha = E.bufA[:, bass.ds(c.v * BT, BT)]
                    nc.vector.tensor_tensor(ha, psL[:, 0, :], ha, ALU.add).then_inc(added, 1)


def norm_out(nc, t, sb, ps, sems, E):
    with ExitStack() as st:
        def two(name, shape):
            return [sb(st, f"{name}{i}", shape) for i in range(2)]

        hb, xn, xs = (two(n, [P, CH]) for n in ("ohb", "oxn", "oxs"))
        stats, mv, std, rstd = two("ostats", [P, 4, 6]), two("omv", [P, 4, 2]), two("ostd", [P, 4]), two("orstd", [P, 4])
        spare = sb(st, "ospare", [P, 1])
        p0, p1, p2, pl = ([ps(st, f"o{n}{i}", [P, w]) for i in range(2)]
                          for n, w in (("p0", CH), ("p1", CH), ("p2", CH), ("pl", 4 * NE)))
        (hb_ready, turned0, stats_made, mv_ready, std_ready, rstd_ready, normed, turned1, xs_ready, turned2,
         logit_ready, kept) = sems(
            st, "o_hb_ready", "o_turned0", "o_stats_made", "o_mv_ready", "o_std_ready", "o_rstd_ready", "o_normed",
            "o_turned1", "o_xs_ready", "o_turned2", "o_logit_ready", "o_kept")
        block = st.enter_context(nc.Block())

        @block.gpsimd
        def _(pool):
            ha = E.bufA[:].rearrange("p (b s) -> p s b", s=S)
            for s in turns(pool, NCH, 0):
                if c := s.back(0):
                    wait(pool, turned0, c.times(1, -1))
                    nc.gpsimd.tensor_copy(hb[c.par][:].rearrange("p (s b) -> p s b", b=B),
                                          ha[:, bass.ds(c.v * 2, 2), :]).then_inc(hb_ready, 1)

        @block.tensor
        def _(pe):
            for s in turns(pe, NCH, 2):
                if c := s.back(2):
                    pe.wait_ge(xs_ready, c.times(1, 1))
                    wait(pe, kept, c.times(1, -1))
                    wait(pe, logit_ready, c.times(1, -1))
                    for j in range(4):
                        xj = xs[c.par][:, j * P:(j + 1) * P]
                        nc.tensor.matmul(pl[c.par][:, j * NE:(j + 1) * NE], xj, E.router[:], start=True, stop=True)
                        i = nc.tensor.transpose(p2[c.par][:, j * P:(j + 1) * P], xj, E.ident)
                    i.then_inc(turned2, 1)
                if c := s.back(1):
                    pe.wait_ge(normed, c.times(1, 1))
                    wait(pe, xs_ready, c.times(1, -1))
                    for j in range(4):
                        i = nc.tensor.transpose(p1[c.par][:, j * P:(j + 1) * P], xn[c.par][:, j * P:(j + 1) * P], E.ident)
                    i.then_inc(turned1, 1)
                if c := s.back(0):
                    pe.wait_ge(hb_ready, c.times(1, 1))
                    wait(pe, normed, c.times(1, -1))
                    for j in range(4):
                        i = nc.tensor.transpose(p0[c.par][:, j * P:(j + 1) * P], hb[c.par][:, j * P:(j + 1) * P], E.ident)
                    i.then_inc(turned0, 1)

        @block.vector
        def _(dve):
            for s in turns(dve, NCH, 2):
                if c := s.back(1):
                    dve.wait_ge(std_ready, c.times(1, 1))
                    wait(dve, turned1, c.times(1, -1))
                    nc.vector.reciprocal(rstd[c.par][:], std[c.par][:]).then_inc(rstd_ready, 1)
                    dve.wait_ge(rstd_ready, c.times(1, 1))
                    for j in range(4):
                        i = nc.vector.tensor_scalar(xn[c.par][:, j * P:(j + 1) * P], p0[c.par][:, j * P:(j + 1) * P],
                                                    mv[c.par][:, j, 0:1], rstd[c.par][:, j:j + 1],
                                                    ALU.subtract, ALU.mult)
                    i.then_inc(normed, 1)
                if c := s.back(0):
                    dve.wait_ge(turned0, c.times(1, 1))
                    for j in range(4):
                        i = nc.vector.bn_stats(stats[c.par][:, j, :], p0[c.par][:, j * P:(j + 1) * P])
                    i.then_inc(stats_made, 1)
                    dve.wait_ge(stats_made, c.times(1, 1))
                    nc.vector.tensor_copy(spare[:], E.eps)
                    for j in range(4):
                        i = nc.vector.bn_aggr(mv[c.par][:, j, :], stats[c.par][:, j, :])
                    i.then_inc(mv_ready, 1)
                if c := s.back(2):
                    dve.wait_ge(turned2, c.times(1, 1))
                    nc.vector.tensor_copy(E.logits[:, bass.ds(c.v * 4, 4), :],
                                          pl[c.par][:].rearrange("p (j e) -> p j e", e=NE)).then_inc(logit_ready, 1)

        @block.scalar
        def _(act):
            for s in turns(act, NCH, 2):
                if c := s.back(0):
                    act.wait_ge(mv_ready, c.times(1, 1))
                    nc.scalar.activation(std[c.par][:], mv[c.par][:, :, 1], ACT.Sqrt, bias=E.eps).then_inc(std_ready, 1)
                if c := s.back(1):
                    act.wait_ge(turned1, c.times(1, 1))
                    wait(act, turned2, c.times(1, -1))
                    nc.scalar.activation(xs[c.par][:], p1[c.par][:], ACT.Identity, bias=E.col("ln2b"),
                                         scale=E.col("ln2w")).then_inc(xs_ready, 1)
                if c := s.back(2):
                    act.wait_ge(turned2, c.times(1, 1))
                    nc.scalar.activation(E.bufH[:, bass.ds(c.v * CH, CH)], p2[c.par][:], ACT.Identity).then_inc(kept, 1)


def route(nc, t, sb, ps, sems, E):
    N8 = [P, TILES, NE]
    with ExitStack() as st:
        prob, pick1, pick2, key, rest, both, tot, incl, rank, keep = (
            sb(st, f"r_{n}", N8) for n in ("prob", "pick1", "pick2", "key", "rest", "both", "tot", "incl", "rank", "keep"))
        m1, m2, km, ssum, at, kept, tmp = (sb(st, f"r_{n}", [P, TILES]) for n in ("m1", "m2", "km", "ssum", "at", "kept", "tmp"))
        pre, ptot = ps(st, "r_pre", N8), ps(st, "r_ptot", N8)
        (step, shifted, exped, picked, counted, routed, scattered) = sems(
            st, "r_step", "r_shifted", "r_exped", "r_picked", "r_counted", "r_routed", "r_scattered")
        block = st.enter_context(nc.Block())

        def wide(x):
            return x[:].unsqueeze(2).to_broadcast(N8)

        def row(name):
            return E.const(name).unsqueeze(1).to_broadcast(N8)

        @block.scalar
        def _(act):
            act.wait_ge(shifted, 1)
            nc.scalar.activation(prob[:], prob[:], ACT.Exp).then_inc(exped, 1)

        @block.tensor
        def _(pe):
            pe.wait_ge(picked, 1)
            nc.tensor.matmul(pre[:].rearrange("p t e -> p (t e)"), E.const("before"),
                             both[:].rearrange("p t e -> p (t e)"), start=True, stop=True)
            nc.tensor.matmul(ptot[:].rearrange("p t e -> p (t e)"), E.ones,
                             both[:].rearrange("p t e -> p (t e)"), start=True, stop=True).then_inc(counted, 1)

        @block.vector
        def _(dve):
            n = 0

            def link(ins):
                nonlocal n
                n += 1
                ins.then_inc(step, 1)
                dve.wait_ge(step, n)

            def tt(out, a, b, op):
                link(nc.vector.tensor_tensor(out, a, b, op))

            link(nc.vector.tensor_reduce(m1[:], E.logits[:], AX_X, ALU.max))
            nc.vector.tensor_tensor(prob[:], E.logits[:], wide(m1), ALU.subtract).then_inc(shifted, 1)
            dve.wait_ge(exped, 1)
            link(nc.vector.tensor_reduce(ssum[:], prob[:], AX_X, ALU.add))
            link(nc.vector.reciprocal(ssum[:], ssum[:]))
            tt(prob[:], prob[:], wide(ssum), ALU.mult)

            def pick(src, best, out):
                link(nc.vector.tensor_reduce(best[:], src[:], AX_X, ALU.max))
                tt(key[:], src[:], wide(best), ALU.is_equal)
                tt(key[:], key[:], row("rev"), ALU.mult)
                link(nc.vector.tensor_reduce(km[:], key[:], AX_X, ALU.max))
                tt(out[:], key[:], wide(km), ALU.is_equal)

            pick(prob, m1, pick1)
            link(nc.vector.scalar_tensor_tensor(rest[:], pick1[:], -2.0, prob[:], ALU.mult, ALU.add))
            pick(rest, m2, pick2)
            nc.vector.tensor_tensor(both[:], pick1[:], pick2[:], ALU.add).then_inc(picked, 1)
            tt(ssum[:], m1[:], m2[:], ALU.add)
            link(nc.vector.reciprocal(ssum[:], ssum[:]))
            tt(m1[:], m1[:], ssum[:], ALU.mult)
            tt(m2[:], m2[:], ssum[:], ALU.mult)
            dve.wait_ge(counted, 1)
            link(nc.vector.tensor_copy(tot[:], ptot[:]))
            for e in range(NE):
                i = nc.vector.tensor_tensor_scan(incl[:, :, e], E.ones[:, 0:TILES], tot[:, :, e], 0.0, ALU.mult, ALU.add)
            link(i)
            tt(rank[:], incl[:], tot[:], ALU.subtract)
            tt(rank[:], rank[:], pre[:], ALU.add)
            link(nc.vector.tensor_scalar(keep[:], rank[:], float(CAP), None, ALU.is_lt))
            tt(rank[:], rank[:], row("slot0"), ALU.add)
            for k, (pick_k, m) in enumerate(((pick1, m1), (pick2, m2))):
                tt(key[:], pick_k[:], rank[:], ALU.mult)
                link(nc.vector.tensor_reduce(at[:], key[:], AX_X, ALU.add))
                tt(key[:], pick_k[:], keep[:], ALU.mult)
                link(nc.vector.tensor_reduce(kept[:], key[:], AX_X, ALU.add))
                tt(E.gate[:, k, :], m[:], kept[:], ALU.mult)
                tt(tmp[:], at[:], kept[:], ALU.mult)
                nc.vector.tensor_copy(E.idx[:, 2 + k, :], tmp[:])
                spare = E.const(f"spare{k + 1}")
                tt(at[:], at[:], spare, ALU.subtract)
                tt(at[:], at[:], kept[:], ALU.mult)
                tt(at[:], at[:], spare, ALU.add)
                nc.vector.tensor_copy(E.idx[:, k, :], at[:]).then_inc(routed, 1)

        @block.gpsimd
        def _(pool):
            for k in range(2):
                pool.wait_ge(routed, k + 1)
                for j in range(TILES):
                    pool.indirect_dma_start(t["slots_in"], bass.IndirectOffsetOnAxis(ap=E.idx[:, k, j:j + 1], axis=0),
                                            E.bufH[:, j * P:(j + 1) * P], None).then_inc(scattered, 16)
            pool.wait_ge(scattered, 16 * 2 * TILES)


def experts(nc, t, sb, ps, sems, E):
    PER = CAP // CH
    with ExitStack() as st:
        def two(name, shape):
            return [sb(st, f"{name}{i}", shape) for i in range(2)]

        w1, w2 = two("w1_", [P, FFN]), two("w2_", [P, 4, D])
        xr, xT, yo = two("exr", [P, 4, D]), two("exT", [P, CH]), two("eyo", [P, 4, D])
        hid = two("ehid", [P, 4, CH])
        pX = ps(st, "e_pX", [P, CH])
        pH = ps(st, "e_pH", [P, 4, CH])
        pY = [ps(st, f"e_pY{i}", [P, 4, D]) for i in range(2)]
        w_in = sems(st, "e_w_in0", "e_w_in1")
        x_in = sems(st, "e_x_in0", "e_x_in1")
        y_out = sems(st, "e_y_out0", "e_y_out1")
        (turned, xT_ready, hidden, active, made, y_ready) = sems(
            st, "e_turned", "e_xT_ready", "e_hidden", "e_active", "e_made", "e_y_ready")
        src = t["slots_in"][0:SLOTS, :].rearrange("(c j p) d -> p c j d", p=P, j=4)
        dst = t["slots_out"].rearrange("(c j p) d -> p c j d", p=P, j=4)
        N = NE * PER
        block = st.enter_context(nc.Block())

        def chunk_turns(eng, lag):
            return turns_of(eng, N, lag, 2 * PER)

        @block.sync
        def _(sp):
            for s in chunk_turns(sp, 2):
                if c := s.back(0):
                    if c.phase % PER == 0:
                        e = c.phase // PER
                        if not (c.static and c.v < 2 * PER):
                            sp.wait_ge(made, c.times(1, -PER))
                        sp.dma_start(w1[e][:], t["w1"][:, bass.ds(c.expert(PER), 1), :]).then_inc(w_in[e], 16)
                        sp.dma_start(w2[e][:], t["w2"][:, bass.ds(c.expert(PER), 1), :, :]).then_inc(w_in[e], 16)
                    wait(sp, turned, c.times(1, -1))
                    sp.dma_start(xr[c.par][:], src[:, bass.ds(c.v, 1), :, :]).then_inc(x_in[c.par], 16)
                if c := s.back(2):
                    sp.wait_ge(y_ready, c.times(1, 1))
                    sp.dma_start(dst[:, bass.ds(c.v, 1), :, :], yo[c.par][:]).then_inc(y_out[c.par], 16)
            for k in range(2):
                sp.wait_ge(y_out[k], 16 * (N // 2))

        @block.tensor
        def _(pe):
            for s in chunk_turns(pe, 1):
                if c := s.back(0):
                    pe.wait_ge(x_in[c.par], c.loads())
                    wait(pe, xT_ready, c.times(1, 0))
                    for j in range(4):
                        i = nc.tensor.transpose(pX[:, j * P:(j + 1) * P], xr[c.par][:, j, :], E.ident)
                    i.then_inc(turned, 1)
                    if c.phase % PER == 0:
                        pe.wait_ge(w_in[c.phase // PER], c.weights(PER))
                    pe.wait_ge(xT_ready, c.times(1, 1))
                    for f in range(4):
                        wait(pe, active, c.times(4, f - 3))
                        nc.tensor.matmul(pH[:, f, :], w1[c.phase // PER][:, f * P:(f + 1) * P], xT[c.par][:],
                                         start=True, stop=True).then_inc(hidden, 1)
                if c := s.back(1):
                    wait(pe, y_ready, c.times(1, -1))
                    pe.wait_ge(active, c.times(4, 4))
                    for j in range(4):
                        for f in range(4):
                            i = nc.tensor.matmul(pY[c.par][:, j, :], hid[c.par][:, f, j * P:(j + 1) * P],
                                                 w2[c.phase // PER][:, f, :], start=(f == 0), stop=(f == 3))
                    i.then_inc(made, 1)

        @block.scalar
        def _(act):
            for s in chunk_turns(act, 0):
                if c := s.back(0):
                    wait(act, made, c.times(1, -1))
                    for f in range(4):
                        act.wait_ge(hidden, c.times(4, f + 1))
                        nc.scalar.activation(hid[c.par][:, f, :], pH[:, f, :], ACT.Gelu).then_inc(active, 1)

        @block.vector
        def _(dve):
            for s in chunk_turns(dve, 1):
                if c := s.back(0):
                    dve.wait_ge(turned, c.times(1, 1))
                    wait(dve, hidden, c.times(4, -4))
                    nc.vector.tensor_copy(xT[c.par][:], pX[:]).then_inc(xT_ready, 1)
                if c := s.back(1):
                    dve.wait_ge(made, c.times(1, 1))
                    if not (c.static and c.v < 2):
                        dve.wait_ge(y_out[c.par], c.loads() - 16)
                    nc.vector.tensor_copy(yo[c.par][:], pY[c.par][:]).then_inc(y_ready, 1)


class Chunk(Turn):

    def __init__(self, v, phase, n, static, period):
        super().__init__(v, phase % 2, n, static)
        self.phase, self.period = phase, period

    def back(self, k):
        if self.static:
            c = self.v - k
            return Chunk(c, c % self.period, self.n, True, self.period) if 0 <= c < self.n else None
        return Chunk(self.v - k if k else self.v, (self.phase - k) % self.period, self.n, False, self.period)

    def expert(self, per):
        if self.static:
            return self.v // per
        return self.pass_no * 2 + self.phase // per

    def weights(self, per):
        if self.static:
            return 32 * (self.v // self.period + 1)
        return self.pass_no * 32 + 32


def turns_of(eng, n, lag, period):
    for t in range(period):
        yield Chunk(t, t, n, True, period)
    with eng.Fori(1, n // period) as i:
        for k in range(period):
            c = Chunk(i * period + k, k, n, False, period)
            c.pass_no = i
            yield WithPass(c, i)
    for t in range(n, n + lag):
        yield Chunk(t, t % period, n, True, period)


class WithPass:
    def __init__(self, c, i):
        self.c, self.i = c, i

    def back(self, k):
        c = self.c.back(k)
        c.pass_no = self.i
        return c


def combine(nc, t, sb, ps, sems, E):
    with ExitStack() as st:
        def two(name, shape):
            return [sb(st, f"{name}{i}", shape) for i in range(2)]

        y = [two("cy0", [P, 4, D]), two("cy1", [P, 4, D])]
        ms, mo, fs, fg, fo = (two(n, [P, CH]) for n in ("cms", "cmo", "cfs", "cfg", "cfo"))
        pm = [ps(st, f"c_pm{i}", [P, CH]) for i in range(2)]
        y_in = sems(st, "c_y_in0", "c_y_in1")
        stored = sems(st, "c_stored0", "c_stored1")
        (weighted, moe_ready, turned, f_ready, scaled, o_ready) = sems(
            st, "c_weighted", "c_moe_ready", "c_turned", "c_f_ready", "c_scaled", "c_o_ready")
        block = st.enter_context(nc.Block())
        ha = E.bufA[:].rearrange("p (b s) -> p s b", s=S)

        @block.gpsimd
        def _(pool):
            for c in range(NCH + 2):
                if c >= 2:
                    d = c - 2
                    pool.wait_ge(scaled, d + 1)
                    if d >= 2:
                        pool.wait_ge(stored[d % 2], 16 * (d // 2))
                    nc.gpsimd.tensor_tensor(fo[d % 2][:], fg[d % 2][:], E.bufX[:, d * CH:(d + 1) * CH],
                                            ALU.add).then_inc(o_ready, 1)
                if c < NCH:
                    if c >= 2:
                        pool.wait_ge(moe_ready, c - 1)
                    for j in range(4):
                        for k in range(2):
                            pool.indirect_dma_start(
                                y[k][c % 2][:, j, :], None, t["slots_out"],
                                bass.IndirectOffsetOnAxis(ap=E.idx[:, 2 + k, 4 * c + j:4 * c + j + 1], axis=0)
                            ).then_inc(y_in[c % 2], 16)

        @block.vector
        def _(dve):
            for s in turns(dve, NCH, 1):
                if c := s.back(0):
                    dve.wait_ge(y_in[c.par], (c.v - c.par) * 64 + 128 if c.par else c.v * 64 + 128)
                    wait(dve, turned, c.times(1, -1))
                    for j in range(4):
                        i = nc.vector.tensor_scalar(ms[c.par][:, j * P:(j + 1) * P], y[0][c.par][:, j, :],
                                                    E.gate[:, 0, bass.ds(c.v * 4 + j, 1)], None, ALU.mult)
                    i.then_inc(weighted, 1)
                    dve.wait_ge(weighted, c.times(1, 1))
                    for j in range(4):
                        i = nc.vector.scalar_tensor_tensor(mo[c.par][:, j * P:(j + 1) * P], y[1][c.par][:, j, :],
                                                           E.gate[:, 1, bass.ds(c.v * 4 + j, 1)],
                                                           ms[c.par][:, j * P:(j + 1) * P], ALU.mult, ALU.add)
                    i.then_inc(moe_ready, 1)
                if c := s.back(1):
                    dve.wait_ge(turned, c.times(1, 1))
                    wait(dve, scaled, c.times(1, -1))
                    nc.vector.tensor_tensor(fs[c.par][:].rearrange("p (s b) -> p s b", b=B),
                                            pm[c.par][:].rearrange("p (s b) -> p s b", b=B),
                                            ha[:, bass.ds(c.v * 2, 2), :], ALU.add).then_inc(f_ready, 1)

        @block.tensor
        def _(pe):
            for s in turns(pe, NCH, 0):
                if c := s.back(0):
                    pe.wait_ge(moe_ready, c.times(1, 1))
                    wait(pe, f_ready, c.times(1, -1))
                    for j in range(4):
                        i = nc.tensor.transpose(pm[c.par][:, j * P:(j + 1) * P], mo[c.par][:, j * P:(j + 1) * P], E.ident)
                    i.then_inc(turned, 1)

        @block.scalar
        def _(act):
            for s in turns(act, NCH, 0):
                if c := s.back(0):
                    act.wait_ge(f_ready, c.times(1, 1))
                    wait(act, o_ready, c.times(1, -1))
                    for k in range(2):
                        i = nc.scalar.activation(fg[c.par][:, k * B:(k + 1) * B], fs[c.par][:, k * B:(k + 1) * B],
                                                 ACT.Copy, scale=E.mod[:, 5, bass.ds(c.v * 2 + k, 1)])
                    i.then_inc(scaled, 1)

        @block.sync
        def _(sp):
            for s in turns(sp, NCH, 0):
                if c := s.back(0):
                    sp.wait_ge(o_ready, c.times(1, 1))
                    sp.dma_start(t["out"][:, bass.ds(c.v * CH, CH)], fo[c.par][:]).then_inc(stored[c.par], 16)
            for k in range(2):
                sp.wait_ge(stored[k], 16 * (NCH // 2))


def lay_out(i):
    def f(name):
        return np.asarray(i[name])

    def halves(a):
        a = a.reshape(2, P, -1)
        return a.transpose(1, 0, 2)

    x = f("L0_attn_x").reshape(NT, D)
    qkv = f("L0_ffn_qkv_weight").reshape(NKV, 32, D)
    rep = NH // NKV
    q = qkv[:, :16].reshape(P, D)
    k = np.repeat(qkv[:, None, 16:24], rep, axis=1).reshape(P, D)
    v = np.repeat(qkv[:, None, 24:32], rep, axis=1).reshape(P, D)
    cols = np.concatenate([
        f("L0_attn_bi").reshape(4, P).T,
        halves(f("L0_attn_conv_w").reshape(DI, DCONV)).reshape(P, 8),
        f("L0_attn_conv_b").reshape(2, P).T, f("L0_attn_bdt").reshape(2, P).T,
        f("L0_attn_bo").reshape(P, 1), f("L0_attn_Dv").reshape(2, P).T,
        f("L0_ffn_ln1_weight").reshape(P, 1), f("L0_ffn_ln1_bias").reshape(P, 1),
        f("L0_ffn_ln2_weight").reshape(P, 1), f("L0_ffn_ln2_bias").reshape(P, 1)], axis=1)
    out = {
        "con": np.concatenate(list(CONST.values()), axis=1),
        "x": x.reshape(TILES, P, D).transpose(1, 0, 2),
        "xT": x.T,
        "wi": f("L0_attn_Wi").T,
        "wdt": f("L0_attn_Wdt").T,
        "wo": halves(f("L0_attn_Wo").T),
        "wq": q.T, "wk": k.T, "wv": v.T,
        "wproj": f("L0_ffn_proj_weight").T,
        "router": f("L0_ffn_router_weight"),
        "cols": cols,
        "alog": halves(f("L0_attn_A_log")), "bm": halves(f("L0_attn_Bm")), "cm": halves(f("L0_attn_Cm")),
        "ct": f("L0_c").T,
        "wmod": f("L0_wmod").reshape(P, 6, D),
        "w1": f("L0_ffn_moe_w1").transpose(1, 0, 2),
        "w2": f("L0_ffn_moe_w2").reshape(NE, 4, P, D).transpose(2, 0, 1, 3),
    }
    return {k: np.ascontiguousarray(v) for k, v in out.items()}


STOP = None


def kernel(**inputs):
    import concourse.bacc as _bacc
    from concourse.bass_utils import run_bass_kernel_spmd as _run

    nc = _bacc.Bacc("TRN2", target_bir_lowering=False, num_devices=1)
    arrays, t = {}, {}
    for name, a in lay_out(inputs).items():
        arrays[f"in_{name}"] = a
        t[name] = nc.dram_tensor(f"in_{name}", a.shape, F32, kind="ExternalInput").ap()
    t["out"] = nc.dram_tensor("out_0", [P, NT], F32, kind="ExternalOutput").ap()
    t["slots_in"] = nc.dram_tensor("slots_in", [SLOTS + 2 * NT, D], F32, kind="Internal").ap()
    t["slots_out"] = nc.dram_tensor("slots_out", [SLOTS, D], F32, kind="Internal").ap()
    build(nc, t, STOP)
    r = _run(nc, [arrays], core_ids=[0])
    return np.ascontiguousarray(r.results[0]["out_0"].T.reshape(S, B, D))
```

```python
from contextlib import ExitStack

import numpy as np

import concourse.bass as bass
from concourse import mybir

F32 = mybir.dt.float32
U32 = mybir.dt.uint32
ALU = mybir.AluOpType
ACT = mybir.ActivationFunctionType
AX_X = mybir.AxisListType.X

P = 128
S, B, D = 32, 256, 128
NT = S * B
DI, NST, DCONV, DTR = 256, 16, 4, 32
NH, NKV, HD = 16, 8, 8
KV = NKV * HD
NE, FFN = 8, 512
CAP = -(-NT * 2 * 5 // (NE * 4))
SLOTS = NE * CAP
EPS = 1e-5
BIG = 3e38
NEG = -1e30

CH = 512
NCH = NT // CH
GR = 1024
GS = GR // B
NG = NT // GR
PADB = B + DCONV - 1
RING = 4
TILES = NT // P
ROW = D + 4
EMPTY = 5 * 8 * P
Q = 4
QC, QT = NCH // Q, TILES // Q


def constants():
    p = np.arange(P)
    causal = np.where(np.arange(S)[None, :] <= (p % S)[:, None], 0.0, NEG)
    tile_token = np.arange(TILES)[None, :] * P + p[:, None]
    t = {
        "ident": np.eye(P),
        "ones": np.ones((P, P)),
        "before": (p[:, None] < p[None, :]) * 1.0,
        "causal": causal,
        "head4": ((p[:, None] // HD) % 4 == np.arange(4)[None, :]) * 1.0,
        "slot0": np.tile(np.arange(NE) * float(CAP), (P, 1)),
        "rev": np.tile(NE - np.arange(NE) * 1.0, (P, 1)),
        "eps": np.full((P, 1), EPS),
        "big": np.full((P, 1), BIG),
        "expert": np.tile(np.arange(NE) * 1.0, (P, 1)),
        "token": tile_token,
        "empty": NT + (np.arange(5)[None, :, None] * 8 * P + p[:, None, None] * 8 + np.arange(8)[None, None, :]).reshape(P, 40),
    }
    return {k: np.ascontiguousarray(v, dtype=np.float32) for k, v in t.items()}


CONST = constants()
CONST_AT = {}
_n = 0
for _k, _v in CONST.items():
    CONST_AT[_k] = (_n, _n + _v.shape[1])
    _n += _v.shape[1]
CONST_COLS = _n


def wait(eng, sem, value):
    if isinstance(value, int) and value <= 0:
        return
    eng.wait_ge(sem, value)


class Turn:

    def __init__(self, v, par, n, static):
        self.v, self.par, self.n, self.static = v, par, n, static

    def back(self, k):
        if self.static:
            c = self.v - k
            return Turn(c, c % 2, self.n, True) if 0 <= c < self.n else None
        return Turn(self.v - k if k else self.v, (self.par - k) % 2, self.n, False)

    def times(self, per, plus=0):
        return self.v * per + plus

    def count(self, plus):
        return self.v + plus if plus else self.v

    def upto(self, k):
        return min(self.v - k, self.n) if self.static else self.count(-k)

    def loads(self):
        return (self.v - self.par) * 8 + 16 if self.par else self.v * 8 + 16


def turns(eng, n, lag):
    head = lag + 2 + (lag % 2)
    for t in range(head):
        yield Turn(t, t % 2, n, True)
    if n > head:
        with eng.Fori(head // 2, n // 2) as i:
            yield Turn(i * 2, 0, n, False)
            yield Turn(i * 2 + 1, 1, n, False)
    for t in range(max(n, head), n + lag):
        yield Turn(t, t % 2, n, True)


def steps(n, lag):
    for t in range(n + lag):
        yield Turn(t, t % 2, n, True)


def build(nc, t, stop_after=None):
    top = ExitStack()

    def sb(stack, name, shape, dt=F32):
        return stack.enter_context(nc.sbuf_tensor(name, shape, dt))

    def ps(stack, name, shape):
        return stack.enter_context(nc.psum_tensor(name, shape, F32))

    def sems(stack, *names):
        return [stack.enter_context(nc.semaphore(n)) for n in names]

    with top:
        E = Resident()
        E.con = sb(top, "con", [P, CONST_COLS])
        E.ident, E.ones, E.eps = E.const("ident"), E.const("ones"), E.const("eps")
        E.wi = sb(top, "wi", [P, 4 * P])
        E.wdt = sb(top, "wdt", [DTR, DI])
        E.wo = sb(top, "wo", [P, 2, D])
        E.wq = sb(top, "wq", [P, 2, KV])
        E.wk = sb(top, "wk", [P, KV])
        E.wv = sb(top, "wv", [P, KV])
        E.wp = sb(top, "wp", [P, 2, 2, D])
        E.router = sb(top, "router", [P, NE])
        E.cols = sb(top, "cols", [P, NCOLS])
        E.mod = sb(top, "mod", [P, 6, S])
        E.skip = sb(top, "skip", [P, 2, S])
        E.A = sb(top, "A", [P, 2, NST])
        E.bufX = sb(top, "bufX", [P, NT])
        E.bufH = sb(top, "bufH", [P, NT])

        with ExitStack() as scan_stack:
            E.cb = sb(scan_stack, "cb", [P, 2, NST])
            E.diag_cb = sb(scan_stack, "diag_cb", [P, 2, NST, P])
            prep(nc, t, sb, ps, sems, E)
            norm_in(nc, t, sb, ps, sems, E)
            scan_phase(nc, t, sb, ps, sems, E)
        if stop_after == "scan":
            return dump(nc, t, sems, E.bufX)
        E.bufA = sb(top, "bufA", [P, NT])
        norm_mid(nc, t, sb, ps, sems, E)
        if stop_after == "mid":
            return dump(nc, t, sems, E.bufH)
        attention(nc, t, sb, ps, sems, E)
        if stop_after == "attn":
            return dump(nc, t, sems, E.bufA)
        norm_route(nc, t, sb, ps, sems, E)
        experts(nc, t, sb, ps, sems, E)
        combine(nc, t, sb, ps, sems, E)


COLS = {}
_c = 0
for _name, _w in (("bi", 4), ("conv_w", 8), ("conv_b", 2), ("bdt", 2), ("bo", 1), ("dv", 2),
                  ("ln1w", 1), ("ln1b", 1), ("ln2w", 1), ("ln2b", 1)):
    COLS[_name] = _c
    _c += _w
NCOLS = _c


class Resident:

    def col(self, name, k=0):
        lo = COLS[name] + k
        return self.cols[:, lo:lo + 1]

    def const(self, name):
        lo, hi = CONST_AT[name]
        return self.con[:, lo:hi]


def dump(nc, t, sems, buf):
    with ExitStack() as st:
        (stored,) = sems(st, "stored")
        block = st.enter_context(nc.Block())

        @block.sync
        def _(sp):
            sp.dma_start(t["out"], buf[:]).then_inc(stored, 16)
            sp.wait_ge(stored, 16)


def prep(nc, t, sb, ps, sems, E):
    with ExitStack() as st:
        alog = sb(st, "alog", [P, 2, NST])
        bm = sb(st, "bm", [P, 2, NST])
        cm = sb(st, "cm", [P, 2, NST])
        ct = sb(st, "ct", [P, S])
        sct = sb(st, "sct", [P, S])
        wmod = sb(st, "wmod", [P, 6, D])
        aexp = sb(st, "aexp", [P, 2, NST])
        sign = sb(st, "sign", [P, S])
        mag = sb(st, "mag", [P, S])
        dvm = sb(st, "dvm", [P, 1])
        pmod = ps(st, "pmod", [P, 6, S])
        pdv = ps(st, "pdv", [P, 1])
        (loaded, c_silu, a_exp, mod_ready, dv_ready, done, x_loaded) = sems(
            st, "loaded", "c_silu", "a_exp", "mod_ready", "dv_ready", "prep_done", "x_all_loaded")
        pairs = [(E.con[:], "con"), (E.wi[:], "wi"), (E.wdt[:], "wdt"), (E.wo[:], "wo"), (E.wq[:], "wq"),
                 (E.wk[:], "wk"), (E.wv[:], "wv"), (E.wp[:], "wp"), (E.router[:], "router"),
                 (E.cols[:], "cols"), (alog[:], "alog"), (bm[:], "bm"), (cm[:], "cm"),
                 (ct[:], "ct"), (wmod[:], "wmod")]
        block = st.enter_context(nc.Block())

        @block.sync
        def _(sp):
            for dst, name in pairs:
                sp.dma_start(dst, t[name]).then_inc(loaded, 16)
            sp.dma_start(E.bufH[:], t["x"].rearrange("p n d -> p (n d)")).then_inc(x_loaded, 16)
            sp.dma_start(E.bufX[:], t["xT"]).then_inc(x_loaded, 16)
            sp.wait_ge(x_loaded, 32)

        @block.scalar
        def _(act):
            act.wait_ge(loaded, 16 * len(pairs))
            nc.scalar.activation(sct[:], ct[:], ACT.Silu).then_inc(c_silu, 1)
            nc.scalar.activation(aexp[:], alog[:], ACT.Exp).then_inc(a_exp, 1)

        @block.tensor
        def _(pe):
            pe.wait_ge(loaded, 16 * len(pairs))
            for k in range(2):
                mm = nc.tensor.matmul(pdv[:], E.ones, E.col("dv", k), start=(k == 0), stop=(k == 1))
            mm.then_inc(dv_ready, 1)
            pe.wait_ge(c_silu, 1)
            for k in range(6):
                mm = nc.tensor.matmul(pmod[:, k, :], wmod[:, k, :], sct[:], start=True, stop=True)
            mm.then_inc(mod_ready, 1)

        @block.vector
        def _(dve):
            n = 0

            def link(ins):
                nonlocal n
                n += 1
                ins.then_inc(done, 1)
                dve.wait_ge(done, n)

            dve.wait_ge(loaded, 16 * len(pairs))
            nc.vector.tensor_tensor(E.cb[:], cm[:], bm[:], ALU.mult)
            dve.wait_ge(dv_ready, 1)
            link(nc.vector.tensor_scalar(dvm[:], pdv[:], 1.0 / DI, None, ALU.mult))
            dve.wait_ge(a_exp, 1)
            nc.vector.tensor_scalar(E.A[:], aexp[:], -1.0, -1e-30, ALU.mult, ALU.min)
            dve.wait_ge(mod_ready, 1)
            link(nc.vector.tensor_copy(E.mod[:], pmod[:]))
            for k in (1, 4):
                nc.vector.tensor_scalar(E.mod[:, k, :], E.mod[:, k, :], 1.0, None, ALU.add)
            for k in (2, 5):
                link(nc.vector.tensor_scalar(mag[:], E.mod[:, k, :], -1.0, 0.25, ALU.mult, ALU.max))
                link(nc.vector.tensor_tensor(mag[:], mag[:], E.mod[:, k, :], ALU.max))
                link(nc.vector.tensor_scalar(sign[:], E.mod[:, k, :], 0.0, None, ALU.is_ge))
                link(nc.vector.tensor_scalar(sign[:], sign[:], 2.0, -1.0, ALU.mult, ALU.add))
                link(nc.vector.tensor_tensor(E.mod[:, k, :], sign[:], mag[:], ALU.mult))
            link(nc.vector.tensor_scalar(mag[:], E.mod[:, 1, :], dvm[:, 0:1], None, ALU.mult))
            link(nc.vector.tensor_tensor(E.skip[:, 0, :], mag[:], E.mod[:, 2, :], ALU.mult))
            link(nc.vector.tensor_scalar(sign[:], E.mod[:, 0, :], dvm[:, 0:1], E.col("bo"), ALU.mult, ALU.add))
            link(nc.vector.tensor_tensor(E.skip[:, 1, :], sign[:], E.mod[:, 2, :], ALU.mult))


def norm_in(nc, t, sb, ps, sems, E):
    with ExitStack() as st:
        xn = [sb(st, f"xn{i}", [P, CH]) for i in range(2)]
        sk = [sb(st, f"sk{i}", [P, CH]) for i in range(2)]
        stats = [sb(st, f"stats{i}", [P, 4, 6]) for i in range(2)]
        mv = [sb(st, f"mv{i}", [P, 4, 2]) for i in range(2)]
        std = [sb(st, f"std{i}", [P, 4]) for i in range(2)]
        rstd = [sb(st, f"rstd{i}", [P, 4]) for i in range(2)]
        spare = sb(st, "spare", [P, 1])
        pt = [ps(st, f"pt{i}", [P, CH]) for i in range(2)]
        (stats_made, mv_ready, std_ready, rstd_ready, normed, turned, h_ready, skip_added) = sems(
            st, "stats_made", "mv_ready", "std_ready", "rstd_ready", "normed", "turned", "h_ready", "skip_added")
        block = st.enter_context(nc.Block())

        @block.vector
        def _(dve):
            for s in turns(dve, NCH, 1):
                if c := s.back(0):
                    for j in range(4):
                        i = nc.vector.bn_stats(stats[c.par][:, j, :], E.bufH[:, bass.ds(c.v * CH + j * P, P)])
                    i.then_inc(stats_made, 1)
                    dve.wait_ge(stats_made, c.times(1, 1))
                    nc.vector.tensor_copy(spare[:], E.eps)
                    for j in range(4):
                        i = nc.vector.bn_aggr(mv[c.par][:, j, :], stats[c.par][:, j, :])
                    i.then_inc(mv_ready, 1)
                if c := s.back(1):
                    dve.wait_ge(std_ready, c.times(1, 1))
                    wait(dve, turned, c.times(1, -1))
                    nc.vector.reciprocal(rstd[c.par][:], std[c.par][:]).then_inc(rstd_ready, 1)
                    dve.wait_ge(rstd_ready, c.times(1, 1))
                    for j in range(4):
                        i = nc.vector.tensor_scalar(xn[c.par][:, j * P:(j + 1) * P], E.bufH[:, bass.ds(c.v * CH + j * P, P)],
                                                    mv[c.par][:, j, 0:1], rstd[c.par][:, j:j + 1],
                                                    ALU.subtract, ALU.mult)
                    i.then_inc(normed, 1)

        @block.tensor
        def _(pe):
            for s in turns(pe, NCH, 1):
                if c := s.back(1):
                    pe.wait_ge(normed, c.times(1, 1))
                    wait(pe, h_ready, c.times(1, -1))
                    for j in range(4):
                        i = nc.tensor.transpose(pt[c.par][:, j * P:(j + 1) * P], xn[c.par][:, j * P:(j + 1) * P], E.ident)
                    i.then_inc(turned, 1)

        @block.scalar
        def _(act):
            for s in turns(act, NCH, 2):
                if c := s.back(0):
                    act.wait_ge(mv_ready, c.times(1, 1))
                    nc.scalar.activation(std[c.par][:], mv[c.par][:, :, 1], ACT.Sqrt, bias=E.eps).then_inc(std_ready, 1)
                if c := s.back(2):
                    act.wait_ge(turned, c.times(1, 1))
                    wait(act, skip_added, c.times(1, -1))
                    for k in range(2):
                        at = bass.ds(c.v * 2 + k, 1)
                        nc.scalar.activation(sk[c.par][:, k * B:(k + 1) * B], pt[c.par][:, k * B:(k + 1) * B],
                                             ACT.Identity, bias=E.skip[:, 1, at], scale=E.skip[:, 0, at])
                        i = nc.scalar.activation(E.bufH[:, bass.ds(c.v * CH + k * B, B)], pt[c.par][:, k * B:(k + 1) * B],
                                                 ACT.Identity, bias=E.mod[:, 0, at], scale=E.mod[:, 1, at])
                    i.then_inc(h_ready, 1)

        @block.gpsimd
        def _(pool):
            def diagonals(c):
                for q in range(2 * c, 2 * c + 2):
                    nc.gpsimd.tensor_scalar(E.diag_cb[:, q // NST, q % NST, :], E.ident,
                                            E.cb[:, q // NST, q % NST:q % NST + 1], None, ALU.mult)

            for c in range(NCH):
                diagonals(c)
                pool.wait_ge(h_ready, c + 1)
                x = E.bufX[:, c * CH:(c + 1) * CH]
                nc.gpsimd.tensor_tensor(x, x, sk[c % 2][:], ALU.add).then_inc(skip_added, 1)


def scan_phase(nc, t, sb, ps, sems, E):
    ITEMS = 2 * NST
    with ExitStack() as st:
        xin = [sb(st, f"xin{i}", [P, GS, PADB]) for i in range(2)]
        u = [sb(st, f"u{i}", [P, 2, GR]) for i in range(2)]
        dt = [sb(st, f"dt{i}", [P, 2, GR]) for i in range(2)]
        z = [sb(st, f"z{i}", [P, 2, GR]) for i in range(2)]
        tap = [sb(st, f"tap{i}", [P, GR]) for i in range(2)]
        soft = [sb(st, f"soft{i}", [P, GR]) for i in range(2)]
        a = [sb(st, f"a{i}", [P, GR]) for i in range(RING)]
        g_ = [sb(st, f"g{i}", [P, GR]) for i in range(RING)]
        yg = [sb(st, f"yg{i}", [P, GR]) for i in range(2)]
        mix = sb(st, "mix", [P, GR])
        fp = [ps(st, f"fp{i}", [P, GR]) for i in range(2)]
        yp = [ps(st, f"yp{i}", [P, GR]) for i in range(2)]
        (padded, filled, drained, tap_ready, tap_added, relu_ready, exp1_ready, soft_ready, dt_added, u_ready,
         w_ready, dt_set, decay_ready, scanned, summed, gated, x1_ready) = sems(
            st, "padded", "filled", "drained", "tap_ready", "tap_added", "relu_ready", "exp1_ready", "soft_ready",
            "dt_added", "u_ready", "w_ready", "dt_set", "decay_ready", "scanned", "summed", "gated", "x1_ready")

        OUT, XIN0, DT0, Z0 = 0, 1, 3, 5

        def unit(g, k):
            if isinstance(g, int) and g < 1:
                return 6 * (g + 1) + k - 1
            if isinstance(g, int) and g == NG:
                return unit(NG - 1, 0) + 1
            return g * 7 + (5 + k)

        def slot(par, g, k):
            if isinstance(g, int):
                return unit(g, k) % 2
            return (par + 5 + k) % 2

        def groups(eng, slots):
            slots(-1, 1, False, True)
            slots(0, 0, False, True)
            with eng.Fori(0, NG // 2 - 1) as i:
                slots(i * 2 + 1, 1, True, True)
                slots(i * 2 + 2, 0, True, True)
            slots(NG - 1, 1, True, False)
            slots(NG, 0, True, False)

        block = st.enter_context(nc.Block())

        @block.tensor
        def _(pe):
            def project(g, par, k, m):
                f = fp[slot(par, g, k)]
                wait(pe, drained, unit(g, k) - 1)
                for n in range(2):
                    i = nc.tensor.matmul(f[:, n * CH:(n + 1) * CH], E.wi[:, m * P:(m + 1) * P],
                                         E.bufH[:, bass.ds((g + 1) * GR + n * CH, CH)], start=True, stop=True)
                i.then_inc(filled, 1)

            def project_dt(g, par, k, h):
                f = fp[slot(par, g, k)]
                wait(pe, drained, unit(g, k) - 1)
                pe.wait_ge(drained, unit(g, XIN0) + 1)
                for n in range(2):
                    i = nc.tensor.matmul(f[:, n * CH:(n + 1) * CH], E.wdt[:, h * P:(h + 1) * P],
                                         xin[0][0:DTR, 2 * n:2 * n + 2, DCONV - 1:PADB], start=True, stop=True)
                i.then_inc(filled, 1)

            def output(g, par):
                f = fp[slot(par, g, OUT)]
                wait(pe, drained, unit(g, OUT) - 1)
                pe.wait_ge(gated, g * 2)
                for n in range(2):
                    o = f[:, n * CH:(n + 1) * CH]
                    nc.tensor.matmul(o, E.wo[:, 0, :], yg[0][:, n * CH:(n + 1) * CH], start=True, stop=False)
                    i = nc.tensor.matmul(o, E.wo[:, 1, :], yg[1][:, n * CH:(n + 1) * CH], start=False, stop=True)
                i.then_inc(filled, 1)

            def sum_states(g, j):
                h, n = j // NST, j % NST
                if n == 0:
                    wait(pe, gated, g * 2 + h - 1)
                pe.wait_ge(scanned, g * ITEMS + j + 1)
                for q in range(2):
                    i = nc.tensor.matmul(yp[h][:, q * CH:(q + 1) * CH], E.diag_cb[:, h, n, :],
                                         g_[j % RING][:, q * CH:(q + 1) * CH], start=(n == 0), stop=(n == NST - 1))
                i.then_inc(summed, 1)

            def slots(g, par, prev, nxt):
                scans = nxt or (isinstance(g, int) and g == NG - 1)
                if isinstance(g, int) and g < 0:
                    scans = False
                for j in range(ITEMS):
                    if j == 4 and prev:
                        output(g, par)
                    if nxt:
                        if j in (6, 8):
                            project(g, par, XIN0 + (j - 6) // 2, (j - 6) // 2)
                        if j in (12, 14):
                            project_dt(g, par, DT0 + (j - 12) // 2, (j - 12) // 2)
                        if j in (24, 26):
                            project(g, par, Z0 + (j - 24) // 2, 2 + (j - 24) // 2)
                    if scans:
                        sum_states(g, j)

            pe.wait_ge(padded, 2)
            groups(pe, slots)

        @block.scalar
        def _(act):
            def evac_xin(g, par, h):
                k = XIN0 + h
                act.wait_ge(filled, unit(g, k) + 1)
                wait(act, tap_ready, (g + 1) * 8)
                i = nc.scalar.activation(xin[h][:, :, DCONV - 1:PADB], fp[slot(par, g, k)][:].rearrange("p (s b) -> p s b", s=GS),
                                         ACT.Identity, bias=E.col("bi", h))
                i.then_inc(drained, 1)

            def taps(g, par, h, ks):
                act.wait_ge(drained, unit(g, XIN0 + h) + 1)
                for k in ks:
                    src = xin[h][:, :, k:k + B]
                    w = E.col("conv_w", h * 4 + k)
                    n = (g + 1) * 6 + h * 3 + k - 1
                    if k == 0:
                        wait(act, scanned, g * ITEMS)
                        dst = u[1 - par][:, h, :].rearrange("p (s b) -> p s b", s=GS)
                        i = nc.scalar.activation(dst, src, ACT.Identity, bias=E.col("conv_b", h), scale=w)
                    else:
                        wait(act, tap_added, n - 1)
                        dst = tap[(h * 3 + k - 1) % 2][:].rearrange("p (s b) -> p s b", s=GS)
                        i = nc.scalar.activation(dst, src, ACT.Identity, scale=w)
                    i.then_inc(tap_ready, 1)

            def soft_plus(g, par, h, part):
                k = DT0 + h
                if part == 0:
                    act.wait_ge(filled, unit(g, k) + 1)
                    wait(act, dt_added, (g + 1) * 2 + h - 1)
                    nc.scalar.activation(dt[1 - par][:, h, :], fp[slot(par, g, k)][:], ACT.Relu,
                                         bias=E.col("bdt", h)).then_inc(relu_ready, 1)
                    i = nc.scalar.activation(soft[h][:], fp[slot(par, g, k)][:], ACT.Abs, bias=E.col("bdt", h))
                    i.then_inc(drained, 1)
                elif part == 1:
                    act.wait_ge(drained, unit(g, k) + 1)
                    nc.scalar.activation(soft[h][:], soft[h][:], ACT.Exp, scale=-1.0).then_inc(exp1_ready, 1)
                else:
                    act.wait_ge(exp1_ready, (g + 1) * 2 + h + 1)
                    nc.scalar.activation(soft[h][:], soft[h][:], ACT.Ln, bias=E.ones[:, 0:1]).then_inc(soft_ready, 1)

            def silu_u(g, par, h):
                act.wait_ge(tap_added, (g + 1) * 6 + 3 * h + 3)
                nc.scalar.activation(u[1 - par][:, h, :], u[1 - par][:, h, :], ACT.Silu).then_inc(u_ready, 1)

            def silu_z(g, par, h):
                k = Z0 + h
                act.wait_ge(filled, unit(g, k) + 1)
                wait(act, gated, g * 2)
                i = nc.scalar.activation(z[1 - par][:, h, :], fp[slot(par, g, k)][:], ACT.Silu, bias=E.col("bi", 2 + h))
                i.then_inc(drained, 1)

            def evac_out(g, par):
                act.wait_ge(filled, unit(g, OUT) + 1)
                wait(act, x1_ready, g - 1)
                for s in range(GS):
                    at = bass.ds((g - 1) * GS + s, 1)
                    i = nc.scalar.activation(mix[:, s * B:(s + 1) * B], fp[slot(par, g, OUT)][:, s * B:(s + 1) * B],
                                             ACT.Identity, scale=E.mod[:, 2, at])
                i.then_inc(drained, 1)

            def decay(g, par, j):
                h, n = j // NST, j % NST
                if j == 0:
                    act.wait_ge(dt_set, g + 1)
                wait(act, scanned, g * ITEMS + j - RING + 1)
                nc.scalar.activation(a[j % RING][:], dt[par][:, h, :], ACT.Exp, scale=E.A[:, h, n:n + 1]).then_inc(decay_ready, 1)

            def slots(g, par, prev, nxt):
                scans = not (isinstance(g, int) and (g < 0 or g == NG))
                for j in range(ITEMS):
                    if scans:
                        decay(g, par, j)
                    if j == 5 and prev:
                        evac_out(g, par)
                    if nxt:
                        if j == 7:
                            evac_xin(g, par, 0)
                        if j == 9:
                            taps(g, par, 0, (0, 1))
                        if j == 10:
                            evac_xin(g, par, 1)
                        if j == 11:
                            taps(g, par, 0, (2, 3))
                        if j in (12, 13):
                            taps(g, par, 1, ((0, 1), (2, 3))[j - 12])
                        if j in (14, 16):
                            soft_plus(g, par, (j - 14) // 2, 0)
                        if j in (15, 17):
                            soft_plus(g, par, (j - 15) // 2, 1)
                        if j == 27:
                            soft_plus(g, par, 0, 2)
                            soft_plus(g, par, 1, 2)
                            silu_u(g, par, 0)
                            silu_u(g, par, 1)
                            silu_z(g, par, 0)
                            silu_z(g, par, 1)

            act.wait_ge(padded, 2)
            groups(act, slots)

        @block.gpsimd
        def _(pool):
            def slots(g, par, prev, nxt):
                if prev:
                    pool.wait_ge(drained, unit(g, OUT) + 1)
                    x1 = E.bufX[:, bass.ds((g - 1) * GR, GR)]
                    nc.gpsimd.tensor_tensor(x1, x1, mix[:], ALU.add).then_inc(x1_ready, 1)
                if nxt:
                    for h in range(2):
                        uh = u[1 - par][:, h, :]
                        for k in range(1, DCONV):
                            pool.wait_ge(tap_ready, (g + 1) * 8 + h * 4 + k + 1)
                            wait(pool, tap_added, (g + 1) * 6 + h * 3 + k - 1)
                            nc.gpsimd.tensor_tensor(uh, uh, tap[(h * 3 + k - 1) % 2][:], ALU.add).then_inc(tap_added, 1)
                    for h in range(2):
                        dh = dt[1 - par][:, h, :]
                        pool.wait_ge(soft_ready, (g + 1) * 2 + h + 1)
                        nc.gpsimd.tensor_tensor(dh, dh, soft[h][:], ALU.add).then_inc(dt_added, 1)
                    for h in range(2):
                        uh, dh = u[1 - par][:, h, :], dt[1 - par][:, h, :]
                        pool.wait_ge(u_ready, (g + 1) * 2 + h + 1)
                        pool.wait_ge(dt_added, (g + 1) * 2 + h + 1)
                        nc.gpsimd.tensor_tensor(uh, uh, dh, ALU.mult).then_inc(w_ready, 1)
                    pool.wait_ge(w_ready, (g + 1) * 2 + 2)
                    firsts = dt[1 - par][:].rearrange("p h (s b) -> p (h s) b", s=GS)[:, :, 0:1]
                    nc.gpsimd.tensor_tensor(firsts, firsts, E.const("big").unsqueeze(1).to_broadcast([P, 2 * GS, 1]),
                                            ALU.add).then_inc(dt_set, 1)

            for h in range(2):
                nc.gpsimd.memset(xin[h][:, :, 0:DCONV - 1], 0.0).then_inc(padded, 1)
            groups(pool, slots)

        @block.vector
        def _(dve):
            def gate_y(g, h, par):
                dve.wait_ge(summed, g * ITEMS + (h + 1) * NST)
                if h == 0:
                    dve.wait_ge(drained, unit(g - 1, Z0 + 1) + 1)
                if not (isinstance(g, int) and g == 0):
                    dve.wait_ge(filled, unit(g, OUT) + 1)
                nc.vector.tensor_tensor(yg[h][:], yp[h][:], z[par][:, h, :], ALU.mult).then_inc(gated, 1)

            def slots(g, par, prev, nxt):
                scans = not (isinstance(g, int) and (g < 0 or g == NG))
                for j in range(ITEMS):
                    h = j // NST
                    if scans:
                        if j % NST == 0:
                            dve.wait_ge(w_ready, g * 2 + h + 1)
                        dve.wait_ge(decay_ready, g * ITEMS + j + 1)
                        wait(dve, summed, g * ITEMS + j - RING + 1)
                        nc.vector.tensor_tensor_scan(g_[j % RING][:], a[j % RING][:], u[par][:, h, :], 0.0,
                                                     ALU.mult, ALU.add).then_inc(scanned, 1)
                    if j == 2 and prev:
                        gate_y(g - 1, 1, 1 - par)
                    if j == NST + 2 and scans:
                        gate_y(g, 0, par)

            groups(dve, slots)


def norm_mid(nc, t, sb, ps, sems, E):
    NB = CH // S
    with ExitStack() as st:
        def two(name, shape):
            return [sb(st, f"{name}{i}", shape) for i in range(2)]

        xb, xn, hm, hb, xm = (two(n, [P, CH]) for n in ("mxb", "mxn", "mhm", "mhb", "mxm"))
        stats = [two("mstatsA", [P, 4, 6]), two("mstatsB", [P, 4, 6])]
        mv = [two("mmvA", [P, 4, 2]), two("mmvB", [P, 4, 2])]
        std = [two("mstdA", [P, 4]), two("mstdB", [P, 4])]
        rstd = [two("mrstdA", [P, 4]), two("mrstdB", [P, 4])]
        pp = [[ps(st, f"mp{k}{i}", [P, CH]) for i in range(2)] for k in range(4)]
        shift = two("mshift", [P, 4])
        blank = sb(st, "blank", [P, 5, 8, ROW])
        spare = sb(st, "mspare", [P, 1])
        (xb_ready, scaled, h_ready, h_kept, zeroed, blanked, cleared) = sems(
            st, "m_xb_ready", "m_scaled", "m_h_ready", "m_h_kept", "m_zeroed", "m_blanked", "m_cleared")
        turn_in, stats_made, mv_ready, std_ready, rstd_ready, normed, turn_out = (
            sems(st, f"m_{n}_A", f"m_{n}_B")
            for n in ("turn_in", "stats_made", "mv_ready", "std_ready", "rstd_ready", "normed", "turn_out"))
        l1_ready, shift_ready = sems(st, "m_l1_ready", "m_shift_ready")
        block = st.enter_context(nc.Block())
        first, second = (xb, xn), (hb, xm)

        @block.sync
        def _(sp):
            sp.wait_ge(blanked, 1)
            rows = t["slots"][0:SLOTS, :].rearrange("(n p r) d -> n p (r d)", p=P, r=8)
            n_rows = SLOTS // (P * 8)
            for k in range(n_rows):
                sp.dma_start(rows[k], blank[:, k % 5, :, :].rearrange("p r d -> p (r d)")).then_inc(cleared, 16)
            sums = t["sums"].rearrange("(n p r) d -> n p r d", p=P, r=8)
            n_sums = (NT + EMPTY) // (P * 8)
            for k in range(n_sums):
                sp.dma_start(sums[k], blank[:, 0, :, 0:D]).then_inc(cleared, 16)
            sp.wait_ge(cleared, 16 * (n_rows + n_sums))

        @block.gpsimd
        def _(pool):
            nc.gpsimd.memset(blank[:], 0.0).then_inc(zeroed, 1)
            pool.wait_ge(zeroed, 1)
            nc.gpsimd.tensor_copy(blank[:, :, :, D], E.const("empty").rearrange("p (n r) -> p n r", r=8)).then_inc(blanked, 1)
            x1 = E.bufX[:].rearrange("p (s b) -> p b s", s=S)
            for s in turns(pool, NCH, 3):
                if c := s.back(0):
                    wait(pool, turn_in[0], c.times(1, -1))
                    nc.gpsimd.tensor_copy(xb[c.par][:].rearrange("p (b s) -> p b s", s=S),
                                          x1[:, bass.ds(c.v * NB, NB), :]).then_inc(xb_ready, 1)
                if c := s.back(3):
                    pool.wait_ge(scaled, c.times(1, 1))
                    wait(pool, turn_in[1], c.times(1, -1))
                    wait(pool, h_kept, c.times(1, -1))
                    nc.gpsimd.tensor_tensor(hb[c.par][:].rearrange("p (b s) -> p b s", s=S),
                                            hm[c.par][:].rearrange("p (b s) -> p b s", s=S),
                                            E.mod[:, 3, :].unsqueeze(1).to_broadcast([P, NB, S]), ALU.add).then_inc(h_ready, 1)

        @block.tensor
        def _(pe):
            def turn(c, src, dst):
                for j in range(4):
                    i = nc.tensor.transpose(dst[c.par][:, j * P:(j + 1) * P], src[c.par][:, j * P:(j + 1) * P], E.ident)
                return i

            for s in turns(pe, NCH, 5):
                if c := s.back(1):
                    pe.wait_ge(xb_ready, c.times(1, 1))
                    wait(pe, normed[0], c.times(1, -1))
                    turn(c, xb, pp[0]).then_inc(turn_in[0], 1)
                if c := s.back(4):
                    pe.wait_ge(h_ready, c.times(1, 1))
                    wait(pe, normed[1], c.times(1, -1))
                    turn(c, hb, pp[2]).then_inc(turn_in[1], 1)
                if c := s.back(2):
                    pe.wait_ge(normed[0], c.times(1, 1))
                    wait(pe, scaled, c.times(1, -1))
                    turn(c, xn, pp[1]).then_inc(turn_out[0], 1)
                if c := s.back(5):
                    pe.wait_ge(normed[1], c.times(1, 1))
                    wait(pe, l1_ready, c.times(1, -1))
                    turn(c, xm, pp[3]).then_inc(turn_out[1], 1)

        @block.vector
        def _(dve):
            def statistics(k, c):
                dve.wait_ge(turn_in[k], c.times(1, 1))
                for j in range(4):
                    i = nc.vector.bn_stats(stats[k][c.par][:, j, :], pp[2 * k][c.par][:, j * P:(j + 1) * P])
                i.then_inc(stats_made[k], 1)
                dve.wait_ge(stats_made[k], c.times(1, 1))
                nc.vector.tensor_copy(spare[:], E.eps)
                for j in range(4):
                    i = nc.vector.bn_aggr(mv[k][c.par][:, j, :], stats[k][c.par][:, j, :])
                i.then_inc(mv_ready[k], 1)

            for s in turns(dve, NCH, 5):
                if c := s.back(2):
                    dve.wait_ge(std_ready[0], c.times(1, 1))
                    wait(dve, turn_out[0], c.times(1, -1))
                    nc.vector.reciprocal(rstd[0][c.par][:], std[0][c.par][:]).then_inc(rstd_ready[0], 1)
                    dve.wait_ge(rstd_ready[0], c.times(1, 1))
                    for j in range(4):
                        i = nc.vector.tensor_scalar(xn[c.par][:, j * P:(j + 1) * P], pp[0][c.par][:, j * P:(j + 1) * P],
                                                    mv[0][c.par][:, j, 0:1], rstd[0][c.par][:, j:j + 1],
                                                    ALU.subtract, ALU.mult)
                    i.then_inc(normed[0], 1)
                if c := s.back(1):
                    statistics(0, c)
                if c := s.back(5):
                    dve.wait_ge(std_ready[1], c.times(1, 1))
                    wait(dve, normed[1], c.times(1, -1))
                    nc.vector.reciprocal(rstd[1][c.par][:], std[1][c.par][:]).then_inc(rstd_ready[1], 1)
                    dve.wait_ge(rstd_ready[1], c.times(1, 1))
                    nc.vector.scalar_tensor_tensor(shift[c.par][:], mv[1][c.par][:, :, 0], -1.0, rstd[1][c.par][:],
                                                   ALU.mult, ALU.mult).then_inc(shift_ready, 1)
                if c := s.back(3):
                    dve.wait_ge(turn_out[0], c.times(1, 1))
                    wait(dve, h_ready, c.times(1, -1))
                    nc.vector.tensor_tensor(hm[c.par][:].rearrange("p (b s) -> p b s", s=S),
                                            pp[1][c.par][:].rearrange("p (b s) -> p b s", s=S),
                                            E.mod[:, 4, :].unsqueeze(1).to_broadcast([P, NB, S]), ALU.mult).then_inc(scaled, 1)
                if c := s.back(4):
                    statistics(1, c)

        @block.scalar
        def _(act):
            for s in turns(act, NCH, 6):
                if c := s.back(1):
                    act.wait_ge(mv_ready[0], c.times(1, 1))
                    nc.scalar.activation(std[0][c.par][:], mv[0][c.par][:, :, 1], ACT.Sqrt, bias=E.eps).then_inc(std_ready[0], 1)
                if c := s.back(5):
                    act.wait_ge(shift_ready, c.times(1, 1))
                    wait(act, turn_out[1], c.times(1, -1))
                    for j in range(4):
                        i = nc.scalar.activation(xm[c.par][:, j * P:(j + 1) * P], pp[2][c.par][:, j * P:(j + 1) * P],
                                                 ACT.Identity, bias=shift[c.par][:, j:j + 1], scale=rstd[1][c.par][:, j:j + 1])
                    i.then_inc(normed[1], 1)
                if c := s.back(4):
                    act.wait_ge(h_ready, c.times(1, 1))
                    nc.scalar.activation(E.bufA[:, bass.ds(c.v * CH, CH)], hb[c.par][:], ACT.Identity).then_inc(h_kept, 1)
                    act.wait_ge(mv_ready[1], c.times(1, 1))
                    nc.scalar.activation(std[1][c.par][:], mv[1][c.par][:, :, 1], ACT.Sqrt, bias=E.eps).then_inc(std_ready[1], 1)
                if c := s.back(6):
                    act.wait_ge(turn_out[1], c.times(1, 1))
                    nc.scalar.activation(E.bufH[:, bass.ds(c.v * CH, CH)], pp[3][c.par][:], ACT.Identity,
                                         bias=E.col("ln1b"), scale=E.col("ln1w")).then_inc(l1_ready, 1)


def attention(nc, t, sb, ps, sems, E):
    NB = 16
    HB = NB // 2
    BT = NB * S
    W = 4 * HB * 2 * S
    NBLK = NT // BT
    with ExitStack() as st:
        def two(name, shape):
            return [sb(st, f"{name}{i}", shape) for i in range(2)]

        lb = two("lb", [P, BT])
        q = two("q", [P, HB, 2, S])
        kd = two("kd", [P, HB, 4, S])
        vd = two("vd", [P, NB, 2, 4 * HD])
        sc = two("sc", [P, W])
        mx, sm, rs = (two(n, [P, W // S]) for n in ("mx", "sm", "rs"))
        pr = two("pr", [P, W])
        pT = two("pT", [P, 4, W // 4])
        ot = two("ot", [P, HB, 2, S])
        psL = ps(st, "psL", [P, 4, 512])
        psQ = ps(st, "psQ", [P, 512])
        psKV = ps(st, "psKV", [P, 512])
        psO = ps(st, "psO", [P, 512])
        psP = ps(st, "psP", [P, 2, 256])
        psK = psKV[:, 0:256].rearrange("p (b s) -> p b s", s=S)
        psV = psKV[:, 256:512].rearrange("p (b f) -> p b f", f=KV)
        (masked, zeroed, lb_ready, qkv_made, q_ready, k_ready, v_ready, scored, turned, max_ready, shifted, exped,
         sum_ready, rcp_ready, probs_ready, pT_ready, av_made, ot_ready, projected, added) = sems(
            st, "masked", "a_zeroed", "lb_ready", "qkv_made", "q_ready", "k_ready", "v_ready", "scored", "a_turned",
            "max_ready", "shifted", "exped", "sum_ready", "rcp_ready", "probs_ready", "pT_ready", "av_made", "ot_ready",
            "projected", "added")
        block = st.enter_context(nc.Block())

        def rows(x):
            return x[:].rearrange("p (c t) -> p c t", t=S)

        @block.tensor
        def _(pe):
            for s in turns(pe, NBLK, 4):
                if c := s.back(1):
                    pe.wait_ge(q_ready, c.times(1, 1))
                    pe.wait_ge(k_ready, c.times(1, 1))
                    wait(pe, turned, c.times(1, 0))
                    for b in range(HB):
                        for r in range(4):
                            at = slice(32 * r, 32 * r + 32)
                            i = nc.tensor.matmul(psL[:, r, b * 64:(b + 1) * 64],
                                                 kd[c.par][at, b].rearrange("p j s -> p (j s)"), q[c.par][at, b, :, :],
                                                 start=True, stop=True, tile_position=(32 * r, 0))
                    i.then_inc(scored, 1)
                if s.back(0) or s.back(1):
                    if c := s.back(0):
                        pe.wait_ge(lb_ready, c.times(1, 1))
                        wait(pe, q_ready, c.times(1, 0))
                        wait(pe, k_ready, c.times(1, 0))
                        wait(pe, v_ready, c.times(1, -1))
                        for bh in range(2):
                            at, x = slice(64 * bh, 64 * bh + 64), lb[c.par][:, bh * 256:(bh + 1) * 256]
                            for g in range(2):
                                nc.tensor.matmul(psQ[at, g * 256:(g + 1) * 256], E.wq[:, g, :], x, start=True, stop=True,
                                                 tile_position=(0, 64 * bh))
                            i = nc.tensor.matmul(psK[at], E.wk[:], x, start=True, stop=True,
                                                 tile_position=(0, 64 * bh))
                    if c := s.back(1):
                        wait(pe, v_ready, c.times(1, 0))
                        for b4 in range(NB // 4):
                            i = nc.tensor.matmul(psV[:, b4, :], lb[c.par][:, b4 * P:(b4 + 1) * P], E.wv[:],
                                                 start=True, stop=True)
                    i.then_inc(qkv_made, 1)
                if c := s.back(4):
                    pe.wait_ge(ot_ready, c.times(1, 1))
                    wait(pe, added, c.times(1, 0))
                    for bh in range(2):
                        for g in range(2):
                            i = nc.tensor.matmul(psP[:, bh, :], E.wp[:, bh, g, :], ot[c.par][:, :, g, :],
                                                 start=(g == 0), stop=(g == 1))
                    i.then_inc(projected, 1)
                if c := s.back(3):
                    pe.wait_ge(pT_ready, c.times(1, 1))
                    pe.wait_ge(v_ready, c.times(1, 1))
                    wait(pe, ot_ready, c.times(1, 0))
                    for b in range(HB):
                        for r in range(4):
                            bh, jg = divmod(r, 2)
                            i = nc.tensor.matmul(psO[32 * r:32 * r + 32, b * 64:(b + 1) * 64],
                                                 vd[c.par][:, bh * HB + b, jg, :], pT[c.par][:, r, b * 64:(b + 1) * 64],
                                                 start=True, stop=True, tile_position=(0, 32 * r))
                    i.then_inc(av_made, 1)

        @block.gpsimd
        def _(pool):
            for k in range(2):
                nc.gpsimd.memset(vd[k][:], 0.0).then_inc(zeroed, 1)
            for s in turns(pool, NBLK, 2):
                if c := s.back(0):
                    wait(pool, qkv_made, c.times(1, 0))
                    nc.gpsimd.tensor_copy(lb[c.par][:], E.bufH[:, bass.ds(c.v * BT, BT)]).then_inc(lb_ready, 1)
                if c := s.back(2):
                    pool.wait_ge(rcp_ready, c.times(1, 1))
                    wait(pool, pT_ready, c.times(1, -1))
                    nc.gpsimd.tensor_tensor(rows(pr[c.par]), rows(sc[c.par]),
                                            rs[c.par][:].unsqueeze(2).to_broadcast([P, W // S, S]),
                                            ALU.mult).then_inc(probs_ready, 1)

        @block.scalar
        def _(act):
            act.wait_ge(zeroed, 2)
            for s in turns(act, NBLK, 3):
                if c := s.back(0):
                    act.wait_ge(qkv_made, c.times(1, 1))
                    wait(act, scored, c.times(1, -1))
                    nc.scalar.activation(q[c.par][:].rearrange("p b g s -> p g b s"),
                                         psQ[:].rearrange("p (g b s) -> p g b s", g=2, s=S), ACT.Identity).then_inc(q_ready, 1)
                    for j in range(4):
                        i = nc.scalar.activation(kd[c.par][:, :, j, :], psK, ACT.Copy, scale=E.const("head4")[:, j:j + 1])
                    i.then_inc(k_ready, 1)
                if c := s.back(1):
                    act.wait_ge(shifted, c.times(1, 1))
                    nc.scalar.activation(sc[c.par][:], sc[c.par][:], ACT.Exp, scale=float(HD) ** -0.5).then_inc(exped, 1)
                if c := s.back(3):
                    act.wait_ge(av_made, c.times(1, 1))
                    wait(act, projected, c.times(1, -1))
                    nc.scalar.activation(ot[c.par][:], psO[:].rearrange("p (b g s) -> p b g s", g=2, s=S),
                                         ACT.Identity).then_inc(ot_ready, 1)
                if c := s.back(1):
                    act.wait_ge(qkv_made, c.times(1, 2))
                    wait(act, av_made, c.times(1, -1))
                    for j in range(4):
                        for b in range(4):
                            i = nc.scalar.activation(
                                vd[c.par][32 * j:32 * j + 32, b::4, :, j * HD:(j + 1) * HD],
                                psV[32 * b:32 * b + 32].rearrange("p b (g x) -> p b g x", g=2)[:, :, :, j * HD:(j + 1) * HD],
                                ACT.Identity)
                    i.then_inc(v_ready, 1)

        @block.vector
        def _(dve):
            for s in turns(dve, NBLK, 4):
                if c := s.back(2):
                    dve.wait_ge(exped, c.times(1, 1))
                    nc.vector.tensor_reduce(sm[c.par][:], rows(sc[c.par]), AX_X, ALU.add).then_inc(sum_ready, 1)
                    dve.wait_ge(sum_ready, c.times(1, 1))
                    nc.vector.reciprocal(rs[c.par][:], sm[c.par][:]).then_inc(rcp_ready, 1)
                if c := s.back(3):
                    dve.wait_ge(probs_ready, c.times(1, 1))
                    wait(dve, av_made, c.times(1, -1))
                    nc.vector.transpose(pT[c.par][:].rearrange("p q c -> p (q c)"), pr[c.par][:]).then_inc(pT_ready, 1)
                if c := s.back(1):
                    dve.wait_ge(scored, c.times(1, 1))
                    wait(dve, probs_ready, c.times(1, -1))
                    nc.vector.transpose(sc[c.par][:], psL[:].rearrange("p q c -> p (q c)")).then_inc(turned, 1)
                    dve.wait_ge(turned, c.times(1, 1))
                    nc.vector.tensor_tensor(rows(sc[c.par]), rows(sc[c.par]),
                                            E.const("causal").unsqueeze(1).to_broadcast([P, W // S, S]),
                                            ALU.add).then_inc(masked, 1)
                    dve.wait_ge(masked, c.times(1, 1))
                    nc.vector.tensor_reduce(mx[c.par][:], rows(sc[c.par]), AX_X, ALU.max).then_inc(max_ready, 1)
                    dve.wait_ge(max_ready, c.times(1, 1))
                    nc.vector.tensor_tensor(rows(sc[c.par]), rows(sc[c.par]),
                                            mx[c.par][:].unsqueeze(2).to_broadcast([P, W // S, S]),
                                            ALU.subtract).then_inc(shifted, 1)
                if c := s.back(4):
                    dve.wait_ge(projected, c.times(1, 1))
                    ha = E.bufA[:, bass.ds(c.v * BT, BT)].rearrange("p (h x) -> p h x", h=2)
                    nc.vector.tensor_tensor(ha, psP[:], ha, ALU.add).then_inc(added, 1)



def norm_route(nc, t, sb, ps, sems, E):
    with ExitStack() as st:
        def two(name, shape, dt=F32):
            return [sb(st, f"{name}{i}", shape, dt) for i in range(2)]

        hb, xn, xs = (two(n, [P, CH]) for n in ("ohb", "oxn", "oxs"))
        stats, mv, std, rstd = two("ostats", [P, 4, 6]), two("omv", [P, 4, 2]), two("ostd", [P, 4]), two("orstd", [P, 4])
        rows = two("orows", [P, QT, ROW])
        idx = two("oidx", [P, 2, QT], U32)
        N8 = [P, QT, NE]
        logit = sb(st, "ologit", N8)
        prob, pick1, pick2, key, rest, both, past, rank, keep = (
            sb(st, f"r_{n}", N8) for n in ("prob", "pick1", "pick2", "key", "rest", "both", "past", "rank", "keep"))
        carried = sb(st, "r_carried", [P, NE])
        m1, m2, km, ssum, at, kept, spare1 = (
            sb(st, f"r_{n}", [P, QT]) for n in ("m1", "m2", "km", "ssum", "at", "kept", "spare"))
        p0, p1, p2 = ([ps(st, f"o{n}{i}", [P, CH]) for i in range(2)] for n in ("p0", "p1", "p2"))
        pl = ps(st, "opl", [P, 4, NE])
        pr = ps(st, "opr", N8)
        (hb_ready, turned0, stats_made, mv_ready, std_ready, rstd_ready, normed, turned1, xs_ready, turned2,
         logit_ready, kept_rows, step, shifted, exped, picked, counted, routed) = sems(
            st, "o_hb_ready", "o_turned0", "o_stats_made", "o_mv_ready", "o_std_ready", "o_rstd_ready", "o_normed",
            "o_turned1", "o_xs_ready", "o_turned2", "o_logit_ready", "o_kept_rows", "r_step", "r_shifted", "r_exped",
            "r_picked", "r_counted", "r_routed")
        scattered = sems(st, "r_scattered0", "r_scattered1")
        block = st.enter_context(nc.Block())

        def part_after(s):
            c = s.back(4)
            return c.v // QC if c and c.v % QC == QC - 1 else None

        @block.tensor
        def _(pe):
            for s in steps(NCH, 4):
                if c := s.back(1):
                    pe.wait_ge(hb_ready, c.v + 1)
                    wait(pe, normed, c.v - 1)
                    for j in range(4):
                        i = nc.tensor.transpose(p0[c.par][:, j * P:(j + 1) * P], hb[c.par][:, j * P:(j + 1) * P], E.ident)
                    i.then_inc(turned0, 1)
                if c := s.back(4):
                    pe.wait_ge(xs_ready, c.v + 1)
                    wait(pe, kept_rows, c.v - 1)
                    wait(pe, logit_ready, c.v)
                    for j in range(4):
                        xj = xs[c.par][:, j * P:(j + 1) * P]
                        nc.tensor.matmul(pl[:, j, :], xj, E.router[:], start=True, stop=True)
                        i = nc.tensor.transpose(p2[c.par][:, j * P:(j + 1) * P], xj, E.ident)
                    i.then_inc(turned2, 1)
                if c := s.back(2):
                    pe.wait_ge(normed, c.v + 1)
                    wait(pe, xs_ready, c.v - 1)
                    for j in range(4):
                        i = nc.tensor.transpose(p1[c.par][:, j * P:(j + 1) * P], xn[c.par][:, j * P:(j + 1) * P], E.ident)
                    i.then_inc(turned1, 1)
                if (q := part_after(s)) is not None:
                    pe.wait_ge(picked, q + 1)
                    o = pr[:].rearrange("p t e -> p (t e)")
                    nc.tensor.matmul(o, E.const("before"), both[:].rearrange("p t e -> p (t e)"), start=True, stop=False)
                    nc.tensor.matmul(o, E.ones, past[:].rearrange("p t e -> p (t e)"), start=False,
                                     stop=True).then_inc(counted, 1)

        @block.scalar
        def _(act):
            ha = E.bufA[:].rearrange("p (b s) -> p s b", s=S)
            for s in steps(NCH, 4):
                if c := s.back(1):
                    act.wait_ge(mv_ready, c.v + 1)
                    nc.scalar.activation(std[c.par][:], mv[c.par][:, :, 1], ACT.Sqrt, bias=E.eps).then_inc(std_ready, 1)
                if c := s.back(0):
                    wait(act, turned0, c.v - 1)
                    nc.scalar.activation(hb[c.par][:].rearrange("p (s b) -> p s b", b=B),
                                         ha[:, 2 * c.v:2 * c.v + 2, :], ACT.Identity).then_inc(hb_ready, 1)
                if c := s.back(3):
                    act.wait_ge(turned1, c.v + 1)
                    wait(act, turned2, c.v - 1)
                    nc.scalar.activation(xs[c.par][:], p1[c.par][:], ACT.Identity, bias=E.col("ln2b"),
                                         scale=E.col("ln2w")).then_inc(xs_ready, 1)
                if c := s.back(4):
                    act.wait_ge(turned2, c.v + 1)
                    q, k = divmod(c.v, QC)
                    wait(act, scattered[q % 2], 16 * 2 * QT * (q // 2))
                    nc.scalar.activation(rows[q % 2][:, 4 * k:4 * k + 4, 0:D],
                                         p2[c.par][:].rearrange("p (j d) -> p j d", j=4), ACT.Identity).then_inc(kept_rows, 1)
                if (q := part_after(s)) is not None:
                    act.wait_ge(shifted, q + 1)
                    nc.scalar.activation(prob[:], prob[:], ACT.Exp).then_inc(exped, 1)

        @block.vector
        def _(dve):
            n = 0

            def link(ins):
                nonlocal n
                n += 1
                ins.then_inc(step, 1)
                dve.wait_ge(step, n)

            def tt(out, a, b, op):
                link(nc.vector.tensor_tensor(out, a, b, op))

            def total(out, x):
                link(nc.vector.tensor_reduce(out, x, AX_X, ALU.add))

            def wide(x):
                return x[:].unsqueeze(2).to_broadcast(N8)

            def row(name):
                return E.const(name).unsqueeze(1).to_broadcast(N8)

            def pick(src, best, out):
                link(nc.vector.tensor_reduce(best[:], src[:], AX_X, ALU.max))
                tt(key[:], src[:], wide(best), ALU.is_equal)
                tt(key[:], key[:], row("rev"), ALU.mult)
                link(nc.vector.tensor_reduce(km[:], key[:], AX_X, ALU.max))
                tt(out[:], key[:], wide(km), ALU.is_equal)

            def route(q):
                token = E.const("token")[:, q * QT:(q + 1) * QT]
                r = rows[q % 2]
                link(nc.vector.tensor_reduce(m1[:], logit[:], AX_X, ALU.max))
                nc.vector.tensor_tensor(prob[:], logit[:], wide(m1), ALU.subtract).then_inc(shifted, 1)
                dve.wait_ge(exped, q + 1)
                total(ssum[:], prob[:])
                link(nc.vector.reciprocal(ssum[:], ssum[:]))
                tt(prob[:], prob[:], wide(ssum), ALU.mult)
                pick(prob, m1, pick1)
                wait(dve, scattered[q % 2], 16 * 2 * QT * (q // 2))
                nc.vector.tensor_scalar(r[:, :, D + 3], km[:], -1.0, float(NE), ALU.mult, ALU.add)
                nc.vector.tensor_copy(r[:, :, D], token)
                link(nc.vector.scalar_tensor_tensor(rest[:], pick1[:], -2.0, prob[:], ALU.mult, ALU.add))
                pick(rest, m2, pick2)
                tt(both[:], pick1[:], pick2[:], ALU.add)
                for j in range(QT):
                    if j == 0:
                        link(nc.vector.tensor_copy(past[:, 0, :], carried[:]))
                    else:
                        tt(past[:, j, :], past[:, j - 1, :], both[:, j - 1, :], ALU.add)
                nc.vector.tensor_tensor(carried[:], past[:, QT - 1, :], both[:, QT - 1, :], ALU.add).then_inc(picked, 1)
                tt(ssum[:], m1[:], m2[:], ALU.add)
                link(nc.vector.reciprocal(ssum[:], ssum[:]))
                nc.vector.tensor_tensor(r[:, :, D + 1], m1[:], ssum[:], ALU.mult)
                nc.vector.tensor_tensor(r[:, :, D + 2], m2[:], ssum[:], ALU.mult)
                dve.wait_ge(counted, q + 1)
                nc.vector.tensor_scalar(keep[:], pr[:], float(CAP), None, ALU.is_lt)
                tt(rank[:], pr[:], row("slot0"), ALU.add)
                for k, pick_k in enumerate((pick1, pick2)):
                    link(nc.vector.tensor_scalar(spare1[:], token, float(SLOTS + k * NT), None, ALU.add))
                    tt(key[:], pick_k[:], rank[:], ALU.mult)
                    total(at[:], key[:])
                    tt(key[:], pick_k[:], keep[:], ALU.mult)
                    total(kept[:], key[:])
                    tt(at[:], at[:], spare1[:], ALU.subtract)
                    tt(at[:], at[:], kept[:], ALU.mult)
                    tt(at[:], at[:], spare1[:], ALU.add)
                    i = nc.vector.tensor_copy(idx[q % 2][:, k, :], at[:])
                    i.then_inc(routed, 1)

            link(nc.vector.memset(carried[:], 0.0))
            for s in steps(NCH, 4):
                if c := s.back(2):
                    dve.wait_ge(std_ready, c.v + 1)
                    wait(dve, turned1, c.v - 1)
                    nc.vector.reciprocal(rstd[c.par][:], std[c.par][:]).then_inc(rstd_ready, 1)
                    dve.wait_ge(rstd_ready, c.v + 1)
                    for j in range(4):
                        i = nc.vector.tensor_scalar(xn[c.par][:, j * P:(j + 1) * P], p0[c.par][:, j * P:(j + 1) * P],
                                                    mv[c.par][:, j, 0:1], rstd[c.par][:, j:j + 1],
                                                    ALU.subtract, ALU.mult)
                    i.then_inc(normed, 1)
                if c := s.back(1):
                    dve.wait_ge(turned0, c.v + 1)
                    for j in range(4):
                        i = nc.vector.bn_stats(stats[c.par][:, j, :], p0[c.par][:, j * P:(j + 1) * P])
                    i.then_inc(stats_made, 1)
                    dve.wait_ge(stats_made, c.v + 1)
                    for j in range(4):
                        i = nc.vector.bn_aggr(mv[c.par][:, j, :], stats[c.par][:, j, :])
                    i.then_inc(mv_ready, 1)
                if c := s.back(4):
                    k = c.v % QC
                    dve.wait_ge(turned2, c.v + 1)
                    nc.vector.tensor_copy(logit[:, 4 * k:4 * k + 4, :], pl[:]).then_inc(logit_ready, 1)
                if (q := part_after(s)) is not None:
                    dve.wait_ge(logit_ready, (q + 1) * QC)
                    route(q)

        @block.gpsimd
        def _(pool):
            for q in range(Q):
                pool.wait_ge(kept_rows, (q + 1) * QC)
                for k in range(2):
                    pool.wait_ge(routed, 2 * q + k + 1)
                    for j in range(QT):
                        pool.indirect_dma_start(t["slots"], bass.IndirectOffsetOnAxis(ap=idx[q % 2][:, k, j:j + 1], axis=0),
                                                rows[q % 2][:, j, :], None).then_inc(scattered[q % 2], 16)
            for k in range(2):
                pool.wait_ge(scattered[k], 16 * 2 * QT * (Q // 2))


class Chunk(Turn):

    def __init__(self, v, phase, n, static, per, pass_no):
        super().__init__(v, phase % 2, n, static)
        self.phase, self.per, self.pass_no = phase, per, pass_no

    def back(self, k):
        if self.static:
            c = self.v - k
            period = 2 * self.per
            return Chunk(c, c % period, self.n, True, self.per, c // period) if 0 <= c < self.n else None
        phase = (self.phase - k) % (2 * self.per)
        passes = self.pass_no - 1 if self.phase < k else self.pass_no
        return Chunk(self.v - k if k else self.v, phase, self.n, False, self.per, passes)

    def half(self):
        return self.phase // self.per

    def expert(self):
        return self.pass_no * 2 + self.half()

    def seat(self):
        return self.phase % self.per

    def uses(self, plus=0):
        return self.pass_no * 2 + (self.half() + 1 + plus)

    def before(self, par):
        return self.pass_no * self.per + (self.half() * (self.per + 1 - par)) // 2


def expert_steps(eng, n, lag, per):
    period = 2 * per
    for t in range(period):
        yield Chunk(t, t, n, True, per, 0)
    with eng.Fori(1, n // period) as i:
        for k in range(period):
            yield Chunk(i * period + k, k, n, False, per, i)
    for t in range(n, n + lag):
        yield Chunk(t, t % period, n, True, per, t // period)


def experts(nc, t, sb, ps, sems, E):
    PER = CAP // CH
    N = NE * PER
    with ExitStack() as st:
        def many(n, name, shape, dt=F32):
            return [sb(st, f"{name}{i}", shape, dt) for i in range(n)]

        w1, w2 = many(2, "w1_", [P, FFN]), many(2, "w2_", [P, 4, D])
        xr = many(PER, "exr", [P, 4, ROW])
        token = many(PER, "etoken", [P, 4], U32)
        first, part, weight = (many(PER, f"e{n}", [P, 4]) for n in ("first", "part", "weight"))
        xT, yo = many(2, "exT", [P, CH]), many(2, "eyo", [P, 4, D])
        hid = many(2, "ehid", [P, 4, CH])
        scrap = sb(st, "escrap", [P, 1])
        pX = [ps(st, f"e_pX{i}", [P, CH]) for i in range(2)]
        pH = ps(st, "e_pH", [P, 4, CH])
        pY = [ps(st, f"e_pY{i}", [P, 4, D]) for i in range(2)]
        w_in = sems(st, "e_w_in0", "e_w_in1")
        x_in = sems(st, *[f"e_x_in{i}" for i in range(PER)])
        added = sems(st, "e_added0", "e_added1")
        (turned, xT_ready, hidden, active, made, y_ready, is_first, parts_made, weight_ready,
         scrapped) = sems(
            st, "e_turned", "e_xT_ready", "e_hidden", "e_active", "e_made", "e_y_ready", "e_is_first", "e_parts_made",
            "e_weight_ready", "e_scrapped")
        src = t["slots"][0:SLOTS, :].rearrange("(c j p) d -> p c j d", p=P, j=4)
        block = st.enter_context(nc.Block())

        @block.sync
        def _(sp):
            for s in expert_steps(sp, N, 0, PER):
                if c := s.back(0):
                    if c.seat() == 0:
                        if not (c.static and c.v < 2 * PER):
                            sp.wait_ge(made, c.times(1, -PER))
                        sp.dma_start(w1[c.half()][:], t["w1"][:, bass.ds(c.expert(), 1), :]).then_inc(w_in[c.half()], 16)
                        sp.dma_start(w2[c.half()][:], t["w2"][:, bass.ds(c.expert(), 1), :, :]).then_inc(w_in[c.half()], 16)
                    wait(sp, turned, c.times(1, 1 - PER))
                    wait(sp, weight_ready, c.times(1, 1 - PER))
                    sp.dma_start(xr[c.seat()][:], src[:, bass.ds(c.v, 1), :, :]).then_inc(x_in[c.seat()], 16)

        @block.tensor
        def _(pe):
            for s in expert_steps(pe, N, 2, PER):
                if c := s.back(0):
                    pe.wait_ge(x_in[c.seat()], c.uses() * 16)
                    wait(pe, xT_ready, c.times(1, -1))
                    for j in range(4):
                        i = nc.tensor.transpose(pX[c.par][:, j * P:(j + 1) * P], xr[c.seat()][:, j, 0:D], E.ident)
                    i.then_inc(turned, 1)
                if c := s.back(1):
                    if c.seat() == 0:
                        pe.wait_ge(w_in[c.half()], c.pass_no * 32 + 32)
                    pe.wait_ge(xT_ready, c.times(1, 1))
                    for f in range(4):
                        wait(pe, active, c.times(4, f - 3))
                        nc.tensor.matmul(pH[:, f, :], w1[c.half()][:, f * P:(f + 1) * P], xT[c.par][:],
                                         start=True, stop=True).then_inc(hidden, 1)
                if c := s.back(2):
                    wait(pe, y_ready, c.times(1, -1))
                    pe.wait_ge(active, c.times(4, 4))
                    for j in range(4):
                        for f in range(4):
                            i = nc.tensor.matmul(pY[c.par][:, j, :], hid[c.par][:, f, j * P:(j + 1) * P],
                                                 w2[c.half()][:, f, :], start=(f == 0), stop=(f == 3))
                    i.then_inc(made, 1)

        @block.scalar
        def _(act):
            for s in expert_steps(act, N, 1, PER):
                if c := s.back(1):
                    wait(act, made, c.times(1, -1))
                    for f in range(4):
                        act.wait_ge(hidden, c.times(4, f + 1))
                        nc.scalar.activation(hid[c.par][:, f, :], pH[:, f, :], ACT.Gelu).then_inc(active, 1)

        @block.vector
        def _(dve):
            for s in expert_steps(dve, N, 2, PER):
                if c := s.back(0):
                    dve.wait_ge(turned, c.times(1, 1))
                    wait(dve, hidden, c.times(4, -4))
                    nc.vector.tensor_copy(xT[c.par][:], pX[c.par][:]).then_inc(xT_ready, 1)
                if c := s.back(2):
                    dve.wait_ge(made, c.times(1, 1))
                    dve.wait_ge(weight_ready, c.times(1, 1))
                    if not (c.static and c.v < 2):
                        dve.wait_ge(added[c.par], (c.v - c.par) * 32 if c.par else c.v * 32)
                    for j in range(4):
                        i = nc.vector.tensor_scalar(yo[c.par][:, j, :], pY[c.par][:, j, :],
                                                    weight[c.seat()][:, j:j + 1], None, ALU.mult)
                    i.then_inc(y_ready, 1)
                if c := s.back(0):
                    k = c.seat()
                    e1, wa, wb = xr[k][:, :, D + 3], xr[k][:, :, D + 1], xr[k][:, :, D + 2]
                    nc.vector.tensor_scalar(first[k][:], e1, E.const("expert")[:, bass.ds(c.expert(), 1)], None,
                                            ALU.is_equal).then_inc(is_first, 1)
                    nc.vector.tensor_copy(token[k][:], xr[k][:, :, D])
                    dve.wait_ge(is_first, c.times(1, 1))
                    nc.vector.tensor_tensor(part[k][:], first[k][:], wb, ALU.mult)
                    nc.vector.tensor_tensor(weight[k][:], first[k][:], wa, ALU.mult).then_inc(parts_made, 1)
                    dve.wait_ge(parts_made, c.times(2, 1))
                    nc.vector.tensor_tensor(part[k][:], wb, part[k][:], ALU.subtract).then_inc(parts_made, 1)
                    dve.wait_ge(parts_made, c.times(2, 2))
                    nc.vector.tensor_tensor(weight[k][:], weight[k][:], part[k][:], ALU.add).then_inc(weight_ready, 1)

        @block.gpsimd
        def _(pool):
            for s in expert_steps(pool, N, 2, PER):
                if c := s.back(2):
                    pool.wait_ge(y_ready, c.times(1, 1))
                    if c.seat() == 0:
                        for k in range(2):
                            wait(pool, added[k], c.before(k) * 64)
                    wait(pool, scrapped, c.times(1, 0))
                    nc.gpsimd.tensor_tensor(scrap[:], E.ident[:, 0:1], E.ident[:, 0:1], ALU.mult).then_inc(scrapped, 1)
                    for j in range(4):
                        pool.indirect_dma_start(t["sums"], bass.IndirectOffsetOnAxis(ap=token[c.seat()][:, j:j + 1], axis=0),
                                                yo[c.par][:, j, :], None, compute_op=ALU.add).then_inc(added[c.par], 16)
            for k in range(2):
                pool.wait_ge(added[k], 64 * (N // 2))


def combine(nc, t, sb, ps, sems, E):
    with ExitStack() as st:
        def two(name, shape):
            return [sb(st, f"{name}{i}", shape) for i in range(2)]

        mo = two("cmo", [P, 4, D])
        fs, fg, fo = (two(n, [P, CH]) for n in ("cfs", "cfg", "cfo"))
        pm = [ps(st, f"c_pm{i}", [P, CH]) for i in range(2)]
        m_in = sems(st, "c_m_in0", "c_m_in1")
        stored = sems(st, "c_stored0", "c_stored1")
        (turned, f_ready, scaled, o_ready) = sems(st, "c_turned", "c_f_ready", "c_scaled", "c_o_ready")
        block = st.enter_context(nc.Block())
        ha = E.bufA[:].rearrange("p (b s) -> p s b", s=S)
        src = t["sums"][0:NT, :].rearrange("(n p) d -> p n d", p=P)

        @block.sync
        def _(sp):
            for s in turns(sp, NCH, 0):
                if c := s.back(0):
                    wait(sp, turned, c.times(1, -1))
                    sp.dma_start(mo[c.par][:], src[:, bass.ds(c.v * 4, 4), :]).then_inc(m_in[c.par], 16)

        @block.tensor
        def _(pe):
            for s in turns(pe, NCH, 0):
                if c := s.back(0):
                    pe.wait_ge(m_in[c.par], c.loads())
                    wait(pe, f_ready, c.times(1, -1))
                    for j in range(4):
                        i = nc.tensor.transpose(pm[c.par][:, j * P:(j + 1) * P], mo[c.par][:, j, :], E.ident)
                    i.then_inc(turned, 1)

        @block.vector
        def _(dve):
            for s in turns(dve, NCH, 0):
                if c := s.back(0):
                    dve.wait_ge(turned, c.times(1, 1))
                    wait(dve, scaled, c.times(1, -1))
                    nc.vector.tensor_tensor(fs[c.par][:].rearrange("p (s b) -> p s b", b=B),
                                            pm[c.par][:].rearrange("p (s b) -> p s b", b=B),
                                            ha[:, bass.ds(c.v * 2, 2), :], ALU.add).then_inc(f_ready, 1)

        @block.scalar
        def _(act):
            for s in turns(act, NCH, 1):
                if c := s.back(0):
                    act.wait_ge(f_ready, c.times(1, 1))
                    wait(act, o_ready, c.times(1, -1))
                    for k in range(2):
                        i = nc.scalar.activation(fg[c.par][:, k * B:(k + 1) * B], fs[c.par][:, k * B:(k + 1) * B],
                                                 ACT.Copy, scale=E.mod[:, 5, bass.ds(c.v * 2 + k, 1)])
                    i.then_inc(scaled, 1)
                if c := s.back(1):
                    act.wait_ge(o_ready, c.times(1, 1))
                    act.dma_start(t["out"][:, bass.ds(c.v * CH, CH)], fo[c.par][:]).then_inc(stored[c.par], 16)
            for k in range(2):
                act.wait_ge(stored[k], 16 * (NCH // 2))

        @block.gpsimd
        def _(pool):
            for s in turns(pool, NCH, 0):
                if c := s.back(0):
                    pool.wait_ge(scaled, c.times(1, 1))
                    if not (c.static and c.v < 2):
                        pool.wait_ge(stored[c.par], c.loads() - 16)
                    nc.gpsimd.tensor_tensor(fo[c.par][:], fg[c.par][:], E.bufX[:, bass.ds(c.v * CH, CH)],
                                            ALU.add).then_inc(o_ready, 1)


def lay_out(i):
    def f(name):
        return np.asarray(i[name])

    def halves(a):
        a = a.reshape(2, P, -1)
        return a.transpose(1, 0, 2)

    x = f("L0_attn_x").reshape(NT, D)
    qkv = f("L0_ffn_qkv_weight").reshape(NKV, 4, HD, D)
    proj = f("L0_ffn_proj_weight").T.reshape(NKV, 2, HD, D).transpose(0, 2, 1, 3).reshape(KV, 2, D)
    none = np.zeros_like(proj)
    cols = np.concatenate([
        f("L0_attn_bi").reshape(4, P).T,
        halves(f("L0_attn_conv_w").reshape(DI, DCONV)).reshape(P, 8),
        f("L0_attn_conv_b").reshape(2, P).T, f("L0_attn_bdt").reshape(2, P).T,
        f("L0_attn_bo").reshape(P, 1), f("L0_attn_Dv").reshape(2, P).T,
        f("L0_ffn_ln1_weight").reshape(P, 1), f("L0_ffn_ln1_bias").reshape(P, 1),
        f("L0_ffn_ln2_weight").reshape(P, 1), f("L0_ffn_ln2_bias").reshape(P, 1)], axis=1)
    out = {
        "con": np.concatenate(list(CONST.values()), axis=1),
        "x": x.reshape(TILES, P, D).transpose(1, 0, 2),
        "xT": x.T,
        "wi": f("L0_attn_Wi").T,
        "wdt": f("L0_attn_Wdt").T,
        "wo": halves(f("L0_attn_Wo").T),
        "wq": qkv[:, 0:2].transpose(3, 1, 0, 2).reshape(D, 2, KV),
        "wk": qkv[:, 2].reshape(KV, D).T, "wv": qkv[:, 3].reshape(KV, D).T,
        "wp": np.stack([np.concatenate([proj, none]), np.concatenate([none, proj])], axis=1),
        "router": f("L0_ffn_router_weight"),
        "cols": cols,
        "alog": halves(f("L0_attn_A_log")), "bm": halves(f("L0_attn_Bm")), "cm": halves(f("L0_attn_Cm")),
        "ct": f("L0_c").T,
        "wmod": f("L0_wmod").reshape(P, 6, D),
        "w1": f("L0_ffn_moe_w1").transpose(1, 0, 2),
        "w2": f("L0_ffn_moe_w2").reshape(NE, 4, P, D).transpose(2, 0, 1, 3),
    }
    return {k: np.ascontiguousarray(v) for k, v in out.items()}


STOP = None


def kernel(**inputs):
    import concourse.bacc as _bacc
    from concourse.bass_utils import run_bass_kernel_spmd as _run

    nc = _bacc.Bacc("TRN2", target_bir_lowering=False, num_devices=1)
    arrays, t = {}, {}
    for name, a in lay_out(inputs).items():
        arrays[f"in_{name}"] = a
        t[name] = nc.dram_tensor(f"in_{name}", a.shape, F32, kind="ExternalInput").ap()
    t["out"] = nc.dram_tensor("out_0", [P, NT], F32, kind="ExternalOutput").ap()
    t["slots"] = nc.dram_tensor("slots", [SLOTS + 2 * NT, ROW], F32, kind="Internal").ap()
    t["sums"] = nc.dram_tensor("sums", [NT + EMPTY, D], F32, kind="Internal").ap()
    build(nc, t, STOP)
    r = _run(nc, [arrays], core_ids=[0])
    return np.ascontiguousarray(r.results[0]["out_0"].T.reshape(S, B, D))
```

```python
from contextlib import ExitStack

import numpy as np

import concourse.bass as bass
from concourse import mybir

F32 = mybir.dt.float32
BF16 = mybir.dt.bfloat16
U32 = mybir.dt.uint32
ALU = mybir.AluOpType
ACT = mybir.ActivationFunctionType
AX_X = mybir.AxisListType.X

P = 128
S, B, D = 32, 256, 128
NT = S * B
DI, NST, DCONV, DTR = 256, 16, 4, 32
NH, NKV, HD = 16, 8, 8
KV = NKV * HD
NE, FFN = 8, 512
CAP = -(-NT * 2 * 5 // (NE * 4))
SLOTS = NE * CAP
EPS = 1e-5
BIG = 3e38
NEG = -1e30

CH = 512
NCH = NT // CH
GR = 1024
GS = GR // B
NG = NT // GR
PADB = B + DCONV - 1
RING = 4
TILES = NT // P
ROW = D + 4
EMPTY = 5 * 8 * P
Q = 4
QC, QT = NCH // Q, TILES // Q


def constants():
    p = np.arange(P)
    causal = np.where((p % S)[:, None] <= np.arange(S)[None, :], 0.0, NEG)
    tile_token = np.arange(TILES)[None, :] * P + p[:, None]
    t = {
        "ident": np.eye(P),
        "ones": np.ones((P, P)),
        "before": (p[:, None] < p[None, :]) * 1.0,
        "causal": causal,
        "head4": ((p[:, None] // HD) % 4 == np.arange(4)[None, :]) * 1.0,
        "slot0": np.tile(np.arange(NE) * float(CAP), (P, 1)),
        "rev": np.tile(NE - np.arange(NE) * 1.0, (P, 1)),
        "eps": np.full((P, 1), EPS),
        "big": np.full((P, 1), BIG),
        "expert": np.tile(np.arange(NE) * 1.0, (P, 1)),
        "token": tile_token,
        "empty": NT + (np.arange(5)[None, :, None] * 8 * P + p[:, None, None] * 8 + np.arange(8)[None, None, :]).reshape(P, 40),
    }
    return {k: np.ascontiguousarray(v, dtype=np.float32) for k, v in t.items()}


CONST = constants()
CONST_AT = {}
_n = 0
for _k, _v in CONST.items():
    CONST_AT[_k] = (_n, _n + _v.shape[1])
    _n += _v.shape[1]
CONST_COLS = _n


def wait(eng, sem, value):
    if isinstance(value, int) and value <= 0:
        return
    eng.wait_ge(sem, value)


class Turn:

    def __init__(self, v, par, n, static):
        self.v, self.par, self.n, self.static = v, par, n, static

    def back(self, k):
        if self.static:
            c = self.v - k
            return Turn(c, c % 2, self.n, True) if 0 <= c < self.n else None
        return Turn(self.v - k if k else self.v, (self.par - k) % 2, self.n, False)

    def times(self, per, plus=0):
        return self.v * per + plus

    def count(self, plus):
        return self.v + plus if plus else self.v

    def upto(self, k):
        return min(self.v - k, self.n) if self.static else self.count(-k)

    def loads(self):
        return (self.v - self.par) * 8 + 16 if self.par else self.v * 8 + 16


def turns(eng, n, lag):
    head = lag + 2 + (lag % 2)
    for t in range(head):
        yield Turn(t, t % 2, n, True)
    if n > head:
        with eng.Fori(head // 2, n // 2) as i:
            yield Turn(i * 2, 0, n, False)
            yield Turn(i * 2 + 1, 1, n, False)
    for t in range(max(n, head), n + lag):
        yield Turn(t, t % 2, n, True)


def steps(n, lag):
    for t in range(n + lag):
        yield Turn(t, t % 2, n, True)


def build(nc, t):
    top = ExitStack()

    def sb(stack, name, shape, dt=F32):
        return stack.enter_context(nc.sbuf_tensor(name, shape, dt))

    def ps(stack, name, shape):
        return stack.enter_context(nc.psum_tensor(name, shape, F32))

    def sems(stack, *names):
        return [stack.enter_context(nc.semaphore(n)) for n in names]

    with top:
        E = Resident()
        E.con = sb(top, "con", [P, CONST_COLS])
        E.ident, E.ones, E.eps = E.const("ident"), E.const("ones"), E.const("eps")
        E.wi = sb(top, "wi", [P, 4 * P])
        E.wdt = sb(top, "wdt", [DTR, DI])
        E.wo = sb(top, "wo", [P, 2, D])
        E.wq = sb(top, "wq", [P, 2 * KV])
        E.wk = sb(top, "wk", [P, KV])
        E.wv = sb(top, "wv", [P, KV])
        E.wp = sb(top, "wp", [P, D])
        E.router = sb(top, "router", [P, NE])
        E.cols = sb(top, "cols", [P, NCOLS])
        E.mod = sb(top, "mod", [P, 6, S])
        E.skip = sb(top, "skip", [P, 2, S])
        E.A = sb(top, "A", [P, 2, NST])
        E.bufX = sb(top, "bufX", [P, NT])
        E.bufH = sb(top, "bufH", [P, NT])

        with ExitStack() as scan_stack:
            E.cb = sb(scan_stack, "cb", [P, 2, NST])
            E.diag_cb = sb(scan_stack, "diag_cb", [P, 2, NST, P])
            prep_and_norm_in(nc, t, sb, ps, sems, E)
            scan_phase(nc, t, sb, ps, sems, E)
        E.bufA = sb(top, "bufA", [P, NT])
        norm_mid(nc, t, sb, ps, sems, E)
        attention(nc, t, sb, ps, sems, E)
        norm_route(nc, t, sb, ps, sems, E)
        experts(nc, t, sb, ps, sems, E)
        combine(nc, t, sb, ps, sems, E)


COLS = {}
_c = 0
for _name, _w in (("bi", 4), ("conv_w", 8), ("conv_b", 2), ("bdt", 2), ("bo", 1), ("dv", 2),
                  ("ln1w", 1), ("ln1b", 1), ("ln2w", 1), ("ln2b", 1)):
    COLS[_name] = _c
    _c += _w
NCOLS = _c


class Resident:

    def col(self, name, k=0):
        lo = COLS[name] + k
        return self.cols[:, lo:lo + 1]

    def const(self, name):
        lo, hi = CONST_AT[name]
        return self.con[:, lo:hi]


def prep_and_norm_in(nc, t, sb, ps, sems, E):
    EARLY = 4
    with ExitStack() as st:
        alog = sb(st, "alog", [P, 2, NST])
        bm = sb(st, "bm", [P, 2, NST])
        cm = sb(st, "cm", [P, 2, NST])
        ct = sb(st, "ct", [P, S])
        sct = sb(st, "sct", [P, S])
        wmod = sb(st, "wmod", [P, 6, D])
        aexp = sb(st, "aexp", [P, 2, NST])
        sign = sb(st, "sign", [P, S])
        mag = sb(st, "mag", [P, S])
        dvm = sb(st, "dvm", [P, 1])
        pmod = ps(st, "pmod", [P, 6, S])
        pdv = ps(st, "pdv", [P, 1])
        xn = [sb(st, f"xn{i}", [P, CH]) for i in range(2)]
        sk = [sb(st, f"sk{i}", [P, CH]) for i in range(2)]
        stats = [sb(st, f"stats{i}", [P, 4, 6]) for i in range(2)]
        mv = [sb(st, f"mv{i}", [P, 4, 2]) for i in range(2)]
        std = [sb(st, f"std{i}", [P, 4]) for i in range(2)]
        rstd = [sb(st, f"rstd{i}", [P, 4]) for i in range(2)]
        spare = sb(st, "spare", [P, 1])
        pt = [ps(st, f"pt{i}", [P, CH]) for i in range(2)]
        (loaded, c_silu, a_exp, mod_made, dv_made, cb_ready, step, mod_ready, weights_in) = sems(
            st, "loaded", "c_silu", "a_exp", "mod_made", "dv_made", "cb_ready", "prep_step", "mod_ready", "weights_in")
        (stats_made, mv_ready, std_ready, rstd_ready, normed, turned, h_ready, skip_added) = sems(
            st, "stats_made", "mv_ready", "std_ready", "rstd_ready", "normed", "turned", "h_ready", "skip_added")
        x_early, x_late, xT_early, xT_late = sems(st, "x_early", "x_late", "xT_early", "xT_late")
        first = [(E.con[:], "con"), (E.cols[:], "cols"), (ct[:], "ct"), (wmod[:], "wmod"), (cm[:], "cm"),
                 (bm[:], "bm"), (alog[:], "alog")]
        later = [(E.wi[:], "wi"), (E.wdt[:], "wdt"), (E.wo[:], "wo"), (E.wq[:], "wq"), (E.wk[:], "wk"),
                 (E.wv[:], "wv"), (E.wp[:], "wp"), (E.router[:], "router")]
        block = st.enter_context(nc.Block())

        @block.sync
        def _(sp):
            xTok, cut = t["x"].rearrange("p n d -> p (n d)"), EARLY * CH
            for dst, name in first[:1]:
                sp.dma_start(dst, t[name]).then_inc(loaded, 16)
            sp.dma_start(E.bufH[:, 0:cut], xTok[:, 0:cut]).then_inc(x_early, 16)
            for dst, name in first[1:]:
                sp.dma_start(dst, t[name]).then_inc(loaded, 16)
            sp.dma_start(E.bufX[:, 0:cut], t["xT"][:, 0:cut]).then_inc(xT_early, 16)
            sp.dma_start(E.bufH[:, cut:NT], xTok[:, cut:NT]).then_inc(x_late, 16)
            sp.dma_start(E.bufX[:, cut:NT], t["xT"][:, cut:NT]).then_inc(xT_late, 16)
            for dst, name in later:
                sp.dma_start(dst, t[name]).then_inc(weights_in, 16)
            sp.wait_ge(weights_in, 16 * len(later))

        @block.tensor
        def _(pe):
            pe.wait_ge(loaded, 16 * len(first))
            for k in range(2):
                mm = nc.tensor.matmul(pdv[:], E.ones, E.col("dv", k), start=(k == 0), stop=(k == 1))
            mm.then_inc(dv_made, 1)
            pe.wait_ge(c_silu, 1)
            for k in range(6):
                mm = nc.tensor.matmul(pmod[:, k, :], wmod[:, k, :], sct[:], start=True, stop=True)
            mm.then_inc(mod_made, 1)
            for s in turns(pe, NCH, 1):
                if c := s.back(1):
                    pe.wait_ge(normed, c.times(1, 1))
                    wait(pe, h_ready, c.times(1, -1))
                    for j in range(4):
                        i = nc.tensor.transpose(pt[c.par][:, j * P:(j + 1) * P], xn[c.par][:, j * P:(j + 1) * P], E.ident)
                    i.then_inc(turned, 1)

        @block.vector
        def _(dve):
            n = 0

            def link(ins):
                nonlocal n
                n += 1
                ins.then_inc(step, 1)
                dve.wait_ge(step, n)

            dve.wait_ge(loaded, 16 * len(first))
            nc.vector.tensor_tensor(E.cb[:], cm[:], bm[:], ALU.mult).then_inc(cb_ready, 1)
            dve.wait_ge(dv_made, 1)
            link(nc.vector.tensor_scalar(dvm[:], pdv[:], 1.0 / DI, None, ALU.mult))
            dve.wait_ge(a_exp, 1)
            nc.vector.tensor_scalar(E.A[:], aexp[:], -1.0, -1e-30, ALU.mult, ALU.min)
            dve.wait_ge(mod_made, 1)
            link(nc.vector.tensor_copy(E.mod[:], pmod[:]))
            for k in (1, 4):
                nc.vector.tensor_scalar(E.mod[:, k, :], E.mod[:, k, :], 1.0, None, ALU.add)
            for k in (2, 5):
                link(nc.vector.tensor_scalar(mag[:], E.mod[:, k, :], -1.0, 0.25, ALU.mult, ALU.max))
                link(nc.vector.tensor_tensor(mag[:], mag[:], E.mod[:, k, :], ALU.max))
                link(nc.vector.tensor_scalar(sign[:], E.mod[:, k, :], 0.0, None, ALU.is_ge))
                link(nc.vector.tensor_scalar(sign[:], sign[:], 2.0, -1.0, ALU.mult, ALU.add))
                link(nc.vector.tensor_tensor(E.mod[:, k, :], sign[:], mag[:], ALU.mult))
            link(nc.vector.tensor_scalar(mag[:], E.mod[:, 1, :], dvm[:, 0:1], None, ALU.mult))
            link(nc.vector.tensor_tensor(E.skip[:, 0, :], mag[:], E.mod[:, 2, :], ALU.mult))
            link(nc.vector.tensor_scalar(sign[:], E.mod[:, 0, :], dvm[:, 0:1], E.col("bo"), ALU.mult, ALU.add))
            nc.vector.tensor_tensor(E.skip[:, 1, :], sign[:], E.mod[:, 2, :], ALU.mult).then_inc(mod_ready, 1)

            dve.wait_ge(x_early, 16)
            for s in turns(dve, NCH, 1):
                if c := s.back(0):
                    if not (c.static and c.v < EARLY):
                        dve.wait_ge(x_late, 16)
                    for j in range(4):
                        i = nc.vector.bn_stats(stats[c.par][:, j, :], E.bufH[:, bass.ds(c.v * CH + j * P, P)])
                    i.then_inc(stats_made, 1)
                    dve.wait_ge(stats_made, c.times(1, 1))
                    nc.vector.tensor_copy(spare[:], E.eps)
                    for j in range(4):
                        i = nc.vector.bn_aggr(mv[c.par][:, j, :], stats[c.par][:, j, :])
                    i.then_inc(mv_ready, 1)
                if c := s.back(1):
                    dve.wait_ge(std_ready, c.times(1, 1))
                    wait(dve, turned, c.times(1, -1))
                    nc.vector.reciprocal(rstd[c.par][:], std[c.par][:]).then_inc(rstd_ready, 1)
                    dve.wait_ge(rstd_ready, c.times(1, 1))
                    for j in range(4):
                        i = nc.vector.tensor_scalar(xn[c.par][:, j * P:(j + 1) * P], E.bufH[:, bass.ds(c.v * CH + j * P, P)],
                                                    mv[c.par][:, j, 0:1], rstd[c.par][:, j:j + 1],
                                                    ALU.subtract, ALU.mult)
                    i.then_inc(normed, 1)

        @block.scalar
        def _(act):
            act.wait_ge(loaded, 16 * len(first))
            nc.scalar.activation(sct[:], ct[:], ACT.Silu).then_inc(c_silu, 1)
            nc.scalar.activation(aexp[:], alog[:], ACT.Exp).then_inc(a_exp, 1)
            act.wait_ge(mod_ready, 1)
            for s in turns(act, NCH, 2):
                if c := s.back(0):
                    act.wait_ge(mv_ready, c.times(1, 1))
                    nc.scalar.activation(std[c.par][:], mv[c.par][:, :, 1], ACT.Sqrt, bias=E.eps).then_inc(std_ready, 1)
                if c := s.back(2):
                    act.wait_ge(turned, c.times(1, 1))
                    wait(act, skip_added, c.times(1, -1))
                    for k in range(2):
                        at = bass.ds(c.v * 2 + k, 1)
                        nc.scalar.activation(sk[c.par][:, k * B:(k + 1) * B], pt[c.par][:, k * B:(k + 1) * B],
                                             ACT.Identity, bias=E.skip[:, 1, at], scale=E.skip[:, 0, at])
                        i = nc.scalar.activation(E.bufH[:, bass.ds(c.v * CH + k * B, B)], pt[c.par][:, k * B:(k + 1) * B],
                                                 ACT.Identity, bias=E.mod[:, 0, at], scale=E.mod[:, 1, at])
                    i.then_inc(h_ready, 1)

        @block.gpsimd
        def _(pool):
            def diagonals(c):
                for q in range(2 * c, 2 * c + 2):
                    nc.gpsimd.tensor_scalar(E.diag_cb[:, q // NST, q % NST, :], E.ident,
                                            E.cb[:, q // NST, q % NST:q % NST + 1], None, ALU.mult)

            pool.wait_ge(cb_ready, 1)
            for c in range(NCH):
                diagonals(c)
                pool.wait_ge(h_ready, c + 1)
                if c == 0:
                    pool.wait_ge(xT_early, 16)
                if c == EARLY:
                    pool.wait_ge(xT_late, 16)
                x = E.bufX[:, c * CH:(c + 1) * CH]
                nc.gpsimd.tensor_tensor(x, x, sk[c % 2][:], ALU.add).then_inc(skip_added, 1)


def scan_phase(nc, t, sb, ps, sems, E):
    ITEMS = 2 * NST
    with ExitStack() as st:
        xin = [sb(st, f"xin{i}", [P, GS, PADB]) for i in range(2)]
        u = [sb(st, f"u{i}", [P, 2, GR]) for i in range(2)]
        dt = [sb(st, f"dt{i}", [P, 2, GR]) for i in range(2)]
        z = [sb(st, f"z{i}", [P, 2, GR]) for i in range(2)]
        tap = [sb(st, f"tap{i}", [P, GR]) for i in range(2)]
        soft = [sb(st, f"soft{i}", [P, GR]) for i in range(2)]
        a = [sb(st, f"a{i}", [P, GR]) for i in range(RING)]
        g_ = [sb(st, f"g{i}", [P, GR]) for i in range(RING)]
        yg = [sb(st, f"yg{i}", [P, GR]) for i in range(2)]
        mix = sb(st, "mix", [P, GR])
        fp = [ps(st, f"fp{i}", [P, GR]) for i in range(2)]
        yp = [ps(st, f"yp{i}", [P, GR]) for i in range(2)]
        (padded, filled, drained, tap_ready, tap_added, relu_ready, exp1_ready, soft_ready, dt_added, u_ready,
         w_ready, dt_set, decay_ready, scanned, summed, gated, x1_ready, front_tap) = sems(
            st, "padded", "filled", "drained", "tap_ready", "tap_added", "relu_ready", "exp1_ready", "soft_ready",
            "dt_added", "u_ready", "w_ready", "dt_set", "decay_ready", "scanned", "summed", "gated", "x1_ready", "front_tap")

        OUT, XIN0, DT0, Z0 = 0, 1, 3, 5

        def unit(g, k):
            if isinstance(g, int) and g < 1:
                return 6 * (g + 1) + k - 1
            if isinstance(g, int) and g == NG:
                return unit(NG - 1, 0) + 1
            return g * 7 + (5 + k)

        def slot(par, g, k):
            if isinstance(g, int):
                return unit(g, k) % 2
            return (par + 5 + k) % 2

        def groups(eng, slots):
            slots(-1, 1, False, True)
            slots(0, 0, False, True)
            with eng.Fori(0, NG // 2 - 1) as i:
                slots(i * 2 + 1, 1, True, True)
                slots(i * 2 + 2, 0, True, True)
            slots(NG - 1, 1, True, False)
            slots(NG, 0, True, False)

        block = st.enter_context(nc.Block())

        @block.tensor
        def _(pe):
            def project(g, par, k, m):
                f = fp[slot(par, g, k)]
                wait(pe, drained, unit(g, k) - 1)
                for n in range(2):
                    i = nc.tensor.matmul(f[:, n * CH:(n + 1) * CH], E.wi[:, m * P:(m + 1) * P],
                                         E.bufH[:, bass.ds((g + 1) * GR + n * CH, CH)], start=True, stop=True)
                i.then_inc(filled, 1)

            def project_dt(g, par, k, h):
                f = fp[slot(par, g, k)]
                wait(pe, drained, unit(g, k) - 1)
                pe.wait_ge(drained, unit(g, XIN0) + 1)
                for n in range(2):
                    i = nc.tensor.matmul(f[:, n * CH:(n + 1) * CH], E.wdt[:, h * P:(h + 1) * P],
                                         xin[0][0:DTR, 2 * n:2 * n + 2, DCONV - 1:PADB], start=True, stop=True)
                i.then_inc(filled, 1)

            def output(g, par):
                f = fp[slot(par, g, OUT)]
                wait(pe, drained, unit(g, OUT) - 1)
                pe.wait_ge(gated, g * 2)
                for n in range(2):
                    o = f[:, n * CH:(n + 1) * CH]
                    nc.tensor.matmul(o, E.wo[:, 0, :], yg[0][:, n * CH:(n + 1) * CH], start=True, stop=False)
                    i = nc.tensor.matmul(o, E.wo[:, 1, :], yg[1][:, n * CH:(n + 1) * CH], start=False, stop=True)
                i.then_inc(filled, 1)

            def sum_states(g, j):
                h, n = j // NST, j % NST
                if n == 0:
                    wait(pe, gated, g * 2 + h - 1)
                pe.wait_ge(scanned, g * ITEMS + j + 1)
                for q in range(2):
                    i = nc.tensor.matmul(yp[h][:, q * CH:(q + 1) * CH], E.diag_cb[:, h, n, :],
                                         g_[j % RING][:, q * CH:(q + 1) * CH], start=(n == 0), stop=(n == NST - 1))
                i.then_inc(summed, 1)

            def slots(g, par, prev, nxt):
                scans = nxt or (isinstance(g, int) and g == NG - 1)
                if isinstance(g, int) and g < 0:
                    scans = False
                for j in range(ITEMS):
                    if j == 4 and prev:
                        output(g, par)
                    if nxt:
                        if j in (6, 8):
                            project(g, par, XIN0 + (j - 6) // 2, (j - 6) // 2)
                        if j in (12, 14):
                            project_dt(g, par, DT0 + (j - 12) // 2, (j - 12) // 2)
                        if j in (24, 26):
                            project(g, par, Z0 + (j - 24) // 2, 2 + (j - 24) // 2)
                    if scans:
                        sum_states(g, j)

            pe.wait_ge(padded, 2)
            groups(pe, slots)

        @block.scalar
        def _(act):
            def evac_xin(g, par, h):
                k = XIN0 + h
                act.wait_ge(filled, unit(g, k) + 1)
                wait(act, tap_ready, g * 8)
                i = nc.scalar.activation(xin[h][:, :, DCONV - 1:PADB], fp[slot(par, g, k)][:].rearrange("p (s b) -> p s b", s=GS),
                                         ACT.Identity, bias=E.col("bi", h))
                i.then_inc(drained, 1)

            def taps(g, par, h, k):
                act.wait_ge(drained, unit(g, XIN0 + h) + 1)
                src = xin[h][:, :, k:k + B]
                w = E.col("conv_w", h * 4 + k)
                n = (g + 1) * 6 + h * 3 + k - 1
                if k == 0:
                    wait(act, scanned, g * ITEMS)
                    dst = u[1 - par][:, h, :].rearrange("p (s b) -> p s b", s=GS)
                    i = nc.scalar.activation(dst, src, ACT.Identity, bias=E.col("conv_b", h), scale=w)
                else:
                    wait(act, tap_added, n - 1)
                    dst = tap[(h * 3 + k - 1) % 2][:].rearrange("p (s b) -> p s b", s=GS)
                    i = nc.scalar.activation(dst, src, ACT.Identity, scale=w)
                i.then_inc(tap_ready, 1)

            def soft_plus(g, par, h, part):
                k = DT0 + h
                if part == 0:
                    act.wait_ge(filled, unit(g, k) + 1)
                    wait(act, dt_added, (g + 1) * 2 + h - 1)
                    nc.scalar.activation(dt[1 - par][:, h, :], fp[slot(par, g, k)][:], ACT.Relu,
                                         bias=E.col("bdt", h)).then_inc(relu_ready, 1)
                    i = nc.scalar.activation(soft[h][:], fp[slot(par, g, k)][:], ACT.Abs, bias=E.col("bdt", h))
                    i.then_inc(drained, 1)
                elif part == 1:
                    act.wait_ge(drained, unit(g, k) + 1)
                    nc.scalar.activation(soft[h][:], soft[h][:], ACT.Exp, scale=-1.0).then_inc(exp1_ready, 1)
                else:
                    act.wait_ge(exp1_ready, (g + 1) * 2 + h + 1)
                    nc.scalar.activation(soft[h][:], soft[h][:], ACT.Ln, bias=E.ones[:, 0:1]).then_inc(soft_ready, 1)

            def silu_u(g, par, h):
                act.wait_ge(tap_added, (g + 1) * 6 + 3 * h + 3)
                nc.scalar.activation(u[1 - par][:, h, :], u[1 - par][:, h, :], ACT.Silu).then_inc(u_ready, 1)

            def silu_z(g, par, h):
                k = Z0 + h
                act.wait_ge(filled, unit(g, k) + 1)
                wait(act, gated, g * 2)
                i = nc.scalar.activation(z[1 - par][:, h, :], fp[slot(par, g, k)][:], ACT.Silu, bias=E.col("bi", 2 + h))
                i.then_inc(drained, 1)

            def evac_out(g, par):
                act.wait_ge(filled, unit(g, OUT) + 1)
                wait(act, x1_ready, g - 1)
                for s in range(GS):
                    at = bass.ds((g - 1) * GS + s, 1)
                    i = nc.scalar.activation(mix[:, s * B:(s + 1) * B], fp[slot(par, g, OUT)][:, s * B:(s + 1) * B],
                                             ACT.Identity, scale=E.mod[:, 2, at])
                i.then_inc(drained, 1)

            def decay(g, par, j):
                h, n = j // NST, j % NST
                if j == 0:
                    act.wait_ge(dt_set, g + 1)
                wait(act, scanned, g * ITEMS + j - RING + 1)
                nc.scalar.activation(a[j % RING][:], dt[par][:, h, :], ACT.Exp, scale=E.A[:, h, n:n + 1]).then_inc(decay_ready, 1)

            TAP_AT = {9: (0, 0), 11: (0, 1), 12: (0, 2), 13: (0, 3), 15: (1, 0), 17: (1, 1), 19: (1, 2), 21: (1, 3)}
            SOFT_AT = {14: (0, 0), 16: (1, 0), 18: (0, 1), 20: (1, 1)}

            def slots(g, par, prev, nxt):
                scans = not (isinstance(g, int) and (g < 0 or g == NG))
                for j in range(ITEMS):
                    if scans:
                        decay(g, par, j)
                    if j == 5 and prev:
                        evac_out(g, par)
                    if nxt:
                        if j == 7:
                            evac_xin(g, par, 0)
                        if j == 10:
                            evac_xin(g, par, 1)
                        front = isinstance(g, int) and g < 0
                        if j in TAP_AT and not front:
                            taps(g, par, *TAP_AT[j])
                        if j in SOFT_AT:
                            soft_plus(g, par, *SOFT_AT[j])
                        if j == 29:
                            soft_plus(g, par, 0, 2)
                            soft_plus(g, par, 1, 2)
                            silu_u(g, par, 0)
                            silu_u(g, par, 1)
                            silu_z(g, par, 0)
                            silu_z(g, par, 1)

            act.wait_ge(padded, 2)
            groups(act, slots)

        @block.gpsimd
        def _(pool):
            def slots(g, par, prev, nxt):
                if prev:
                    pool.wait_ge(drained, unit(g, OUT) + 1)
                    x1 = E.bufX[:, bass.ds((g - 1) * GR, GR)]
                    nc.gpsimd.tensor_tensor(x1, x1, mix[:], ALU.add).then_inc(x1_ready, 1)
                if nxt and not (isinstance(g, int) and g < 0):
                    for h in range(2):
                        uh = u[1 - par][:, h, :]
                        for k in range(1, DCONV):
                            pool.wait_ge(tap_ready, g * 8 + h * 4 + k + 1)
                            wait(pool, tap_added, (g + 1) * 6 + h * 3 + k - 1)
                            nc.gpsimd.tensor_tensor(uh, uh, tap[(h * 3 + k - 1) % 2][:], ALU.add).then_inc(tap_added, 1)
                    for h in range(2):
                        dh = dt[1 - par][:, h, :]
                        pool.wait_ge(soft_ready, (g + 1) * 2 + h + 1)
                        nc.gpsimd.tensor_tensor(dh, dh, soft[h][:], ALU.add).then_inc(dt_added, 1)
                    for h in range(2):
                        uh, dh = u[1 - par][:, h, :], dt[1 - par][:, h, :]
                        pool.wait_ge(u_ready, (g + 1) * 2 + h + 1)
                        pool.wait_ge(dt_added, (g + 1) * 2 + h + 1)
                        nc.gpsimd.tensor_tensor(uh, uh, dh, ALU.mult).then_inc(w_ready, 1)
                    pool.wait_ge(w_ready, (g + 1) * 2 + 2)
                    firsts = dt[1 - par][:].rearrange("p h (s b) -> p (h s) b", s=GS)[:, :, 0:1]
                    nc.gpsimd.tensor_tensor(firsts, firsts, E.const("big").unsqueeze(1).to_broadcast([P, 2 * GS, 1]),
                                            ALU.add).then_inc(dt_set, 1)

            for h in range(2):
                nc.gpsimd.memset(xin[h][:, :, 0:DCONV - 1], 0.0).then_inc(padded, 1)
            groups(pool, slots)

        @block.vector
        def _(dve):
            def gate_y(g, h, par):
                dve.wait_ge(summed, g * ITEMS + (h + 1) * NST)
                if h == 0:
                    dve.wait_ge(drained, unit(g - 1, Z0 + 1) + 1)
                if not (isinstance(g, int) and g == 0):
                    dve.wait_ge(filled, unit(g, OUT) + 1)
                nc.vector.tensor_tensor(yg[h][:], yp[h][:], z[par][:, h, :], ALU.mult).then_inc(gated, 1)

            def front():
                for h in range(2):
                    uh = u[0][:, h, :].rearrange("p (s b) -> p s b", s=GS)
                    dve.wait_ge(drained, unit(-1, XIN0 + h) + 1)
                    nc.vector.tensor_scalar(uh, xin[h][:, :, 0:B], E.col("conv_w", h * 4), E.col("conv_b", h),
                                            ALU.mult, ALU.add).then_inc(front_tap, 1)
                    for k in range(1, DCONV):
                        dve.wait_ge(front_tap, 3 * h + k)
                        i = nc.vector.scalar_tensor_tensor(uh, xin[h][:, :, k:k + B], E.col("conv_w", h * 4 + k), uh,
                                                           ALU.mult, ALU.add)
                        i.then_inc(*((front_tap, 1) if k < DCONV - 1 else (tap_added, 3)))
                for h in range(2):
                    dve.wait_ge(soft_ready, h + 1)
                    nc.vector.tensor_tensor(dt[0][:, h, :], dt[0][:, h, :], soft[h][:], ALU.add).then_inc(dt_added, 1)
                for h in range(2):
                    dve.wait_ge(u_ready, h + 1)
                    dve.wait_ge(dt_added, h + 1)
                    nc.vector.tensor_tensor(u[0][:, h, :], u[0][:, h, :], dt[0][:, h, :], ALU.mult).then_inc(w_ready, 1)
                dve.wait_ge(w_ready, 2)
                firsts = dt[0][:].rearrange("p h (s b) -> p (h s) b", s=GS)[:, :, 0:1]
                nc.vector.tensor_tensor(firsts, firsts, E.const("big").unsqueeze(1).to_broadcast([P, 2 * GS, 1]),
                                        ALU.add).then_inc(dt_set, 1)

            def slots(g, par, prev, nxt):
                scans = not (isinstance(g, int) and (g < 0 or g == NG))
                if isinstance(g, int) and g < 0:
                    front()
                for j in range(ITEMS):
                    h = j // NST
                    if scans:
                        if j % NST == 0:
                            dve.wait_ge(w_ready, g * 2 + h + 1)
                        dve.wait_ge(decay_ready, g * ITEMS + j + 1)
                        wait(dve, summed, g * ITEMS + j - RING + 1)
                        nc.vector.tensor_tensor_scan(g_[j % RING][:], a[j % RING][:], u[par][:, h, :], 0.0,
                                                     ALU.mult, ALU.add).then_inc(scanned, 1)
                    if j == 2 and prev:
                        gate_y(g - 1, 1, 1 - par)
                    if j == NST + 2 and scans:
                        gate_y(g, 0, par)

            groups(dve, slots)


def norm_mid(nc, t, sb, ps, sems, E):
    NB = CH // S
    with ExitStack() as st:
        def two(name, shape):
            return [sb(st, f"{name}{i}", shape) for i in range(2)]

        xb, xn, hm, hb, xm = (two(n, [P, CH]) for n in ("mxb", "mxn", "mhm", "mhb", "mxm"))
        stats = [two("mstatsA", [P, 4, 6]), two("mstatsB", [P, 4, 6])]
        mv = [two("mmvA", [P, 4, 2]), two("mmvB", [P, 4, 2])]
        std = [two("mstdA", [P, 4]), two("mstdB", [P, 4])]
        rstd = [two("mrstdA", [P, 4]), two("mrstdB", [P, 4])]
        pp = [[ps(st, f"mp{k}{i}", [P, CH]) for i in range(2)] for k in range(4)]
        shift = [two("mshiftA", [P, 4]), two("mshiftB", [P, 4])]
        blank = sb(st, "blank", [P, 5, 8, ROW])
        spare = sb(st, "mspare", [P, 1])
        (xb_ready, scaled, h_ready, h_kept, zeroed, blanked, cleared) = sems(
            st, "m_xb_ready", "m_scaled", "m_h_ready", "m_h_kept", "m_zeroed", "m_blanked", "m_cleared")
        turn_in, stats_made, mv_ready, std_ready, rstd_ready, normed, turn_out = (
            sems(st, f"m_{n}_A", f"m_{n}_B")
            for n in ("turn_in", "stats_made", "mv_ready", "std_ready", "rstd_ready", "normed", "turn_out"))
        (l1_ready,) = sems(st, "m_l1_ready")
        shift_ready = sems(st, "m_shift_ready_A", "m_shift_ready_B")
        block = st.enter_context(nc.Block())
        first, second = (xb, xn), (hb, xm)

        @block.sync
        def _(sp):
            sp.wait_ge(blanked, 1)
            rows = t["slots"][0:SLOTS, :].rearrange("(n p r) d -> n p (r d)", p=P, r=8)
            n_rows = SLOTS // (P * 8)
            for k in range(n_rows):
                sp.dma_start(rows[k], blank[:, k % 5, :, :].rearrange("p r d -> p (r d)")).then_inc(cleared, 16)
            sums = t["sums"].rearrange("(n p r) d -> n p r d", p=P, r=8)
            n_sums = (NT + EMPTY) // (P * 8)
            for k in range(n_sums):
                sp.dma_start(sums[k], blank[:, 0, :, 0:D]).then_inc(cleared, 16)
            sp.wait_ge(cleared, 16 * (n_rows + n_sums))

        @block.gpsimd
        def _(pool):
            x1 = E.bufX[:].rearrange("p (s b) -> p b s", s=S)
            for s in turns(pool, NCH, 3):
                if c := s.back(0):
                    wait(pool, turn_in[0], c.times(1, -1))
                    nc.gpsimd.tensor_copy(xb[c.par][:].rearrange("p (b s) -> p b s", s=S),
                                          x1[:, bass.ds(c.v * NB, NB), :]).then_inc(xb_ready, 1)
                if s.static and s.v == 1:
                    nc.gpsimd.memset(blank[:], 0.0).then_inc(zeroed, 1)
                    pool.wait_ge(zeroed, 1)
                    nc.gpsimd.tensor_copy(blank[:, :, :, D], E.const("empty").rearrange("p (n r) -> p n r", r=8)).then_inc(
                        blanked, 1)
                if c := s.back(3):
                    pool.wait_ge(scaled, c.times(1, 1))
                    wait(pool, turn_in[1], c.times(1, -1))
                    wait(pool, h_kept, c.times(1, -1))
                    nc.gpsimd.tensor_tensor(hb[c.par][:].rearrange("p (b s) -> p b s", s=S),
                                            hm[c.par][:].rearrange("p (b s) -> p b s", s=S),
                                            E.mod[:, 3, :].unsqueeze(1).to_broadcast([P, NB, S]), ALU.add).then_inc(h_ready, 1)

        @block.tensor
        def _(pe):
            def turn(c, src, dst):
                for j in range(4):
                    i = nc.tensor.transpose(dst[c.par][:, j * P:(j + 1) * P], src[c.par][:, j * P:(j + 1) * P], E.ident)
                return i

            for s in turns(pe, NCH, 6):
                if c := s.back(3):
                    pe.wait_ge(normed[0], c.times(1, 1))
                    wait(pe, scaled, c.times(1, -1))
                    turn(c, xn, pp[1]).then_inc(turn_out[0], 1)
                if c := s.back(1):
                    pe.wait_ge(xb_ready, c.times(1, 1))
                    wait(pe, normed[0], c.times(1, -1))
                    turn(c, xb, pp[0]).then_inc(turn_in[0], 1)
                if c := s.back(6):
                    pe.wait_ge(normed[1], c.times(1, 1))
                    wait(pe, l1_ready, c.times(1, -1))
                    turn(c, xm, pp[3]).then_inc(turn_out[1], 1)
                if c := s.back(4):
                    pe.wait_ge(h_ready, c.times(1, 1))
                    wait(pe, normed[1], c.times(1, -1))
                    turn(c, hb, pp[2]).then_inc(turn_in[1], 1)

        @block.vector
        def _(dve):
            def statistics(k, c):
                dve.wait_ge(turn_in[k], c.times(1, 1))
                for j in range(4):
                    i = nc.vector.bn_stats(stats[k][c.par][:, j, :], pp[2 * k][c.par][:, j * P:(j + 1) * P])
                i.then_inc(stats_made[k], 1)
                dve.wait_ge(stats_made[k], c.times(1, 1))
                nc.vector.tensor_copy(spare[:], E.eps)
                for j in range(4):
                    i = nc.vector.bn_aggr(mv[k][c.par][:, j, :], stats[k][c.par][:, j, :])
                i.then_inc(mv_ready[k], 1)

            def scale_and_shift(k, c):
                dve.wait_ge(std_ready[k], c.times(1, 1))
                wait(dve, normed[k], c.times(1, -1))
                nc.vector.reciprocal(rstd[k][c.par][:], std[k][c.par][:]).then_inc(rstd_ready[k], 1)
                dve.wait_ge(rstd_ready[k], c.times(1, 1))
                nc.vector.scalar_tensor_tensor(shift[k][c.par][:], mv[k][c.par][:, :, 0], -1.0, rstd[k][c.par][:],
                                               ALU.mult, ALU.mult).then_inc(shift_ready[k], 1)

            for s in turns(dve, NCH, 5):
                if c := s.back(2):
                    scale_and_shift(0, c)
                if c := s.back(1):
                    statistics(0, c)
                if c := s.back(5):
                    scale_and_shift(1, c)
                if c := s.back(3):
                    dve.wait_ge(turn_out[0], c.times(1, 1))
                    wait(dve, h_ready, c.times(1, -1))
                    nc.vector.tensor_tensor(hm[c.par][:].rearrange("p (b s) -> p b s", s=S),
                                            pp[1][c.par][:].rearrange("p (b s) -> p b s", s=S),
                                            E.mod[:, 4, :].unsqueeze(1).to_broadcast([P, NB, S]), ALU.mult).then_inc(scaled, 1)
                if c := s.back(4):
                    statistics(1, c)
                    dve.wait_ge(h_ready, c.times(1, 1))
                    nc.vector.tensor_copy(E.bufA[:, bass.ds(c.v * CH, CH)], hb[c.par][:]).then_inc(h_kept, 1)

        @block.scalar
        def _(act):
            def normalise(k, c, out):
                act.wait_ge(shift_ready[k], c.times(1, 1))
                wait(act, turn_out[k], c.times(1, -1))
                for j in range(4):
                    i = nc.scalar.activation(out[c.par][:, j * P:(j + 1) * P], pp[2 * k][c.par][:, j * P:(j + 1) * P],
                                             ACT.Identity, bias=shift[k][c.par][:, j:j + 1], scale=rstd[k][c.par][:, j:j + 1])
                i.then_inc(normed[k], 1)

            for s in turns(act, NCH, 6):
                if c := s.back(1):
                    act.wait_ge(mv_ready[0], c.times(1, 1))
                    nc.scalar.activation(std[0][c.par][:], mv[0][c.par][:, :, 1], ACT.Sqrt, bias=E.eps).then_inc(std_ready[0], 1)
                if c := s.back(2):
                    normalise(0, c, xn)
                if c := s.back(5):
                    normalise(1, c, xm)
                if c := s.back(4):
                    act.wait_ge(mv_ready[1], c.times(1, 1))
                    nc.scalar.activation(std[1][c.par][:], mv[1][c.par][:, :, 1], ACT.Sqrt, bias=E.eps).then_inc(std_ready[1], 1)
                if c := s.back(6):
                    act.wait_ge(turn_out[1], c.times(1, 1))
                    nc.scalar.activation(E.bufH[:, bass.ds(c.v * CH, CH)], pp[3][c.par][:], ACT.Identity,
                                         bias=E.col("ln1b"), scale=E.col("ln1w")).then_inc(l1_ready, 1)


def attention(nc, t, sb, ps, sems, E):
    NB = 16
    HB = NB // 2
    BT = NB * S
    W = 4 * HB * 2 * S
    NBLK = NT // BT
    with ExitStack() as st:
        def two(name, shape):
            return [sb(st, f"{name}{i}", shape) for i in range(2)]

        lb = two("lb", [P, BT])
        q = two("q", [P, HB, 4, 2 * S])
        kd = two("kd", [P, HB, 4, S])
        vd = two("vd", [P, NB, 2, 4 * HD])
        sc = two("sc", [P, W])
        mx, sm, rs = (two(n, [P, W // S]) for n in ("mx", "sm", "rs"))
        pr = two("pr", [P, W])
        pT = two("pT", [P, HB, 4, 2 * S])
        ot = two("ot", [P, BT])
        identb = sb(st, "identb", [P, P], BF16)
        maskb = sb(st, "maskb", [P, S], BF16)
        psL = ps(st, "psL", [P, HB, 4, 2 * S])
        psQ = ps(st, "psQ", [P, 512])
        psKV = ps(st, "psKV", [P, 512])
        psO = ps(st, "psO", [P, 512])
        psP = ps(st, "psP", [P, BT])
        psK = psKV[:, 0:256].rearrange("p (b s) -> p b s", s=S)
        psV = psKV[:, 256:512].rearrange("p (b f) -> p b f", f=KV)
        (mask_ready, zeroed, lb_ready, qkv_made, q_ready, k_ready, v_ready, scored, turned, max_ready, exped,
         sum_ready, rcp_ready, probs_ready, pT_ready, av_made, ot_ready, projected, added) = sems(
            st, "mask_ready", "a_zeroed", "lb_ready", "qkv_made", "q_ready", "k_ready", "v_ready", "scored", "a_turned",
            "max_ready", "exped", "sum_ready", "rcp_ready", "probs_ready", "pT_ready", "av_made", "ot_ready",
            "projected", "added")
        shifted = sems(st, "shifted0", "shifted1")
        block = st.enter_context(nc.Block())

        def rows(x):
            return x[:].rearrange("p (c t) -> p c t", t=S)

        @block.tensor
        def _(pe):
            pe.wait_ge(mask_ready, 2)
            for s in turns(pe, NBLK, 4):
                if c := s.back(1):
                    pe.wait_ge(q_ready, c.times(1, 1))
                    pe.wait_ge(k_ready, c.times(1, 1))
                    wait(pe, turned, c.times(1, 0))
                    for b in range(0, HB, 2):
                        nc.tensor.matmul(psL[:, b:b + 2].rearrange("p b r x -> p (b r x)"), identb[:],
                                         maskb[:].unsqueeze(1).to_broadcast([P, 16, S]), start=True, stop=False)
                    for b in range(HB):
                        i = nc.tensor.matmul(psL[:, b].rearrange("p r x -> p (r x)"), kd[c.par][:, b].rearrange("p j s -> p (j s)"),
                                             q[c.par][:, b].rearrange("p r x -> p (r x)"), start=False, stop=(b % 2 == 1))
                    i.then_inc(scored, 1)
                if s.back(0) or s.back(1):
                    if c := s.back(0):
                        pe.wait_ge(lb_ready, c.times(1, 1))
                        wait(pe, q_ready, c.times(1, 0))
                        wait(pe, k_ready, c.times(1, 0))
                        wait(pe, v_ready, c.times(1, -1))
                        nc.tensor.matmul(psQ[:], E.wq[:], lb[c.par][:], start=True, stop=True)
                        for bh in range(2):
                            i = nc.tensor.matmul(psK[64 * bh:64 * bh + 64], E.wk[:],
                                                 lb[c.par][:, bh * BT // 2:(bh + 1) * BT // 2],
                                                 start=True, stop=True, tile_position=(0, 64 * bh))
                    if c := s.back(1):
                        wait(pe, v_ready, c.times(1, 0))
                        for b4 in range(NB // 4):
                            i = nc.tensor.matmul(psV[:, b4, :], lb[c.par][:, b4 * P:(b4 + 1) * P], E.wv[:],
                                                 start=True, stop=True)
                    i.then_inc(qkv_made, 1)
                if c := s.back(4):
                    pe.wait_ge(ot_ready, c.times(1, 1))
                    wait(pe, added, c.times(1, 0))
                    nc.tensor.matmul(psP[:], E.wp[:], ot[c.par][:], start=True, stop=True).then_inc(projected, 1)
                if c := s.back(3):
                    pe.wait_ge(pT_ready, c.times(1, 1))
                    pe.wait_ge(v_ready, c.times(1, 1))
                    wait(pe, ot_ready, c.times(1, 0))
                    for b in range(HB):
                        for r in range(4):
                            bh, jg = divmod(r, 2)
                            i = nc.tensor.matmul(psO[32 * r:32 * r + 32, b * 64:(b + 1) * 64],
                                                 vd[c.par][:, bh * HB + b, jg, :], pT[c.par][:, b, r, :],
                                                 start=True, stop=True, tile_position=(0, 32 * r))
                    i.then_inc(av_made, 1)

        def shift(engine, c, half):
            at = slice(half * W // S // 2, (half + 1) * W // S // 2)
            x = rows(sc[c.par])[:, at, :]
            return engine.tensor_tensor(x, x, mx[c.par][:, at].unsqueeze(2).to_broadcast([P, W // S // 2, S]), ALU.subtract)

        @block.gpsimd
        def _(pool):
            for x in (*q, *vd):
                nc.gpsimd.memset(x[:], 0.0).then_inc(zeroed, 1)
            for s in turns(pool, NBLK, 2):
                if c := s.back(2):
                    pool.wait_ge(rcp_ready, c.times(1, 1))
                    wait(pool, pT_ready, c.times(1, -1))
                    nc.gpsimd.tensor_tensor(rows(pr[c.par]), rows(sc[c.par]),
                                            rs[c.par][:].unsqueeze(2).to_broadcast([P, W // S, S]),
                                            ALU.mult).then_inc(probs_ready, 1)
                if c := s.back(1):
                    pool.wait_ge(max_ready, c.times(1, 1))
                    shift(nc.gpsimd, c, 1).then_inc(shifted[1], 1)

        @block.scalar
        def _(act):
            nc.scalar.activation(identb[:], E.ident, ACT.Copy).then_inc(mask_ready, 1)
            nc.scalar.activation(maskb[:], E.const("causal"), ACT.Copy).then_inc(mask_ready, 1)
            act.wait_ge(zeroed, 2)
            for s in turns(act, NBLK, 3):
                if c := s.back(0):
                    act.wait_ge(qkv_made, c.times(1, 1))
                    wait(act, scored, c.times(1, -1))
                    for r in range(4):
                        bh, jg = divmod(r, 2)
                        for g in range(2):
                            at = 64 * g + 32 * jg
                            i = nc.scalar.activation(q[c.par][32 * r:32 * r + 32, :, r, g * S:(g + 1) * S],
                                                     psQ[at:at + 32, bh * BT // 2:(bh + 1) * BT // 2]
                                                     .rearrange("p (b s) -> p b s", s=S), ACT.Identity)
                    i.then_inc(q_ready, 1)
                    for j in range(4):
                        i = nc.scalar.activation(kd[c.par][:, :, j, :], psK, ACT.Copy, scale=E.const("head4")[:, j:j + 1])
                    i.then_inc(k_ready, 1)
                if c := s.back(1):
                    for half in range(2):
                        act.wait_ge(shifted[half], c.times(1, 1))
                        x = sc[c.par][:, half * W // 2:(half + 1) * W // 2]
                        i = nc.scalar.activation(x, x, ACT.Exp, scale=float(HD) ** -0.5)
                    i.then_inc(exped, 1)
                if c := s.back(3):
                    act.wait_ge(av_made, c.times(1, 1))
                    wait(act, projected, c.times(1, -1))
                    for bh in range(2):
                        for g in range(2):
                            i = nc.scalar.activation(ot[c.par][64 * g:64 * g + 64, bh * BT // 2:(bh + 1) * BT // 2]
                                                     .rearrange("p (b s) -> p b s", s=S),
                                                     psO[64 * bh:64 * bh + 64].rearrange("p (b g s) -> p b g s", g=2, s=S)[:, :, g, :],
                                                     ACT.Identity)
                    i.then_inc(ot_ready, 1)
                if c := s.back(1):
                    act.wait_ge(zeroed, 4)
                    act.wait_ge(qkv_made, c.times(1, 2))
                    wait(act, av_made, c.times(1, -1))
                    for j in range(4):
                        for b in range(4):
                            i = nc.scalar.activation(
                                vd[c.par][32 * j:32 * j + 32, b::4, :, j * HD:(j + 1) * HD],
                                psV[32 * b:32 * b + 32].rearrange("p b (g x) -> p b g x", g=2)[:, :, :, j * HD:(j + 1) * HD],
                                ACT.Identity)
                    i.then_inc(v_ready, 1)

        @block.vector
        def _(dve):
            for s in turns(dve, NBLK, 4):
                if c := s.back(0):
                    wait(dve, qkv_made, c.times(1, 0))
                    nc.vector.tensor_copy(lb[c.par][:], E.bufH[:, bass.ds(c.v * BT, BT)]).then_inc(lb_ready, 1)
                if c := s.back(3):
                    dve.wait_ge(probs_ready, c.times(1, 1))
                    wait(dve, av_made, c.times(1, -1))
                    nc.vector.transpose(pT[c.par][:].rearrange("p b r x -> p (b r x)"), pr[c.par][:]).then_inc(pT_ready, 1)
                if c := s.back(2):
                    dve.wait_ge(exped, c.times(1, 1))
                    nc.vector.tensor_reduce(sm[c.par][:], rows(sc[c.par]), AX_X, ALU.add).then_inc(sum_ready, 1)
                    dve.wait_ge(sum_ready, c.times(1, 1))
                    nc.vector.reciprocal(rs[c.par][:], sm[c.par][:]).then_inc(rcp_ready, 1)
                if c := s.back(1):
                    dve.wait_ge(scored, c.times(1, 1))
                    wait(dve, probs_ready, c.times(1, -1))
                    nc.vector.transpose(sc[c.par][:], psL[:].rearrange("p b r x -> p (b r x)")).then_inc(turned, 1)
                    dve.wait_ge(turned, c.times(1, 1))
                    nc.vector.tensor_reduce(mx[c.par][:], rows(sc[c.par]), AX_X, ALU.max).then_inc(max_ready, 1)
                    dve.wait_ge(max_ready, c.times(1, 1))
                    shift(nc.vector, c, 0).then_inc(shifted[0], 1)
                if c := s.back(4):
                    dve.wait_ge(projected, c.times(1, 1))
                    ha = E.bufA[:, bass.ds(c.v * BT, BT)]
                    nc.vector.tensor_tensor(ha, psP[:], ha, ALU.add).then_inc(added, 1)


def norm_route(nc, t, sb, ps, sems, E):
    with ExitStack() as st:
        def two(name, shape, dt=F32):
            return [sb(st, f"{name}{i}", shape, dt) for i in range(2)]

        hb, xn, xs = (two(n, [P, CH]) for n in ("ohb", "oxn", "oxs"))
        stats, mv, std, rstd = two("ostats", [P, 4, 6]), two("omv", [P, 4, 2]), two("ostd", [P, 4]), two("orstd", [P, 4])
        rows = two("orows", [P, QT, ROW])
        idx = two("oidx", [P, 2, QT], U32)
        N8 = [P, QT, NE]
        logit = sb(st, "ologit", N8)
        prob, pick1, pick2, key, rest, both, past, tally, rank, keep = (
            sb(st, f"r_{n}", N8)
            for n in ("prob", "pick1", "pick2", "key", "rest", "both", "past", "tally", "rank", "keep"))
        carried = sb(st, "r_carried", [P, NE])
        m1, m2, km, ssum, at, kept, spare1 = (
            sb(st, f"r_{n}", [P, QT]) for n in ("m1", "m2", "km", "ssum", "at", "kept", "spare"))
        p0, p1, p2 = ([ps(st, f"o{n}{i}", [P, CH]) for i in range(2)] for n in ("p0", "p1", "p2"))
        pl = ps(st, "opl", [P, 4, NE])
        pr = ps(st, "opr", N8)
        (hb_ready, turned0, stats_made, mv_ready, std_ready, rstd_ready, normed, turned1, xs_ready, turned2,
         logit_ready, kept_rows, step, shifted, exped, picked, counted, routed) = sems(
            st, "o_hb_ready", "o_turned0", "o_stats_made", "o_mv_ready", "o_std_ready", "o_rstd_ready", "o_normed",
            "o_turned1", "o_xs_ready", "o_turned2", "o_logit_ready", "o_kept_rows", "r_step", "r_shifted", "r_exped",
            "r_picked", "r_counted", "r_routed")
        scattered = sems(st, "r_scattered0", "r_scattered1")
        block = st.enter_context(nc.Block())

        def part_after(s):
            c = s.back(4)
            return c.v // QC if c and c.v % QC == QC - 1 else None

        @block.tensor
        def _(pe):
            for s in steps(NCH, 4):
                if c := s.back(1):
                    pe.wait_ge(hb_ready, c.v + 1)
                    wait(pe, normed, c.v - 1)
                    for j in range(4):
                        i = nc.tensor.transpose(p0[c.par][:, j * P:(j + 1) * P], hb[c.par][:, j * P:(j + 1) * P], E.ident)
                    i.then_inc(turned0, 1)
                if c := s.back(4):
                    pe.wait_ge(xs_ready, c.v + 1)
                    wait(pe, kept_rows, c.v - 1)
                    wait(pe, logit_ready, c.v)
                    for j in range(4):
                        xj = xs[c.par][:, j * P:(j + 1) * P]
                        nc.tensor.matmul(pl[:, j, :], xj, E.router[:], start=True, stop=True)
                        i = nc.tensor.transpose(p2[c.par][:, j * P:(j + 1) * P], xj, E.ident)
                    i.then_inc(turned2, 1)
                if c := s.back(2):
                    pe.wait_ge(normed, c.v + 1)
                    wait(pe, xs_ready, c.v - 1)
                    for j in range(4):
                        i = nc.tensor.transpose(p1[c.par][:, j * P:(j + 1) * P], xn[c.par][:, j * P:(j + 1) * P], E.ident)
                    i.then_inc(turned1, 1)
                if (q := part_after(s)) is not None:
                    pe.wait_ge(picked, q + 1)
                    o = pr[:].rearrange("p t e -> p (t e)")
                    nc.tensor.matmul(o, E.const("before"), both[:].rearrange("p t e -> p (t e)"), start=True, stop=False)
                    nc.tensor.matmul(o, E.ones, past[:].rearrange("p t e -> p (t e)"), start=False,
                                     stop=True).then_inc(counted, 1)

        @block.scalar
        def _(act):
            ha = E.bufA[:].rearrange("p (b s) -> p s b", s=S)
            for s in steps(NCH, 4):
                if c := s.back(1):
                    act.wait_ge(mv_ready, c.v + 1)
                    nc.scalar.activation(std[c.par][:], mv[c.par][:, :, 1], ACT.Sqrt, bias=E.eps).then_inc(std_ready, 1)
                if c := s.back(0):
                    wait(act, turned0, c.v - 1)
                    nc.scalar.activation(hb[c.par][:].rearrange("p (s b) -> p s b", b=B),
                                         ha[:, 2 * c.v:2 * c.v + 2, :], ACT.Identity).then_inc(hb_ready, 1)
                if c := s.back(3):
                    act.wait_ge(turned1, c.v + 1)
                    wait(act, turned2, c.v - 1)
                    nc.scalar.activation(xs[c.par][:], p1[c.par][:], ACT.Identity, bias=E.col("ln2b"),
                                         scale=E.col("ln2w")).then_inc(xs_ready, 1)
                if c := s.back(4):
                    act.wait_ge(turned2, c.v + 1)
                    q, k = divmod(c.v, QC)
                    wait(act, scattered[q % 2], 16 * 2 * QT * (q // 2))
                    nc.scalar.activation(rows[q % 2][:, 4 * k:4 * k + 4, 0:D],
                                         p2[c.par][:].rearrange("p (j d) -> p j d", j=4), ACT.Identity).then_inc(kept_rows, 1)
                if (q := part_after(s)) is not None:
                    act.wait_ge(shifted, q + 1)
                    nc.scalar.activation(prob[:], prob[:], ACT.Exp).then_inc(exped, 1)

        @block.vector
        def _(dve):
            n = 0

            def link(ins):
                nonlocal n
                n += 1
                ins.then_inc(step, 1)
                dve.wait_ge(step, n)

            def tt(out, a, b, op):
                link(nc.vector.tensor_tensor(out, a, b, op))

            def total(out, x):
                link(nc.vector.tensor_reduce(out, x, AX_X, ALU.add))

            def wide(x):
                return x[:].unsqueeze(2).to_broadcast(N8)

            def row(name):
                return E.const(name).unsqueeze(1).to_broadcast(N8)

            def pick(src, best, out):
                link(nc.vector.tensor_reduce(best[:], src[:], AX_X, ALU.max))
                tt(key[:], src[:], wide(best), ALU.is_equal)
                tt(key[:], key[:], row("rev"), ALU.mult)
                link(nc.vector.tensor_reduce(km[:], key[:], AX_X, ALU.max))
                tt(out[:], key[:], wide(km), ALU.is_equal)

            def route(q):
                token = E.const("token")[:, q * QT:(q + 1) * QT]
                r = rows[q % 2]
                link(nc.vector.tensor_reduce(m1[:], logit[:], AX_X, ALU.max))
                nc.vector.tensor_tensor(prob[:], logit[:], wide(m1), ALU.subtract).then_inc(shifted, 1)
                dve.wait_ge(exped, q + 1)
                total(ssum[:], prob[:])
                link(nc.vector.reciprocal(ssum[:], ssum[:]))
                tt(prob[:], prob[:], wide(ssum), ALU.mult)
                pick(prob, m1, pick1)
                wait(dve, scattered[q % 2], 16 * 2 * QT * (q // 2))
                nc.vector.tensor_scalar(r[:, :, D + 3], km[:], -1.0, float(NE), ALU.mult, ALU.add)
                nc.vector.tensor_copy(r[:, :, D], token)
                link(nc.vector.scalar_tensor_tensor(rest[:], pick1[:], -2.0, prob[:], ALU.mult, ALU.add))
                pick(rest, m2, pick2)
                tt(both[:], pick1[:], pick2[:], ALU.add)
                nc.vector.tensor_copy(past[:, 0, :], carried[:])
                link(nc.vector.tensor_copy(past[:, 1:QT, :], both[:, 0:QT - 1, :]))
                src, dst, d = past, tally, 1
                while d < QT:
                    nc.vector.tensor_copy(dst[:, 0:d, :], src[:, 0:d, :])
                    tt(dst[:, d:QT, :], src[:, d:QT, :], src[:, 0:QT - d, :], ALU.add)
                    src, dst, d = dst, src, 2 * d
                assert src is past
                nc.vector.tensor_tensor(carried[:], past[:, QT - 1, :], both[:, QT - 1, :], ALU.add).then_inc(picked, 1)
                tt(ssum[:], m1[:], m2[:], ALU.add)
                link(nc.vector.reciprocal(ssum[:], ssum[:]))
                nc.vector.tensor_tensor(r[:, :, D + 1], m1[:], ssum[:], ALU.mult)
                nc.vector.tensor_tensor(r[:, :, D + 2], m2[:], ssum[:], ALU.mult)
                dve.wait_ge(counted, q + 1)
                nc.vector.tensor_scalar(keep[:], pr[:], float(CAP), None, ALU.is_lt)
                tt(rank[:], pr[:], row("slot0"), ALU.add)
                for k, pick_k in enumerate((pick1, pick2)):
                    link(nc.vector.tensor_scalar(spare1[:], token, float(SLOTS + k * NT), None, ALU.add))
                    tt(key[:], pick_k[:], rank[:], ALU.mult)
                    total(at[:], key[:])
                    tt(key[:], pick_k[:], keep[:], ALU.mult)
                    total(kept[:], key[:])
                    tt(at[:], at[:], spare1[:], ALU.subtract)
                    tt(at[:], at[:], kept[:], ALU.mult)
                    tt(at[:], at[:], spare1[:], ALU.add)
                    i = nc.vector.tensor_copy(idx[q % 2][:, k, :], at[:])
                    i.then_inc(routed, 1)

            link(nc.vector.memset(carried[:], 0.0))
            for s in steps(NCH, 4):
                if c := s.back(2):
                    dve.wait_ge(std_ready, c.v + 1)
                    wait(dve, turned1, c.v - 1)
                    nc.vector.reciprocal(rstd[c.par][:], std[c.par][:]).then_inc(rstd_ready, 1)
                    dve.wait_ge(rstd_ready, c.v + 1)
                    for j in range(4):
                        i = nc.vector.tensor_scalar(xn[c.par][:, j * P:(j + 1) * P], p0[c.par][:, j * P:(j + 1) * P],
                                                    mv[c.par][:, j, 0:1], rstd[c.par][:, j:j + 1],
                                                    ALU.subtract, ALU.mult)
                    i.then_inc(normed, 1)
                if c := s.back(1):
                    dve.wait_ge(turned0, c.v + 1)
                    for j in range(4):
                        i = nc.vector.bn_stats(stats[c.par][:, j, :], p0[c.par][:, j * P:(j + 1) * P])
                    i.then_inc(stats_made, 1)
                    dve.wait_ge(stats_made, c.v + 1)
                    for j in range(4):
                        i = nc.vector.bn_aggr(mv[c.par][:, j, :], stats[c.par][:, j, :])
                    i.then_inc(mv_ready, 1)
                if c := s.back(4):
                    k = c.v % QC
                    dve.wait_ge(turned2, c.v + 1)
                    nc.vector.tensor_copy(logit[:, 4 * k:4 * k + 4, :], pl[:]).then_inc(logit_ready, 1)
                if (q := part_after(s)) is not None:
                    dve.wait_ge(logit_ready, (q + 1) * QC)
                    route(q)

        @block.gpsimd
        def _(pool):
            for q in range(Q):
                pool.wait_ge(kept_rows, (q + 1) * QC)
                for k in range(2):
                    pool.wait_ge(routed, 2 * q + k + 1)
                    for j in range(QT):
                        pool.indirect_dma_start(t["slots"], bass.IndirectOffsetOnAxis(ap=idx[q % 2][:, k, j:j + 1], axis=0),
                                                rows[q % 2][:, j, :], None).then_inc(scattered[q % 2], 16)
            for k in range(2):
                pool.wait_ge(scattered[k], 16 * 2 * QT * (Q // 2))


class Chunk(Turn):

    def __init__(self, v, phase, n, static, per, pass_no):
        super().__init__(v, phase % 2, n, static)
        self.phase, self.per, self.pass_no = phase, per, pass_no

    def back(self, k):
        if self.static:
            c = self.v - k
            period = 2 * self.per
            return Chunk(c, c % period, self.n, True, self.per, c // period) if 0 <= c < self.n else None
        phase = (self.phase - k) % (2 * self.per)
        passes = self.pass_no - 1 if self.phase < k else self.pass_no
        return Chunk(self.v - k if k else self.v, phase, self.n, False, self.per, passes)

    def half(self):
        return self.phase // self.per

    def expert(self):
        return self.pass_no * 2 + self.half()

    def seat(self):
        return self.phase % self.per

    def uses(self, plus=0):
        return self.pass_no * 2 + (self.half() + 1 + plus)

    def before(self, par):
        return self.pass_no * self.per + (self.half() * (self.per + 1 - par)) // 2


def expert_steps(eng, n, lag, per):
    period = 2 * per
    for t in range(period):
        yield Chunk(t, t, n, True, per, 0)
    with eng.Fori(1, n // period) as i:
        for k in range(period):
            yield Chunk(i * period + k, k, n, False, per, i)
    for t in range(n, n + lag):
        yield Chunk(t, t % period, n, True, per, t // period)


def experts(nc, t, sb, ps, sems, E):
    PER = CAP // CH
    N = NE * PER
    MIX = S // (NE // 2)
    with ExitStack() as st:
        def many(n, name, shape, dt=F32):
            return [sb(st, f"{name}{i}", shape, dt) for i in range(n)]

        w1, w2 = many(2, "w1_", [P, FFN]), many(2, "w2_", [P, 4, D])
        xr = many(PER, "exr", [P, 4, ROW])
        token = many(PER, "etoken", [P, 4], U32)
        first, part, weight = (many(PER, f"e{n}", [P, 4]) for n in ("first", "part", "weight"))
        xT, yo = many(2, "exT", [P, CH]), many(2, "eyo", [P, 4, D])
        hid = many(2, "ehid", [P, 4, CH])
        scrap = sb(st, "escrap", [P, 1])
        pX = [ps(st, f"e_pX{i}", [P, CH]) for i in range(2)]
        pH = ps(st, "e_pH", [P, 4, CH])
        pY = [ps(st, f"e_pY{i}", [P, 4, D]) for i in range(2)]
        w_in = sems(st, "e_w_in0", "e_w_in1")
        x_in = sems(st, *[f"e_x_in{i}" for i in range(PER)])
        added = sems(st, "e_added0", "e_added1")
        (turned, xT_ready, hidden, active, made, y_ready, is_first, parts_made, weight_ready,
         scrapped) = sems(
            st, "e_turned", "e_xT_ready", "e_hidden", "e_active", "e_made", "e_y_ready", "e_is_first", "e_parts_made",
            "e_weight_ready", "e_scrapped")
        src = t["slots"][0:SLOTS, :].rearrange("(c j p) d -> p c j d", p=P, j=4)
        ha = E.bufA[:].rearrange("p (b s) -> p s b", s=S)
        block = st.enter_context(nc.Block())

        @block.sync
        def _(sp):
            for s in expert_steps(sp, N, 0, PER):
                if c := s.back(0):
                    wait(sp, turned, c.times(1, 1 - PER))
                    wait(sp, weight_ready, c.times(1, 1 - PER))
                    sp.dma_start(xr[c.seat()][:], src[:, bass.ds(c.v, 1), :, :]).then_inc(x_in[c.seat()], 16)
                    if c.seat() == 0:
                        if not (c.static and c.v < 2 * PER):
                            sp.wait_ge(made, c.times(1, -PER))
                        sp.dma_start(w1[c.half()][:], t["w1"][:, bass.ds(c.expert(), 1), :]).then_inc(w_in[c.half()], 16)
                        sp.dma_start(w2[c.half()][:], t["w2"][:, bass.ds(c.expert(), 1), :, :]).then_inc(w_in[c.half()], 16)

        @block.tensor
        def _(pe):
            for s in expert_steps(pe, N, 2, PER):
                if c := s.back(0):
                    pe.wait_ge(x_in[c.seat()], c.uses() * 16)
                    wait(pe, xT_ready, c.times(1, -1))
                    for j in range(4):
                        i = nc.tensor.transpose(pX[c.par][:, j * P:(j + 1) * P], xr[c.seat()][:, j, 0:D], E.ident)
                    i.then_inc(turned, 1)
                if c := s.back(1):
                    if c.seat() == 0:
                        pe.wait_ge(w_in[c.half()], c.pass_no * 32 + 32)
                    pe.wait_ge(xT_ready, c.times(1, 1))
                    for f in range(4):
                        wait(pe, active, c.times(4, f - 3))
                        nc.tensor.matmul(pH[:, f, :], w1[c.half()][:, f * P:(f + 1) * P], xT[c.par][:],
                                         start=True, stop=True).then_inc(hidden, 1)
                if c := s.back(2):
                    wait(pe, y_ready, c.times(1, -1))
                    pe.wait_ge(active, c.times(4, 4))
                    for j in range(4):
                        for f in range(4):
                            i = nc.tensor.matmul(pY[c.par][:, j, :], hid[c.par][:, f, j * P:(j + 1) * P],
                                                 w2[c.half()][:, f, :], start=(f == 0), stop=(f == 3))
                    i.then_inc(made, 1)

        @block.scalar
        def _(act):
            for s in expert_steps(act, N, 1, PER):
                if c := s.back(1):
                    wait(act, made, c.times(1, -1))
                    for f in range(4):
                        act.wait_ge(hidden, c.times(4, f + 1))
                        nc.scalar.activation(hid[c.par][:, f, :], pH[:, f, :], ACT.Gelu).then_inc(active, 1)

        @block.vector
        def _(dve):
            for s in expert_steps(dve, N, 2, PER):
                if c := s.back(0):
                    dve.wait_ge(turned, c.times(1, 1))
                    wait(dve, hidden, c.times(4, -4))
                    nc.vector.tensor_copy(xT[c.par][:], pX[c.par][:]).then_inc(xT_ready, 1)
                if c := s.back(2):
                    dve.wait_ge(made, c.times(1, 1))
                    dve.wait_ge(weight_ready, c.times(1, 1))
                    if not (c.static and c.v < 2):
                        dve.wait_ge(added[c.par], (c.v - c.par) * 32 if c.par else c.v * 32)
                    for j in range(4):
                        i = nc.vector.tensor_scalar(yo[c.par][:, j, :], pY[c.par][:, j, :],
                                                    weight[c.seat()][:, j:j + 1], None, ALU.mult)
                    i.then_inc(y_ready, 1)
                if c := s.back(0):
                    k = c.seat()
                    e1, wa, wb = xr[k][:, :, D + 3], xr[k][:, :, D + 1], xr[k][:, :, D + 2]
                    nc.vector.tensor_scalar(first[k][:], e1, E.const("expert")[:, bass.ds(c.expert(), 1)], None,
                                            ALU.is_equal).then_inc(is_first, 1)
                    nc.vector.tensor_copy(token[k][:], xr[k][:, :, D])
                    dve.wait_ge(is_first, c.times(1, 1))
                    nc.vector.tensor_tensor(part[k][:], first[k][:], wb, ALU.mult)
                    nc.vector.tensor_tensor(weight[k][:], first[k][:], wa, ALU.mult).then_inc(parts_made, 1)
                    dve.wait_ge(parts_made, c.times(2, 1))
                    nc.vector.tensor_tensor(part[k][:], wb, part[k][:], ALU.subtract).then_inc(parts_made, 1)
                    dve.wait_ge(parts_made, c.times(2, 2))
                    nc.vector.tensor_tensor(weight[k][:], weight[k][:], part[k][:], ALU.add).then_inc(weight_ready, 1)
                    if c.phase < MIX:
                        n = c.pass_no * MIX + c.phase
                        x = E.bufX[:, bass.ds(n * B, B)]
                        nc.vector.scalar_tensor_tensor(x, ha[:, bass.ds(n, 1), :].rearrange("p n b -> p (n b)"),
                                                       E.mod[:, 5, bass.ds(n, 1)], x, ALU.mult, ALU.add)

        @block.gpsimd
        def _(pool):
            for s in expert_steps(pool, N, 2, PER):
                if c := s.back(2):
                    pool.wait_ge(y_ready, c.times(1, 1))
                    if c.seat() == 0:
                        for k in range(2):
                            wait(pool, added[k], c.before(k) * 64)
                    wait(pool, scrapped, c.times(1, 0))
                    nc.gpsimd.tensor_tensor(scrap[:], E.ident[:, 0:1], E.ident[:, 0:1], ALU.mult).then_inc(scrapped, 1)
                    for j in range(4):
                        pool.indirect_dma_start(t["sums"], bass.IndirectOffsetOnAxis(ap=token[c.seat()][:, j:j + 1], axis=0),
                                                yo[c.par][:, j, :], None, compute_op=ALU.add).then_inc(added[c.par], 16)
            for k in range(2):
                pool.wait_ge(added[k], 64 * (N // 2))


def combine(nc, t, sb, ps, sems, E):
    PIECE = NCH // 8
    with ExitStack() as st:
        fo = [sb(st, f"cfo{i}", [P, CH]) for i in range(4)]
        pm = [ps(st, f"c_pm{i}", [P, CH]) for i in range(4)]
        sums_in = sems(st, *[f"c_sums_in{i}" for i in range(8)])
        stored = sems(st, *[f"c_stored{i}" for i in range(4)])
        (turned, o_ready) = sems(st, "c_turned", "c_o_ready")
        block = st.enter_context(nc.Block())
        src = t["sums"][0:NT, :].rearrange("(n p) d -> p n d", p=P)

        @block.sync
        def _(sp):
            for k in range(8):
                n = 4 * PIECE
                sp.dma_start(E.bufH[:, k * PIECE * CH:(k + 1) * PIECE * CH].rearrange("p (n d) -> p n d", d=D),
                             src[:, k * n:(k + 1) * n, :]).then_inc(sums_in[k], 16)

        @block.tensor
        def _(pe):
            for c in range(NCH):
                if c % PIECE == 0:
                    pe.wait_ge(sums_in[c // PIECE], 16)
                wait(pe, o_ready, c - 3)
                for j in range(4):
                    i = nc.tensor.transpose(pm[c % 4][:, j * P:(j + 1) * P], E.bufH[:, c * CH + j * P:c * CH + (j + 1) * P],
                                            E.ident)
                i.then_inc(turned, 1)

        @block.vector
        def _(dve):
            for c in range(NCH):
                dve.wait_ge(turned, c + 1)
                wait(dve, stored[c % 4], 16 * (c // 4))
                for k in range(2):
                    at = slice(k * B, (k + 1) * B)
                    i = nc.vector.scalar_tensor_tensor(fo[c % 4][:, at], pm[c % 4][:, at],
                                                       E.mod[:, 5, 2 * c + k:2 * c + k + 1],
                                                       E.bufX[:, c * CH + k * B:c * CH + (k + 1) * B], ALU.mult, ALU.add)
                i.then_inc(o_ready, 1)

        @block.scalar
        def _(act):
            for c in range(NCH):
                act.wait_ge(o_ready, c + 1)
                act.dma_start(t["out"][:, c * CH:(c + 1) * CH], fo[c % 4][:]).then_inc(stored[c % 4], 16)
            for k in range(4):
                act.wait_ge(stored[k], 16 * (NCH // 4))


def lay_out(i):
    def f(name):
        return np.asarray(i[name])

    def halves(a):
        a = a.reshape(2, P, -1)
        return a.transpose(1, 0, 2)

    x = f("L0_attn_x").reshape(NT, D)
    qkv = f("L0_ffn_qkv_weight").reshape(NKV, 4, HD, D)
    cols = np.concatenate([
        f("L0_attn_bi").reshape(4, P).T,
        halves(f("L0_attn_conv_w").reshape(DI, DCONV)).reshape(P, 8),
        f("L0_attn_conv_b").reshape(2, P).T, f("L0_attn_bdt").reshape(2, P).T,
        f("L0_attn_bo").reshape(P, 1), f("L0_attn_Dv").reshape(2, P).T,
        f("L0_ffn_ln1_weight").reshape(P, 1), f("L0_ffn_ln1_bias").reshape(P, 1),
        f("L0_ffn_ln2_weight").reshape(P, 1), f("L0_ffn_ln2_bias").reshape(P, 1)], axis=1)
    out = {
        "con": np.concatenate(list(CONST.values()), axis=1),
        "x": x.reshape(TILES, P, D).transpose(1, 0, 2),
        "xT": x.T,
        "wi": f("L0_attn_Wi").T,
        "wdt": f("L0_attn_Wdt").T,
        "wo": halves(f("L0_attn_Wo").T),
        "wq": qkv[:, 0:2].transpose(3, 1, 0, 2).reshape(D, 2 * KV),
        "wk": qkv[:, 2].reshape(KV, D).T, "wv": qkv[:, 3].reshape(KV, D).T,
        "wp": f("L0_ffn_proj_weight").T.reshape(NKV, 2, HD, D).transpose(1, 0, 2, 3).reshape(2 * KV, D),
        "router": f("L0_ffn_router_weight"),
        "cols": cols,
        "alog": halves(f("L0_attn_A_log")), "bm": halves(f("L0_attn_Bm")), "cm": halves(f("L0_attn_Cm")),
        "ct": f("L0_c").T,
        "wmod": f("L0_wmod").reshape(P, 6, D),
        "w1": f("L0_ffn_moe_w1").transpose(1, 0, 2),
        "w2": f("L0_ffn_moe_w2").reshape(NE, 4, P, D).transpose(2, 0, 1, 3),
    }
    return {k: np.ascontiguousarray(v) for k, v in out.items()}


def kernel(**inputs):
    import concourse.bacc as _bacc
    from concourse.bass_utils import run_bass_kernel_spmd as _run

    nc = _bacc.Bacc("TRN2", target_bir_lowering=False, num_devices=1)
    arrays, t = {}, {}
    for name, a in lay_out(inputs).items():
        arrays[f"in_{name}"] = a
        t[name] = nc.dram_tensor(f"in_{name}", a.shape, F32, kind="ExternalInput").ap()
    t["out"] = nc.dram_tensor("out_0", [P, NT], F32, kind="ExternalOutput").ap()
    t["slots"] = nc.dram_tensor("slots", [SLOTS + 2 * NT, ROW], F32, kind="Internal").ap()
    t["sums"] = nc.dram_tensor("sums", [NT + EMPTY, D], F32, kind="Internal").ap()
    build(nc, t)
    r = _run(nc, [arrays], core_ids=[0])
    return np.ascontiguousarray(r.results[0]["out_0"].T.reshape(S, B, D))
```
